# Optimizing a Trainium2 kernel written in Bass

```python
import numpy as np
import jax
import jax.numpy as jnp

def _softmax(x, axis=-1):
    return jax.nn.softmax(x, axis=axis)

def _gelu(x):
    return jax.nn.gelu(x, approximate=True)

def _silu(x):
    return jax.nn.silu(x)

def _sigmoid(x):
    return jax.nn.sigmoid(x)

def _layernorm(x, axis=-1, eps=1e-05):
    m = jnp.mean(x, axis=axis, keepdims=True)
    v = jnp.var(x, axis=axis, keepdims=True)
    return (x - m) / jnp.sqrt(v + eps)

def _scatter_add(tgt, idx, src, axis=0):
    return tgt.at[idx].add(src)

def _segment_sum(src, seg, n):
    return jax.ops.segment_sum(src, seg, n)
kernel_name = 'mk_decoder_postln_d1_seqx_r4_3a9f37'

def setup_inputs(seed: int=0):
    np.random.seed(seed)
    _w = jnp.asarray

    def _rec_inputs():
        import jax
        import jax.numpy as jnp
        _rk = jax.random.key(seed)
        x = -0.000125 + 0.9999 * jax.random.normal(jax.random.fold_in(_rk, 1), (4, 512, 512), jnp.float32)
        _lenS = 512 - jax.random.randint(jax.random.fold_in(_rk, 7), (4,), 0, max(1, 512 // 4) + 1, jnp.int32)
        _lenS2 = 512 - jax.random.randint(jax.random.fold_in(_rk, 8), (4,), 0, max(1, 512 // 4) + 1, jnp.int32)
        _ctx_2048P = jax.random.normal(jax.random.fold_in(_rk, 11), (4, 16, 512), jnp.float32)
        _ctx_2048c = jax.random.dirichlet(jax.random.fold_in(_rk, 511), 0.3 * jnp.ones((16,), jnp.float32), (4, 512))
        _ctx_2048t = jnp.einsum('bsk,bkd->bsd', _ctx_2048c, _ctx_2048P)
        _ctx_2048t = _ctx_2048t * jax.lax.rsqrt(jnp.mean(jnp.square(_ctx_2048t)) + 1e-12) * 0.953939
        ctx_2048 = 0.00139358 + 0.999369 * (_ctx_2048t + 0.3 * jax.random.normal(jax.random.fold_in(_rk, 611), (4, 512, 512), jnp.float32))
        return (x, ctx_2048)
    x, ctx_2048 = _rec_inputs()

    def _L0_attn_setup():
        import jax, jax.numpy as jnp
        import numpy as np
        BATCH, SEQ, EMBED = (8, 256, 512)
        HEADS, LATENT = (16, 128)
        HEAD_DIM = EMBED // HEADS
        NOPE = HEAD_DIM // 4
        ROPE_D = HEAD_DIM - NOPE
        THETA = 10000.0

        def _rope_tables(seq_len):
            freqs = 1.0 / THETA ** (jnp.arange(0, ROPE_D, 2, dtype=jnp.float32) / ROPE_D)
            emb = jnp.arange(seq_len, dtype=jnp.float32)[:, None] * freqs[None, :]
            return (jnp.cos(emb), jnp.sin(emb))

        def _apply_rope(x, cos, sin):
            xe, xo = (x[..., ::2], x[..., 1::2])
            return jnp.concatenate([xe * cos - xo * sin, xo * cos + xe * sin], axis=-1)
        key = jax.random.key(seed)
        ks = jax.random.split(key, 5)
        x = jax.random.normal(ks[0], (BATCH, SEQ, EMBED), jnp.float32)
        Wq = jax.random.normal(ks[1], (EMBED, EMBED), jnp.float32) * 0.02
        Wkv_down = jax.random.normal(ks[2], (EMBED, LATENT), jnp.float32) * 0.02
        Wk_up = jax.random.normal(ks[3], (LATENT, EMBED), jnp.float32) * 0.02
        Wv_up = jax.random.normal(ks[4], (LATENT, EMBED), jnp.float32) * 0.02
        return {'x': x, 'Wq': Wq, 'Wkv_down': Wkv_down, 'Wk_up': Wk_up, 'Wv_up': Wv_up}
    _L0_attn_all = _L0_attn_setup()
    _L0_attn_in = {k: v for k, v in _L0_attn_all.items() if k in ('Wq', 'Wkv_down', 'Wk_up', 'Wv_up')}
    del _L0_attn_all

    def _L0_xattn_setup():
        import jax, jax.numpy as jnp
        import numpy as np
        key = jax.random.key(seed)
        k = jax.random.split(key, 6)
        B, S, D, NKV = (4, 1024, 512, 64)
        inv = D ** (-0.5)
        return {'x': jax.random.normal(k[0], (B, S, D), jnp.float32), 'W_qkv': jax.random.normal(k[1], (3 * D, D), jnp.float32) * inv, 'W_o': jax.random.normal(k[2], (D, D), jnp.float32) * inv, 'beta_q': jnp.array(1.0, jnp.float32), 'beta_k': jnp.array(1.0, jnp.float32), 'gate': jnp.array(0.0, jnp.float32), 'log_tau': jnp.array(0.0, jnp.float32), 'K_mem': jax.random.normal(k[3], (B, NKV, D), jnp.float32), 'V_mem': jax.random.normal(k[4], (B, NKV, D), jnp.float32), 'clip_k': 54}
    _L0_xattn_all = _L0_xattn_setup()
    _L0_xattn_in = {k: v for k, v in _L0_xattn_all.items() if k in ('W_qkv', 'W_o', 'beta_q', 'beta_k', 'gate', 'log_tau')}
    del _L0_xattn_all

    def _L0_ffn_setup():
        import jax, jax.numpy as jnp
        import numpy as np
        import math
        GOLDEN_CENTER = 1.0 / math.e
        GOLDEN_LOWER = 0.5 - math.log(4.0 / 3.0)
        GOLDEN_UPPER = 0.5
        B, T, D = (4, 256, 512)
        E = 8
        F = 2048 // (E // 2)
        R = 64
        NL = 2

        def _router_weights(x, Wr, temperature):
            logits = jnp.einsum('btd,de->bte', x, Wr)
            inhibition = jax.nn.sigmoid(logits / temperature)
            in_zone = (inhibition >= GOLDEN_LOWER) & (inhibition <= GOLDEN_UPPER)
            distance = jnp.abs(inhibition - GOLDEN_CENTER)
            w = jnp.exp(-distance / 0.1) * in_zone.astype(x.dtype)
            wsum = w.sum(axis=-1, keepdims=True)
            no_expert = wsum < 1e-08
            fb = jnp.exp(-distance / 0.3)
            _, top2 = jax.lax.top_k(fb, 2)
            fb_mask = jax.nn.one_hot(top2, E, dtype=x.dtype).sum(axis=-2)
            fb_w = fb * fb_mask
            fb_w = fb_w / jnp.clip(fb_w.sum(axis=-1, keepdims=True), 1e-08)
            w = jnp.where(no_expert, fb_w, w)
            return w / jnp.clip(w.sum(axis=-1, keepdims=True), 1e-08)
        key = jax.random.key(seed)
        ks = jax.random.split(key, 13)
        s = 0.02
        x = jax.random.normal(ks[0], (B, T, D), dtype=jnp.float32)
        Wg = jax.random.normal(ks[1], (E, D, F), dtype=jnp.float32) * s
        Wu = jax.random.normal(ks[2], (E, D, F), dtype=jnp.float32) * s
        Wd = jax.random.normal(ks[3], (E, F, D), dtype=jnp.float32) * s
        Ga = jax.random.normal(ks[4], (NL, D, R), dtype=jnp.float32) * s
        Gb = jax.random.normal(ks[5], (NL, R, F), dtype=jnp.float32) * s
        Ua = jax.random.normal(ks[6], (NL, D, R), dtype=jnp.float32) * s
        Ub = jax.random.normal(ks[7], (NL, R, F), dtype=jnp.float32) * s
        Da = jax.random.normal(ks[8], (NL, F, R), dtype=jnp.float32) * s
        Db = jax.random.normal(ks[9], (NL, R, D), dtype=jnp.float32) * s
        Wr = jax.random.normal(ks[10], (D, E), dtype=jnp.float32) * s
        temperature = jnp.ones((1,), dtype=jnp.float32)
        return {'x': x, 'Wg': Wg, 'Wu': Wu, 'Wd': Wd, 'Ga': Ga, 'Gb': Gb, 'Ua': Ua, 'Ub': Ub, 'Da': Da, 'Db': Db, 'Wr': Wr, 'temperature': temperature}
    _L0_ffn_all = _L0_ffn_setup()
    _L0_ffn_in = {k: v for k, v in _L0_ffn_all.items() if k in ('Wg', 'Wu', 'Wd', 'Ga', 'Gb', 'Ua', 'Ub', 'Da', 'Db', 'Wr', 'temperature')}
    del _L0_ffn_all
    return {'x': x, 'ctx_2048': ctx_2048, 'L0_attn_Wq': _L0_attn_in['Wq'], 'L0_attn_Wkv_down': _L0_attn_in['Wkv_down'], 'L0_attn_Wk_up': _L0_attn_in['Wk_up'], 'L0_attn_Wv_up': _L0_attn_in['Wv_up'], 'L0_xattn_W_qkv': _L0_xattn_in['W_qkv'], 'L0_xattn_W_o': _L0_xattn_in['W_o'], 'L0_xattn_beta_q': _L0_xattn_in['beta_q'], 'L0_xattn_beta_k': _L0_xattn_in['beta_k'], 'L0_xattn_gate': _L0_xattn_in['gate'], 'L0_xattn_log_tau': _L0_xattn_in['log_tau'], 'L0_ffn_Wg': _L0_ffn_in['Wg'], 'L0_ffn_Wu': _L0_ffn_in['Wu'], 'L0_ffn_Wd': _L0_ffn_in['Wd'], 'L0_ffn_Ga': _L0_ffn_in['Ga'], 'L0_ffn_Gb': _L0_ffn_in['Gb'], 'L0_ffn_Ua': _L0_ffn_in['Ua'], 'L0_ffn_Ub': _L0_ffn_in['Ub'], 'L0_ffn_Da': _L0_ffn_in['Da'], 'L0_ffn_Db': _L0_ffn_in['Db'], 'L0_ffn_Wr': _L0_ffn_in['Wr'], 'L0_ffn_temperature': _L0_ffn_in['temperature']}

def reference(x, ctx_2048, L0_attn_Wq, L0_attn_Wkv_down, L0_attn_Wk_up, L0_attn_Wv_up, L0_xattn_W_qkv, L0_xattn_W_o, L0_xattn_beta_q, L0_xattn_beta_k, L0_xattn_gate, L0_xattn_log_tau, L0_ffn_Wg, L0_ffn_Wu, L0_ffn_Wd, L0_ffn_Ga, L0_ffn_Gb, L0_ffn_Ua, L0_ffn_Ub, L0_ffn_Da, L0_ffn_Db, L0_ffn_Wr, L0_ffn_temperature):
    import jax
    import jax.numpy as jnp

    def _L0_attn_ref(x, Wq, Wkv_down, Wk_up, Wv_up):
        import jax, jax.numpy as jnp
        import numpy as np
        BATCH, SEQ, EMBED = (8, 256, 512)
        HEADS, LATENT = (16, 128)
        HEAD_DIM = EMBED // HEADS
        NOPE = HEAD_DIM // 4
        ROPE_D = HEAD_DIM - NOPE
        THETA = 10000.0

        def _rope_tables(seq_len):
            freqs = 1.0 / THETA ** (jnp.arange(0, ROPE_D, 2, dtype=jnp.float32) / ROPE_D)
            emb = jnp.arange(seq_len, dtype=jnp.float32)[:, None] * freqs[None, :]
            return (jnp.cos(emb), jnp.sin(emb))

        def _apply_rope(x, cos, sin):
            xe, xo = (x[..., ::2], x[..., 1::2])
            return jnp.concatenate([xe * cos - xo * sin, xo * cos + xe * sin], axis=-1)
        B, S, E = x.shape
        q = (x @ Wq).reshape(B, S, HEADS, HEAD_DIM).transpose(0, 2, 1, 3)
        q_nope, q_rope = (q[..., :NOPE], q[..., NOPE:])
        c_kv = x @ Wkv_down
        k = (c_kv @ Wk_up).reshape(B, S, HEADS, HEAD_DIM).transpose(0, 2, 1, 3)
        v = (c_kv @ Wv_up).reshape(B, S, HEADS, HEAD_DIM).transpose(0, 2, 1, 3)
        k_nope, k_rope = (k[..., :NOPE], k[..., NOPE:])
        cos, sin = _rope_tables(S)
        q_rope = _apply_rope(q_rope, cos, sin)
        k_rope = _apply_rope(k_rope, cos, sin)
        qf = jnp.concatenate([q_nope, q_rope], axis=-1)
        kf = jnp.concatenate([k_nope, k_rope], axis=-1)
        scale = jnp.float32(1.0 / np.sqrt(HEAD_DIM))
        scores = jnp.einsum('bhqd,bhkd->bhqk', qf, kf) * scale
        causal = jnp.triu(jnp.ones((S, S), dtype=bool), k=1)
        scores = jnp.where(causal, -jnp.inf, scores)
        weights = jax.nn.softmax(scores, axis=-1)
        out = jnp.einsum('bhqk,bhkd->bhqd', weights, v)
        return out.transpose(0, 2, 1, 3).reshape(B, S, E)

    def _L0_xattn_ref(x, W_qkv, W_o, beta_q, beta_k, gate, log_tau, K_mem, V_mem, clip_k):
        import jax, jax.numpy as jnp
        import numpy as np
        D = x.shape[-1]
        scale = D ** (-0.5)
        qkv = x @ W_qkv.T
        Q = qkv[..., :D]
        alpha = jax.nn.sigmoid(gate)
        tau = jnp.exp(log_tau)
        coef = (alpha * beta_q + (1.0 - alpha) * beta_k) * scale * tau
        scores = coef * jnp.einsum('bsd,bnd->bsn', Q, K_mem)
        scores = scores - jnp.max(scores, axis=-1, keepdims=True)
        thr = jax.lax.top_k(scores, clip_k)[0][..., -1:]
        scores = jnp.where(scores < thr, -jnp.inf, scores)
        att = jax.nn.softmax(scores, axis=-1)
        out = jnp.einsum('bsn,bnd->bsd', att, V_mem)
        return out @ W_o.T

    def _L0_ffn_ref(x, Wg, Wu, Wd, Ga, Gb, Ua, Ub, Da, Db, Wr, temperature):
        import jax, jax.numpy as jnp
        import numpy as np
        import math
        GOLDEN_CENTER = 1.0 / math.e
        GOLDEN_LOWER = 0.5 - math.log(4.0 / 3.0)
        GOLDEN_UPPER = 0.5
        B, T, D = (4, 256, 512)
        E = 8
        F = 2048 // (E // 2)
        R = 64
        NL = 2

        def _router_weights(x, Wr, temperature):
            logits = jnp.einsum('btd,de->bte', x, Wr)
            inhibition = jax.nn.sigmoid(logits / temperature)
            in_zone = (inhibition >= GOLDEN_LOWER) & (inhibition <= GOLDEN_UPPER)
            distance = jnp.abs(inhibition - GOLDEN_CENTER)
            w = jnp.exp(-distance / 0.1) * in_zone.astype(x.dtype)
            wsum = w.sum(axis=-1, keepdims=True)
            no_expert = wsum < 1e-08
            fb = jnp.exp(-distance / 0.3)
            _, top2 = jax.lax.top_k(fb, 2)
            fb_mask = jax.nn.one_hot(top2, E, dtype=x.dtype).sum(axis=-2)
            fb_w = fb * fb_mask
            fb_w = fb_w / jnp.clip(fb_w.sum(axis=-1, keepdims=True), 1e-08)
            w = jnp.where(no_expert, fb_w, w)
            return w / jnp.clip(w.sum(axis=-1, keepdims=True), 1e-08)
        weights = _router_weights(x, Wr, temperature)
        gate = jnp.einsum('btd,edf->ebtf', x, Wg)
        up = jnp.einsum('btd,edf->ebtf', x, Wu)
        gate = gate.at[:NL].add(jnp.einsum('btd,edr,erf->ebtf', x, Ga, Gb))
        up = up.at[:NL].add(jnp.einsum('btd,edr,erf->ebtf', x, Ua, Ub))
        mid = jax.nn.silu(gate) * up
        out = jnp.einsum('ebtf,efd->ebtd', mid, Wd)
        out = out.at[:NL].add(jnp.einsum('ebtf,efr,erd->ebtd', mid[:NL], Da, Db))
        return jnp.einsum('bte,ebtd->btd', weights, out)
    x = _layernorm(x + _L0_attn_ref(x, L0_attn_Wq, L0_attn_Wkv_down, L0_attn_Wk_up, L0_attn_Wv_up), axis=-1)
    x = _layernorm(x + _L0_xattn_ref(x, L0_xattn_W_qkv, L0_xattn_W_o, L0_xattn_beta_q, L0_xattn_beta_k, L0_xattn_gate, L0_xattn_log_tau, ctx_2048, ctx_2048, 54), axis=-1)
    x = _layernorm(x + _L0_ffn_ref(x, L0_ffn_Wg, L0_ffn_Wu, L0_ffn_Wd, L0_ffn_Ga, L0_ffn_Gb, L0_ffn_Ua, L0_ffn_Ub, L0_ffn_Da, L0_ffn_Db, L0_ffn_Wr, L0_ffn_temperature), axis=-1)
    return x

_drawn_inputs = setup_inputs


def setup_inputs(seed=0):
    import zlib

    import numpy as np

    out = dict(_drawn_inputs(seed))
    spreads = {}
    factors = {'L0_attn_Wq': 8.0,
     'L0_attn_Wkv_down': 4.475,
     'L0_attn_Wk_up': 8.0,
     'L0_attn_Wv_up': 4.531,
     'L0_ffn_Ga': 8.0,
     'L0_ffn_Gb': 8.0,
     'L0_ffn_Ua': 8.0,
     'L0_ffn_Ub': 8.0,
     'L0_ffn_Da': 8.0,
     'L0_ffn_Db': 8.0}
    for name, (base, spread) in spreads.items():
        noise = np.random.default_rng([zlib.crc32(name.encode()), seed]).standard_normal(out[name].shape)
        drawn = base * np.exp(spread * noise) if base else spread * noise
        out[name] = jnp.asarray(drawn.astype(out[name].dtype))
    for name, factor in factors.items():
        out[name] = (out[name] * factor).astype(out[name].dtype)
    return out
```

```python
import math
from contextlib import ExitStack

import numpy as np

import concourse.bass as bass
from concourse import mybir
from concourse.alu_op_type import AluOpType as ALU

ACT = mybir.ActivationFunctionType
AX = mybir.AxisListType.X
F32 = mybir.dt.float32
F16 = mybir.dt.float16
BF16 = mybir.dt.bfloat16

P = 128
B, S, D = 4, 512, 512
H, HD, NOPE = 16, 32, 8
ROPE = HD - NOPE
LAT = 128
E, F, R = 8, 512, 64
NL = 2
TOPK = 54
TT = S // P
DT = D // P
FT = F // P
N = B * S
NT = N // P
EPS = 1e-5
NEG = -1.0e30

SX = 16.0
SW = 64.0
SQ = 4.0
SV = 16.0
SP = 1024.0
SM = 64.0
SNM = 64.0

G = 4
TRI = sum((i + 1) * P for i in range(TT))
OFF = {4: 0, 3: 512, 1: 896, 2: 1024}

A_SEQ = [("xT", d) for d in range(DT)] + [("c",)]
for _t in range(TT):
    A_SEQ += [("q", _t), ("k", _t), ("v", _t)]
    if _t:
        A_SEQ += [("cat", 2 * (_t - 1) + x, y) for x in range(2) for y in range(2)]
A_SEQ += [("cat", 2 * (TT - 1) + x, y) for x in range(2) for y in range(2)]
A_SEQ += [("mT", 0)]
for _h in range(H):
    if _h % G == G - 1 and _h < H - 1:
        A_SEQ += [("mT", (_h + 1) // G)]
    if _h:
        A_SEQ += [("pv", _h - 1)]
A_SEQ += [("pv", H - 1)]
A_AT = {u: n for n, u in enumerate(A_SEQ)}
A_N = len(A_SEQ)
A_PER = [(A_N + 1) // 2, A_N // 2]

B_SEQ = [("cT", d) for d in range(DT)] + [("A", d) for d in range(DT)] + [("CW", n) for n in range(4)]
B_SEQ += [("xT", 0), ("xT", 1), ("sc", 0), ("xT", 2), ("sc", 1), ("xT", 3), ("sc", 2), ("sc", 3)]
for _t in range(TT):
    B_SEQ += [("aT", _t), ("out", _t)]
    if _t:
        B_SEQ += [("x2", _t - 1)]
B_SEQ += [("x2", TT - 1)]
B_AT = {u: n for n, u in enumerate(B_SEQ)}
B_N = len(B_SEQ)
assert B_N % 8 == 0

C_SEQ = []
for _c in range(B + 1):
    if _c < B:
        C_SEQ += [(x, _c, f) for f in range(FT) for x in ("g", "u")]
    if _c:
        C_SEQ += [("d", _c - 1, t) for t in range(TT)]
C_AT = {u: n for n, u in enumerate(C_SEQ)}
C_N = len(C_SEQ)
assert C_N % 8 == 0

GOLDEN_CENTER = 1.0 / math.e
GOLDEN_LOWER = 0.5 - math.log(4.0 / 3.0)
GOLDEN_UPPER = 0.5


class Chain:

    def __init__(self, eng, sem, base=0):
        self.eng, self.sem, self.base, self.n = eng, sem, base, 0

    def link(self, ins, wait=None):
        self.n += 1
        ins.then_inc(self.sem, 1)
        (wait or self.eng.wait_ge)(self.sem, self.base + self.n)


def decoder(nc, a):
    ctx = ExitStack()

    def sem(name):
        return ctx.enter_context(nc.semaphore(name))

    def sb(stack, name, shape, dt=F32):
        return stack.enter_context(nc.sbuf_tensor(name, shape, dt))

    with ctx:
        banks = ctx.enter_context(nc.psum_tensor("banks", [P, 8, 512], F32))
        max_ps = banks[:, 0:3, :].rearrange("p b n -> p (b n)")
        st_ps = banks[:, 3:6, :].rearrange("p b n -> p (b n)")
        resid = sb(ctx, "resid", [P, NT, D])
        identf = sb(ctx, "identf", [P, P])
        ident16 = sb(ctx, "ident16", [P, P], F16)
        identb = sb(ctx, "identb", [P, P], BF16)
        eps = sb(ctx, "eps", [P, 1])
        negc = sb(ctx, "negc", [P, 1])
        stats = sb(ctx, "stats", [P, TT, 6])
        mv = sb(ctx, "mv", [P, TT, 2])
        lnv = sb(ctx, "lnv", [P, TT])
        rstd = sb(ctx, "rstd", [P, TT])
        nwt = sb(ctx, "nwt", [P, TT])
        coef = sb(ctx, "coef", [P, 8])
        wr_raw = sb(ctx, "wr_raw", [P, DT, E])
        wr16 = sb(ctx, "wr16", [P, DT, 2 * E], F16)
        temp = sb(ctx, "temp", [P, 2])

        sa = ctx.enter_context(ExitStack())
        x_in = sb(sa, "x_in", [P, TT, D])
        x_res = sb(sa, "x_res", [P, TT, D])
        xT = sb(sa, "xT", [P, 2, DT, S], F16)
        cT = sb(sa, "cT", [P, 2, S], F16)
        wq = sb(sa, "wq", [P, 2, DT, D], F16)
        wkvd = sb(sa, "wkvd", [P, 2, DT, LAT], F16)
        wku = sb(sa, "wku", [P, 2, D], F16)
        wvu = sb(sa, "wvu", [P, 2, D], F16)
        rows = sb(sa, "rows", [P, 2, H, HD])
        turn_a = sb(sa, "turn_a", [P, H, ROPE // 2, 2])
        turn_b = sb(sa, "turn_b", [P, H, ROPE // 2, 2])
        cossin = sb(sa, "cossin", [P, 2, TT, ROPE // 2, 2])
        cat = sb(sa, "cat", [P, 2, H, 3, HD], F16)
        qcT = sb(sa, "qcT", [P, H, S], F16)
        kcT = sb(sa, "kcT", [P, H, S], F16)
        vcat = sb(sa, "vcat", [P, TT, H, 66], F16)
        pf = sb(sa, "pf", [P, 2, TRI])
        phi = sb(sa, "phi", [P, 2, TRI], F16)
        plo = sb(sa, "plo", [P, 2, TRI], F16)
        osb = sb(sa, "osb", [P, H, TT, 65])
        nmf = sb(sa, "nmf", [P, TT, G])
        nm16 = sb(sa, "nm16", [P, TT, P], F16)
        mT = sb(sa, "mT", [P, 2, S], F16)
        sel = sb(sa, "sel", [P, G, P], F16)
        mask_qk = sb(sa, "mask_qk", [P, P], BF16)
        mask_kq = sb(sa, "mask_kq", [P, P], BF16)
        rsum = sb(sa, "rsum", [P, H, TT])
        att = sb(sa, "att", [P, D])
        raw_wq = pf[:, :, :].rearrange("p a n -> p (a n)")[:, 0:DT * D].rearrange("p (t n) -> p t n", t=DT)
        raw_osb = osb[:, :, :, :].rearrange("p h t n -> p (h t n)")
        raw_kvd = raw_osb[:, 0:DT * LAT].rearrange("p (t n) -> p t n", t=DT)
        raw_ku = raw_osb[:, 512:1024]
        raw_vu = raw_osb[:, 1024:1536]
        sa.close()

        x2T = sb(ctx, "x2T", [P, 2, DT, N], F16)
        stage = sb(ctx, "stage", [P, 3, 4, 512])
        ca = ctx.enter_context(ExitStack())
        c_raw = sb(ca, "c_raw", [P, 4, D])
        cxT = sb(ca, "cxT", [P, 2, DT, 512], F16)
        wqw = sb(ca, "wqw", [P, 2, 4, D], F16)
        woT = sb(ca, "woT", [P, 2, DT, D], F16)
        raw_q = sb(ca, "raw_q", [P, 4, D])
        raw_o = sb(ca, "raw_o", [P, 4, D])
        kq = sb(ca, "kq", [P, 2, DT, 512], F16)
        cw = sb(ca, "cw", [P, 2, 4, D], F16)
        x1row = sb(ca, "x1row", [P, TT, D])
        x2row = sb(ca, "x2row", [P, TT, D])
        x1T = sb(ca, "x1T", [P, 2, 2, DT, P], F16)
        tsc = sb(ca, "tsc", [P, 4, 512])
        wk = sb(ca, "wk", [P, 2, 512])
        top8 = sb(ca, "top8", [P, 7, 8])
        small = sb(ca, "small", [P, 2, 4])
        tm = sb(ca, "tm", [P, 512])
        ex = sb(ca, "ex", [P, 2, 512])
        attf = sb(ca, "attf", [P, 2, 512])
        attT = sb(ca, "attT", [P, 2, 2, 4, P], F16)
        ca.close()

        w16 = sb(ctx, "w16", [P, 2, 3, 2, 4, 512], F16)
        mid16 = sb(ctx, "mid16", [P, 2, 2, FT, 512], F16)
        sil = sb(ctx, "sil", [P, 2, 512])
        midf = sb(ctx, "midf", [P, 2, 512])
        la_raw = sb(ctx, "la_raw", [P, 4, R])
        lb_raw = sb(ctx, "lb_raw", [R, 512])
        laT = sb(ctx, "laT", [R, 2, 512], F16)
        lb16 = sb(ctx, "lb16", [R, 2, 512], F16)
        rt = sb(ctx, "rt", [P, 14, NT, E])
        rs1 = sb(ctx, "rs1", [P, 8, NT])
        wt = sb(ctx, "wt", [P, NT, E])

        w_loaded = sem("w_loaded")
        consts = sem("consts")
        sel_ready = sem("sel_ready")
        w_hi = sem("w_hi")
        w_lo = sem("w_lo")
        x_loaded = sem("x_loaded")
        res_loaded = sem("res_loaded")
        a_ready = sem("a_ready")
        a_hi = sem("a_hi")
        a_drained = [sem("bank6_drained"), sem("bank7_drained")]
        roped = sem("roped")
        cat_hi = sem("cat_hi")
        cat_lo = sem("cat_lo")
        max_ready = sem("max_ready")
        max_done = sem("max_done")
        nm_ready = sem("nm_ready")
        st_ready = sem("st_ready")
        exp_done = sem("exp_done")
        p_hi = sem("p_hi")
        p_lo_pool = sem("p_lo_pool")
        p_lo_dve = sem("p_lo_dve")
        norm_step = sem("norm_step")
        res_read = sem("res_read")
        passed = sem("passed")
        var_ready = sem("var_ready")
        ln_done = sem("ln_done")
        rstd_ready = sem("rstd_ready")
        x1_written = sem("x1_written")
        b_loaded = sem("b_loaded")
        s_loaded = sem("s_loaded")
        coef_step = sem("coef_step")
        coef_act = sem("coef_act")
        ctx_loaded = sem("ctx_loaded")
        bw_hi = sem("bw_hi")
        bw_lo = sem("bw_lo")
        wo_ready = sem("wo_ready")
        wo_hi = sem("wo_hi")
        wo_drained = sem("wo_drained")
        b_ready = sem("b_ready")
        b_hi = sem("b_hi")
        b_drained = [sem(f"b_bank{k}_drained") for k in range(8)]
        top_step = sem("top_step")
        ex_ready = sem("ex_ready")
        att_ready = sem("att_ready")
        b_step = sem("b_step")
        b_var = sem("b_var")
        b_ln = sem("b_ln")
        b_rstd = sem("b_rstd")
        x2_written = sem("x2_written")
        x1_fetched = sem("x1_fetched")
        x2_kept = sem("x2_kept")
        stage_loaded = [sem(f"stage{m}_loaded") for m in range(3)]
        lora_loaded = sem("lora_loaded")
        la_turned = sem("la_turned")
        lora_hi = sem("lora_hi")
        lora_lo = sem("lora_lo")
        lora_mm = sem("lora_mm")
        lora_added = sem("lora_added")
        e_hi = sem("e_hi")
        e_lo = sem("e_lo")
        wr_step = sem("wr_step")
        logits_ready = sem("logits_ready")
        r_act = sem("r_act")
        r_step = sem("r_step")
        wt_ready = sem("wt_ready")
        c_ready = sem("c_ready")
        c_drained = [sem(f"c_bank{k}_drained") for k in range(8)]
        mid_hi = sem("mid_hi")
        mid_lo = sem("mid_lo")
        f_step = sem("f_step")
        f_var = sem("f_var")
        f_ln = sem("f_ln")
        f_rstd = sem("f_rstd")
        y_ready = sem("y_ready")
        y_stored = sem("y_stored")

        def a_slot(u):
            return A_AT[u] % 2

        def wait_a_filled(eng, b, u):
            eng.wait_ge(a_ready, b * A_N + (A_AT[u] + 1))

        def wait_a_drained(eng, b, u):
            n = A_AT[u]
            eng.wait_ge(a_drained[n % 2], b * A_PER[n % 2] + (n // 2 + 1))

        def wait_a_free(eng, b, u):
            n = A_AT[u]
            eng.wait_ge(a_drained[n % 2], b * A_PER[n % 2] + n // 2)

        def a_bank(u):
            return banks[:, 6 + a_slot(u), :]

        A_HI = [("xT", d) for d in range(DT)] + [("c",)] + [("v", t) for t in range(TT)]

        def b_bank(u):
            return banks[:, B_AT[u] % 8, :]

        def wait_b_filled(eng, b, u):
            eng.wait_ge(b_ready, b * B_N + (B_AT[u] + 1))

        def wait_b_drained(eng, b, u):
            n = B_AT[u]
            eng.wait_ge(b_drained[n % 8], b * (B_N // 8) + (n // 8 + 1))

        def wait_b_free(eng, b, u):
            n = B_AT[u]
            eng.wait_ge(b_drained[n % 8], b * (B_N // 8) + n // 8)

        B_SPLIT = [u for u in B_SEQ if u[0] not in ("sc", "out")]
        B_HI = {u: n for n, u in enumerate(B_SPLIT)}

        def c_bank(u):
            return banks[:, C_AT[u] % 8, :]

        def wait_c_filled(eng, e, u):
            eng.wait_ge(c_ready, e * C_N + (C_AT[u] + 1))

        def wait_c_free(eng, e, u):
            n = C_AT[u]
            eng.wait_ge(c_drained[n % 8], e * (C_N // 8) + n // 8)

        def wait_c_drained(eng, e, u):
            n = C_AT[u]
            eng.wait_ge(c_drained[n % 8], e * (C_N // 8) + (n // 8 + 1))

        LORA = [("Ga", "Gb"), ("Ua", "Ub"), ("Da", "Db")]
        WN = ["Wg", "Wu", "Wd"]

        block = ctx.enter_context(nc.Block())

        @block.sync
        def _(sp):
            sp.dma_start(raw_wq, a["Wq"].rearrange("(t p) n -> p t n", p=P)).then_inc(w_loaded, 16)
            sp.dma_start(raw_kvd, a["Wkv"].rearrange("(t p) n -> p t n", p=P)).then_inc(w_loaded, 16)
            sp.dma_start(raw_ku, a["Wku"]).then_inc(w_loaded, 16)
            sp.dma_start(raw_vu, a["Wvu"]).then_inc(w_loaded, 16)
            sp.dma_start(cossin[:, :, :, :, :], a["cossin"]).then_inc(w_loaded, 16)
            sp.dma_start(wr_raw[:, :, :], a["Wr"].rearrange("(t p) e -> p t e", p=P)).then_inc(s_loaded, 16)
            for n, name in enumerate(("gate", "beta_q", "beta_k", "log_tau")):
                sp.dma_start(coef[:, n:n + 1], a[name].partition_broadcast(P)).then_inc(s_loaded, 16)
            sp.dma_start(temp[:, 0:1], a["temperature"].partition_broadcast(P)).then_inc(s_loaded, 16)
            def load_x(dst, b, done):
                sp.dma_start(dst[:, :, :], a["x"][b].rearrange("(t p) d -> p t d", p=P)).then_inc(done, 16)

            load_x(x_in, 0, x_loaded)
            load_x(x_res, 0, res_loaded)
            with sp.Fori(0, B - 1) as b:
                wait_a_filled(sp, b, ("xT", DT - 1))
                load_x(x_in, b + 1, x_loaded)
                sp.wait_ge(res_read, b * TT + TT)
                load_x(x_res, b + 1, res_loaded)

            sp.wait_ge(x1_written, NT)
            sp.dma_start(raw_q[:, :, :], a["W_qkv"][0:D].rearrange("(t p) n -> p t n", p=P)).then_inc(b_loaded, 16)
            sp.dma_start(raw_o[:, :, :], a["W_o"].rearrange("(t p) n -> p t n", p=P)).then_inc(b_loaded, 16)
            def load_x1(b):
                sp.dma_start(x1row[:, :, :], resid[:, bass.ds(b * TT, TT), :]).then_inc(x1_fetched, 16)

            def load_context(b):
                sp.dma_start(c_raw[:, :, :], a["ctx"][b].rearrange("(t p) d -> p t d", p=P)).then_inc(ctx_loaded, 16)

            load_context(0)
            load_x1(0)
            with sp.Fori(0, B - 1) as b:
                wait_b_filled(sp, b, ("cT", DT - 1))
                load_context(b + 1)
                sp.wait_ge(b_var, b * TT + TT)
                load_x1(b + 1)
            for m in range(3):
                sp.dma_start(stage[:, m], a[WN[m]][0].rearrange("(t p) n -> p t n", p=P)).then_inc(stage_loaded[m], 16)
            sp.wait_ge(x2_kept, 16 * B)
            for e in range(NL):
                for m in range(3):
                    n = 3 * e + m
                    if n:
                        sp.wait_ge(lora_lo, 2 * n)
                    sp.dma_start(la_raw[:, :, :], a[LORA[m][0]][e].rearrange("(t p) r -> p t r", p=P)).then_inc(lora_loaded, 16)
                    sp.dma_start(lb_raw[:, :], a[LORA[m][1]][e]).then_inc(lora_loaded, 16)
                if e == 0:
                    for m in range(3):
                        sp.wait_ge(e_lo, m + 1)
                        sp.dma_start(stage[:, m], a[WN[m]][1].rearrange("(t p) n -> p t n", p=P)).then_inc(stage_loaded[m], 16)
            with sp.Fori(1, E - 1) as e:
                for m in range(3):
                    sp.wait_ge(e_lo, e * 3 + (m + 1))
                    sp.dma_start(stage[:, m], a[WN[m]][e + 1].rearrange("(t p) n -> p t n", p=P)).then_inc(stage_loaded[m], 16)
            y = a["y"].rearrange("(c t p) d -> c p t d", p=P, t=TT)
            for c in range(B):
                sp.wait_ge(y_ready, c + 1)
                sp.dma_start(y[c], resid[:, c * TT:(c + 1) * TT, :]).then_inc(y_stored, 16)
            sp.wait_ge(y_stored, 16 * B)

        @block.gpsimd
        def _(pool):
            for t in (identf, ident16, identb):
                pool.memset(t[:, :], 0.0).then_inc(consts, 1)
            pool.memset(mask_qk[:, :], 0.0).then_inc(consts, 1)
            pool.memset(mask_kq[:, :], 0.0).then_inc(consts, 1)
            pool.memset(sel[:, :, :], 0.0).then_inc(consts, 1)
            pool.memset(eps[:, :], EPS).then_inc(consts, 1)
            pool.memset(negc[:, :], -GOLDEN_CENTER).then_inc(consts, 1)
            pool.memset(nm16[:, :, :], 0.0).then_inc(consts, 1)
            pool.memset(vcat[:, :, :, 64:66], 1.0).then_inc(consts, 1)
            pool.wait_ge(consts, 10)
            for t in (identf, ident16, identb):
                pool.affine_select(out=t[:, :], in_=t[:, :], compare_op=ALU.not_equal, fill=1.0, base=0,
                                   pattern=[[-1, P]], channel_multiplier=1).then_inc(consts, 1)
            pool.affine_select(out=mask_qk[:, :], in_=mask_qk[:, :], compare_op=ALU.is_ge, fill=NEG, base=0,
                               pattern=[[-1, P]], channel_multiplier=1).then_inc(consts, 1)
            pool.affine_select(out=mask_kq[:, :], in_=mask_kq[:, :], compare_op=ALU.is_ge, fill=NEG, base=0,
                               pattern=[[1, P]], channel_multiplier=-1).then_inc(consts, 1)
            pool.affine_select(out=sel[:, :, :], in_=sel[:, :, :], compare_op=ALU.not_equal, fill=SNM, base=0,
                               pattern=[[-1, G], [0, P]], channel_multiplier=1).then_inc(consts, 1)

            pool.wait_ge(w_loaded, 80)
            with pool.Fori(0, B) as b:
                for u in range(2 * TT):
                    t = u // 2
                    wait_a_drained(pool, b, ("qk"[u % 2], t))
                    pool.wait_ge(roped, b * (8 * TT) + 4 * u)
                    pair = rows[:, u % 2, :, NOPE:HD].rearrange("p h (i two) -> p h i two", two=2)
                    for n, dst in ((0, turn_a), (1, turn_b)):
                        cs = cossin[:, n, t].unsqueeze(1).to_broadcast([P, H, ROPE // 2, 2])
                        nc.gpsimd.tensor_tensor(dst[:, :, :, :], pair, cs, ALU.mult).then_inc(roped, 1)
                    pool.wait_ge(roped, b * (8 * TT) + (4 * u + 2))
                    half = NOPE + ROPE // 2
                    nc.gpsimd.tensor_tensor(rows[:, u % 2, :, NOPE:half], turn_a[:, :, :, 0], turn_a[:, :, :, 1],
                                            ALU.subtract).then_inc(roped, 1)
                    nc.gpsimd.tensor_tensor(rows[:, u % 2, :, half:HD], turn_b[:, :, :, 1], turn_b[:, :, :, 0],
                                            ALU.add).then_inc(roped, 1)
                for h in range(H):
                    pool.wait_ge(p_hi, b * H + (h + 1))
                    nc.gpsimd.tensor_tensor(plo[:, h % 2, 0:POOL_COLS], pf[:, h % 2, 0:POOL_COLS],
                                            phi[:, h % 2, 0:POOL_COLS], ALU.subtract).then_inc(p_lo_pool, 1)

            with pool.Fori(0, E) as e:
                for n in range(B * FT):
                    pool.wait_ge(mid_hi, e * (B * FT) + (n + 1))
                    c, f = n // FT, n % FT
                    nc.gpsimd.tensor_tensor(mid16[:, c % 2, 1, f, :], midf[:, n % 2, :], mid16[:, c % 2, 0, f, :],
                                            ALU.subtract).then_inc(mid_lo, 1)

        @block.tensor
        def _(pe):
            def three(out, l, r, n, done=None):
                for i in range(n):
                    for j, (x, y) in enumerate(((0, 0), (0, 1), (1, 0))):
                        mm = nc.tensor.matmul(out, l(x, i), r(y, i), start=(i == 0 and j == 0),
                                              stop=(i == n - 1 and j == 2))
                if done is not None:
                    mm.then_inc(done, 1)
                return mm

            pe.wait_ge(consts, 16)
            pe.wait_ge(w_lo, 4)
            with pe.Fori(0, B) as b:
                pe.wait_ge(x_loaded, b * 16 + 16)
                for d in range(DT):
                    u = ("xT", d)
                    wait_a_free(pe, b, u)
                    for t in range(TT):
                        mm = nc.tensor.transpose(a_bank(u)[:, t * P:(t + 1) * P], x_in[:, t, d * P:(d + 1) * P], identf[:, :])
                    mm.then_inc(a_ready, 1)
                for d in range(DT):
                    wait_a_drained(pe, b, ("xT", d))
                wait_a_free(pe, b, ("c",))
                three(a_bank(("c",)), lambda x, i: wkvd[:, x, i, :], lambda y, i: xT[:, y, i, :], DT, a_ready)

                def qkv(t):
                    ts = slice(t * P, (t + 1) * P)
                    wait_a_free(pe, b, ("q", t))
                    three(a_bank(("q", t)), lambda x, i: xT[:, x, i, ts], lambda y, i: wq[:, y, i, :], DT, a_ready)
                    if t == 0:
                        wait_a_drained(pe, b, ("c",))
                    for name, w in (("k", wku), ("v", wvu)):
                        wait_a_free(pe, b, (name, t))
                        three(a_bank((name, t)), lambda x, i: cT[:, x, ts], lambda y, i, w=w: w[:, y, :], 1, a_ready)

                def turn_cat(v):
                    pe.wait_ge(cat_lo, b * (2 * TT) + (v + 1))
                    for half in range(2):
                        u = ("cat", v, half)
                        wait_a_free(pe, b, u)
                        out = a_bank(u).bitcast(F16)
                        for j in range(8):
                            src = cat[:, v % 2, half * 8 + j].rearrange("p a n -> p (a n)")
                            mm = nc.tensor.transpose(out[0:3 * HD, j * P:(j + 1) * P], src, ident16[:, :])
                        mm.then_inc(a_ready, 1)

                for t in range(TT):
                    qkv(t)
                    if t:
                        turn_cat(2 * t - 2)
                        turn_cat(2 * t - 1)
                turn_cat(2 * TT - 2)
                turn_cat(2 * TT - 1)
                for v in (2 * TT - 2, 2 * TT - 1):
                    for half in range(2):
                        wait_a_drained(pe, b, ("cat", v, half))

                K3 = 3 * HD

                def by_query(h):
                    pe.wait_ge(max_done, b * (4 * H) + 4 * h)
                    for i in range(TT):
                        w = (i + 1) * P
                        o = OFF[i + 1]
                        nc.tensor.matmul(max_ps[:, o:o + w], qcT[0:K3, h, i * P:(i + 1) * P], kcT[0:K3, h, 0:w],
                                         start=True, stop=False)
                        mm = nc.tensor.matmul(max_ps[:, o + w - P:o + w], identb[:, :], mask_qk[:, :],
                                              start=False, stop=True)
                    mm.then_inc(max_ready, 1)

                def turn_max(g):
                    u = ("mT", g)
                    pe.wait_ge(nm_ready, b * (H // G) + (g + 1))
                    wait_a_free(pe, b, u)
                    out = a_bank(u).bitcast(F16)
                    for i in range(TT):
                        mm = nc.tensor.transpose(out[:, i * P:(i + 1) * P], nm16[:, i, :], ident16[:, :])
                    mm.then_inc(a_ready, 1)

                def by_key(h):
                    if h % G == 0:
                        wait_a_drained(pe, b, ("mT", h // G))
                    pe.wait_ge(exp_done, b * H + h)
                    for k in range(TT):
                        w = S - k * P
                        o = OFF[TT - k]
                        nc.tensor.matmul(st_ps[:, o:o + w], kcT[0:K3, h, k * P:(k + 1) * P], qcT[0:K3, h, k * P:S],
                                         start=True, stop=False)
                        nc.tensor.matmul(st_ps[:, o:o + P], identb[:, :], mask_kq[:, :], start=False, stop=False)
                        mm = nc.tensor.matmul(st_ps[:, o:o + w], sel[:, h % G, :], mT[:, (h // G) % 2, k * P:S],
                                              start=False, stop=True)
                    mm.then_inc(st_ready, 1)

                def values(h):
                    u = ("pv", h)
                    pe.wait_ge(p_lo_pool, b * H + (h + 1))
                    pe.wait_ge(p_lo_dve, b * H + (h + 1))
                    wait_a_free(pe, b, u)
                    for i in range(TT):
                        out = a_bank(u)[:, i * 65:(i + 1) * 65]
                        for k in range(i + 1):
                            o = OFF[TT - k] + (i - k) * P
                            for n, w in enumerate((phi, plo)):
                                mm = nc.tensor.matmul(out, w[:, h % 2, o:o + P], vcat[:, k, h, 0:65],
                                                      start=(k == 0 and n == 0), stop=(k == i and n == 1))
                    mm.then_inc(a_ready, 1)

                for h in range(AHEAD):
                    by_query(h)
                turn_max(0)
                for h in range(H):
                    if h + AHEAD < H:
                        by_query(h + AHEAD)
                    if h % G == G - 1 and h < H - 1:
                        turn_max((h + 1) // G)
                    by_key(h)
                    if h:
                        values(h - 1)
                values(H - 1)

            pe.wait_ge(x1_written, NT)
            pe.wait_ge(b_loaded, 32)
            for d in range(DT):
                if d:
                    pe.wait_ge(wo_drained, d)
                for t in range(4):
                    mm = nc.tensor.transpose(banks[:, 0, t * P:(t + 1) * P], raw_o[:, t, d * P:(d + 1) * P], identf[:, :])
                mm.then_inc(wo_ready, 1)
            pe.wait_ge(wo_drained, DT)
            pe.wait_ge(bw_lo, 1)
            with pe.Fori(0, B) as b:
                pe.wait_ge(ctx_loaded, b * 16 + 16)
                for d in range(DT):
                    u = ("cT", d)
                    wait_b_free(pe, b, u)
                    for t in range(4):
                        mm = nc.tensor.transpose(b_bank(u)[:, t * P:(t + 1) * P], c_raw[:, t, d * P:(d + 1) * P], identf[:, :])
                    mm.then_inc(b_ready, 1)
                for d in range(DT):
                    wait_b_drained(pe, b, ("cT", d))
                for d in range(DT):
                    wait_b_free(pe, b, ("A", d))
                    three(b_bank(("A", d)), lambda x, i: wqw[:, x, i, d * P:(d + 1) * P], lambda y, i: cxT[:, y, i, :], 4, b_ready)
                for t in range(4):
                    wait_b_free(pe, b, ("CW", t))
                    three(b_bank(("CW", t)), lambda x, i: cxT[:, x, i, t * P:(t + 1) * P], lambda y, i: woT[:, y, i, :], 4, b_ready)

                def turn_x(t, name, src):
                    u = (name, t)
                    wait_b_free(pe, b, u)
                    for d in range(DT):
                        mm = nc.tensor.transpose(b_bank(u)[:, d * P:(d + 1) * P], src(d), identf[:, :])
                    mm.then_inc(b_ready, 1)

                def scores(t):
                    u = ("sc", t)
                    wait_b_drained(pe, b, ("xT", t))
                    if t == 0:
                        for d in range(DT):
                            wait_b_drained(pe, b, ("A", d))
                    wait_b_free(pe, b, u)
                    three(b_bank(u), lambda x, i: x1T[:, t % 2, x, i, :], lambda y, i: kq[:, y, i, :], DT, b_ready)

                def weighted(t):
                    pe.wait_ge(att_ready, b * TT + (t + 1))
                    turn_x(t, "aT", lambda n: attf[:, t % 2, n * P:(n + 1) * P])
                    wait_b_drained(pe, b, ("aT", t))
                    if t == 0:
                        for n in range(4):
                            wait_b_drained(pe, b, ("CW", n))
                    u = ("out", t)
                    wait_b_free(pe, b, u)
                    three(b_bank(u), lambda x, i: attT[:, t % 2, x, i, :], lambda y, i: cw[:, y, i, :], 4, b_ready)

                def turn_x2(t):
                    pe.wait_ge(x2_written, b * TT + (t + 1))
                    turn_x(t, "x2", lambda d: x2row[:, t, d * P:(d + 1) * P])

                def turn_x1(t):
                    turn_x(t, "xT", lambda d: x1row[:, t, d * P:(d + 1) * P])

                pe.wait_ge(x1_fetched, b * 16 + 16)
                turn_x1(0)
                turn_x1(1)
                scores(0)
                turn_x1(2)
                scores(1)
                turn_x1(3)
                scores(2)
                scores(3)
                for t in range(TT):
                    weighted(t)
                    if t:
                        turn_x2(t - 1)
                turn_x2(TT - 1)

            for t in range(TT):
                wait_b_drained(pe, B - 1, ("x2", t))
            for t in range(8):
                pe.wait_ge(b_drained[t], B * (B_N // 8))
            pe.wait_ge(wr_step, 2)
            for t in range(NT):
                ts = slice(t * P, (t + 1) * P)
                out = banks[:, 7, t * 16:(t + 1) * 16]
                for i in range(DT):
                    for x in range(2):
                        mm = nc.tensor.matmul(out, x2T[:, x, i, ts], wr16[:, i, :], start=(i == 0 and x == 0),
                                              stop=(i == DT - 1 and x == 1))
            mm.then_inc(logits_ready, 1)

            def low_rank(e, m):
                n = 3 * e + m
                pe.wait_ge(lora_loaded, 32 * (n + 1))
                if n:
                    pe.wait_ge(lora_added, 4 * n)
                for t in range(4):
                    mm = nc.tensor.transpose(banks[0:R, 0, t * P:(t + 1) * P], la_raw[:, t, :], identf[:, :])
                mm.then_inc(la_turned, 1)
                pe.wait_ge(lora_lo, 2 * (n + 1))
                for t in range(4):
                    ts = slice(t * P, (t + 1) * P)
                    three(banks[:, 1 + t, :], lambda x, i: laT[:, x, ts], lambda y, i: lb16[:, y, :], 1, lora_mm)

            for m in range(3):
                low_rank(0, m)
            for m in range(3):
                low_rank(1, m)
            pe.wait_ge(lora_added, 24)
            pe.wait_ge(r_act, 1)

            def expert(e, par):
                def ffn_in(c):
                    cs = slice(c * 512, (c + 1) * 512)
                    for f in range(FT):
                        for m, name in enumerate("gu"):
                            u = (name, c, f)
                            wait_c_free(pe, e, u)
                            if c == 0 and f == 0:
                                pe.wait_ge(e_lo, e * 3 + (m + 1))
                            three(c_bank(u), lambda x, i: w16[:, par, m, x, i, f * P:(f + 1) * P],
                                  lambda y, i: x2T[:, y, i, cs], DT, c_ready)

                def ffn_out(c):
                    pe.wait_ge(mid_lo, e * (B * FT) + FT * (c + 1))
                    if c == 0:
                        pe.wait_ge(e_lo, e * 3 + 3)
                    for t in range(TT):
                        u = ("d", c, t)
                        wait_c_free(pe, e, u)
                        three(c_bank(u), lambda x, i: mid16[:, c % 2, x, i, t * P:(t + 1) * P],
                              lambda y, i: w16[:, par, 2, y, i, :], FT, c_ready)

                for c in range(B + 1):
                    if c < B:
                        ffn_in(c)
                    if c:
                        ffn_out(c - 1)

            with pe.Fori(0, E // 2) as pair:
                for par in range(2):
                    expert(pair * 2 + par, par)

        @block.scalar
        def _(act):
            def scaled(out, in_, scale):
                return nc.scalar.activation(out, in_, ACT.Copy, scale=scale)

            act.wait_ge(w_loaded, 80)
            scaled(wq[:, 0], raw_wq, SW).then_inc(w_hi, 1)
            scaled(wkvd[:, 0], raw_kvd, SW).then_inc(w_hi, 1)
            scaled(wku[:, 0], raw_ku, SW).then_inc(w_hi, 1)
            scaled(wvu[:, 0], raw_vu, SW).then_inc(w_hi, 1)
            act.wait_ge(w_lo, 4)
            act.wait_ge(consts, 16)
            with act.Fori(0, B) as b:
                for d in range(DT):
                    u = ("xT", d)
                    wait_a_filled(act, b, u)
                    scaled(xT[:, 0, d, :], a_bank(u), SX).then_inc(a_hi, 1)
                wait_a_filled(act, b, ("c",))
                scaled(cT[:, 0, :], a_bank(("c",)), 1.0 / SW).then_inc(a_hi, 1)

                def evac_row(v):
                    u = ("qk"[v % 2], v // 2)
                    if v >= 2:
                        act.wait_ge(cat_lo, b * (2 * TT) + (v - 1))
                    else:
                        act.wait_ge(cat_lo, b * (2 * TT))
                    wait_a_filled(act, b, u)
                    scaled(rows[:, v % 2], a_bank(u).rearrange("p (h n) -> p h n", h=H), SQ / (SX * SW))\
                        .then_inc(a_drained[a_slot(u)], 1)

                def evac_v(t):
                    u = ("v", t)
                    wait_a_filled(act, b, u)
                    scaled(vcat[:, t, :, 0:HD], a_bank(u).rearrange("p (h n) -> p h n", h=H), SV / (SX * SW))\
                        .then_inc(a_hi, 1)

                def high_cat(v):
                    act.wait_ge(roped, b * (8 * TT) + 4 * (v + 1))
                    if v >= 2:
                        wait_a_filled(act, b, ("cat", v - 2, 1))
                    dst = cat[:, v % 2, :, 0:2] if v % 2 == 0 else cat[:, v % 2, :, 0:3:2]
                    scaled(dst, rows[:, v % 2].unsqueeze(2).to_broadcast([P, H, 2, HD]), 1.0).then_inc(cat_hi, 1)

                for t in range(TT):
                    evac_row(2 * t)
                    evac_row(2 * t + 1)
                    evac_v(t)
                    high_cat(2 * t)
                    high_cat(2 * t + 1)

                def exps(h):
                    act.wait_ge(st_ready, b * H + (h + 1))
                    if h >= 2:
                        act.wait_ge(p_lo_pool, b * H + (h - 1))
                        act.wait_ge(p_lo_dve, b * H + (h - 1))
                    else:
                        act.wait_ge(p_lo_pool, b * H)
                        act.wait_ge(p_lo_dve, b * H)
                    nc.scalar.activation(pf[:, h % 2, :], st_ps[:, 0:TRI], ACT.Exp,
                                         scale=1.0 / (SQ * SQ * math.sqrt(HD))).then_inc(exp_done, 1)

                def high_p(h):
                    act.wait_ge(exp_done, b * H + (h + 1))
                    if h >= 2:
                        wait_a_filled(act, b, ("pv", h - 2))
                    scaled(phi[:, h % 2, :], pf[:, h % 2, :], 1.0).then_inc(p_hi, 1)

                def evac_pv(h):
                    u = ("pv", h)
                    wait_a_filled(act, b, u)
                    scaled(osb[:, h], a_bank(u)[:, 0:TT * 65].rearrange("p (t n) -> p t n", t=TT), 1.0)\
                        .then_inc(a_drained[a_slot(u)], 1)

                for h in range(H):
                    exps(h)
                    high_p(h)
                    if h:
                        evac_pv(h - 1)
                evac_pv(H - 1)
                act.wait_ge(var_ready, b + 1)
                nc.scalar.activation(lnv[:, :], mv[:, :, 1], ACT.Ln, bias=eps[:, 0:1]).then_inc(ln_done, 1)
                act.wait_ge(ln_done, b + 1)
                nc.scalar.activation(rstd[:, :], lnv[:, :], ACT.Exp, scale=-0.5).then_inc(rstd_ready, 1)

            act.wait_ge(s_loaded, 96)
            nc.scalar.activation(coef[:, 4:5], coef[:, 0:1], ACT.Exp, scale=-1.0).then_inc(coef_act, 1)
            nc.scalar.activation(coef[:, 5:6], coef[:, 3:4], ACT.Exp).then_inc(coef_act, 1)
            act.wait_ge(x1_written, NT)
            act.wait_ge(b_loaded, 32)
            scaled(wqw[:, 0], raw_q[:, :, :], SW).then_inc(bw_hi, 1)
            for d in range(DT):
                act.wait_ge(wo_ready, d + 1)
                scaled(woT[:, 0, d, :], banks[:, 0, :], SW).then_inc(wo_hi, 1)
            act.wait_ge(coef_step, COEF_STEPS)
            with act.Fori(0, B) as b:
                def high(u, dst, scale):
                    wait_b_filled(act, b, u)
                    scaled(dst, b_bank(u).rearrange("p (t n) -> p t n", n=dst.shape[-1]) if len(dst.shape) == 3 else b_bank(u),
                           scale).then_inc(b_hi, 1)

                act.wait_ge(att_ready, b * TT)
                for d in range(DT):
                    high(("cT", d), cxT[:, 0, d, :], SX)
                for d in range(DT):
                    high(("A", d), kq[:, 0, d, :], 1.0 / SW)
                for t in range(4):
                    high(("CW", t), cw[:, 0, t, :], 1.0 / SW)

                def high_x1(t):
                    high(("xT", t), x1T[:, t % 2, 0], SX)

                def evac_scores(t):
                    u = ("sc", t)
                    wait_b_filled(act, b, u)
                    nc.scalar.activation(tsc[:, t, :], b_bank(u), ACT.Copy, scale=coef[:, 7:8]).then_inc(b_drained[B_AT[u] % 8], 1)

                def exps_of(t):
                    act.wait_ge(top_step, b * (TT * TOP_STEPS) + (t * TOP_STEPS + 2))
                    if t >= 2:
                        act.wait_ge(att_ready, b * TT + (t - 1))
                    nc.scalar.activation(ex[:, t % 2, :], tsc[:, t, :], ACT.Exp, bias=small[:, t % 2, 0:1]).then_inc(ex_ready, 1)

                def ln_tile(t):
                    act.wait_ge(b_var, b * TT + (t + 1))
                    nc.scalar.activation(lnv[:, t:t + 1], mv[:, t, 1:2], ACT.Ln, bias=eps[:, 0:1]).then_inc(b_ln, 1)
                    act.wait_ge(b_ln, b * TT + (t + 1))
                    nc.scalar.activation(rstd[:, t:t + 1], lnv[:, t:t + 1], ACT.Exp, scale=-0.5).then_inc(b_rstd, 1)

                def high_x2(t):
                    cols = bass.ds(b * S + t * P, P)
                    high(("x2", t), x2T[:, 0, :, cols], SX)

                high_x1(0)
                high_x1(1)
                evac_scores(0)
                high_x1(2)
                evac_scores(1)
                high_x1(3)
                evac_scores(2)
                evac_scores(3)
                exps_of(0)
                for t in range(TT):
                    high(("aT", t), attT[:, t % 2, 0], SP)
                    if t + 1 < TT:
                        exps_of(t + 1)
                    ln_tile(t)
                    if t:
                        high_x2(t - 1)
                high_x2(TT - 1)
                act.dma_start(resid[:, bass.ds(b * TT, TT), :], x2row[:, :, :]).then_inc(x2_kept, 16)

            act.wait_ge(x2_written, NT)
            act.wait_ge(x2_kept, 16 * B)
            scaled(wr16[:, :, 0:E], wr_raw[:, :, :], SW).then_inc(wr_step, 1)
            act.wait_ge(logits_ready, 1)
            scaled(rt[:, 0:2].rearrange("p a t e -> p t a e"), banks[:, 7, 0:NT * 16].rearrange("p (t a e) -> p t a e", t=NT, a=2),
                   1.0 / (SX * SW)).then_inc(r_act, 1)
            act.wait_ge(r_step, 2)
            nc.scalar.activation(rt[:, 3], rt[:, 2], ACT.Sigmoid).then_inc(r_act, 1)
            act.wait_ge(r_act, 2)
            nc.scalar.activation(rt[:, 4], rt[:, 3], ACT.Abs, bias=negc[:, 0:1]).then_inc(r_act, 1)
            act.wait_ge(r_act, 3)
            nc.scalar.activation(rt[:, 5], rt[:, 4], ACT.Exp, scale=-1.0 / 0.1).then_inc(r_act, 1)
            nc.scalar.activation(rt[:, 6], rt[:, 4], ACT.Exp, scale=-1.0 / 0.3).then_inc(r_act, 1)

            def low_rank(e, m):
                n = 3 * e + m
                act.wait_ge(la_turned, n + 1)
                if n:
                    act.wait_ge(lora_mm, 4 * n)
                scaled(laT[:, 0, :], banks[0:R, 0, :], SW).then_inc(lora_hi, 1)
                scaled(lb16[:, 0, :], lb_raw[:, :], SW).then_inc(lora_hi, 1)

            for m in range(3):
                low_rank(0, m)
            for m in range(3):
                act.wait_ge(stage_loaded[m], 16)
                act.wait_ge(lora_added, 4 * (m + 1))
                scaled(w16[:, 0, m, 0], stage[:, m], SW).then_inc(e_hi, 1)
            for m in range(3):
                low_rank(1, m)
            for m in range(3):
                act.wait_ge(stage_loaded[m], 32)
                act.wait_ge(lora_added, 4 * (m + 4))
                scaled(w16[:, 1, m, 0], stage[:, m], SW).then_inc(e_hi, 1)

            def expert(e, par):
                for c in range(B):
                    for f in range(FT):
                        n = c * FT + f
                        u = ("g", c, f)
                        wait_c_filled(act, e, u)
                        nc.scalar.activation(sil[:, n % 2, :], c_bank(u), ACT.Silu, scale=1.0 / (SX * SW))\
                            .then_inc(c_drained[C_AT[u] % 8], 1)
                        wait_c_drained(act, e, ("u", c, f))
                        scaled(mid16[:, c % 2, 0, f, :], midf[:, n % 2, :], 1.0).then_inc(mid_hi, 1)

            with act.Fori(0, E // 2 - 1) as pair:
                for par in range(2):
                    expert(pair * 2 + par, par)
                    for m in range(3):
                        wait_c_filled(act, pair * 2 + par, ("d", B - 1, TT - 1))
                        act.wait_ge(stage_loaded[m], (pair * 2 + par) * 16 + 48)
                        scaled(w16[:, par, m, 0], stage[:, m], SW).then_inc(e_hi, 1)
            for par in range(2):
                expert(E - 2 + par, par)

            for c in range(B):
                act.wait_ge(f_var, c + 1)
                nc.scalar.activation(lnv[:, :], mv[:, :, 1], ACT.Ln, bias=eps[:, 0:1]).then_inc(f_ln, 1)
                act.wait_ge(f_ln, c + 1)
                nc.scalar.activation(rstd[:, :], lnv[:, :], ACT.Exp, scale=-0.5).then_inc(f_rstd, 1)

        @block.vector
        def _(dve):
            ts_, tt_, stt = nc.vector.tensor_scalar, nc.vector.tensor_tensor, nc.vector.scalar_tensor_tensor

            def low(out, src, hi, scale):
                return stt(out=out, in0=src, scalar=scale, in1=hi, op0=ALU.mult, op1=ALU.subtract)

            dve.wait_ge(w_loaded, 80)
            for n, (w, raw) in enumerate(((wq, raw_wq), (wkvd, raw_kvd), (wku, raw_ku), (wvu, raw_vu))):
                dve.wait_ge(w_hi, n + 1)
                if len(raw.shape) == 3:
                    low(w[:, 1].rearrange("p t n -> p (t n)"), raw.rearrange("p t n -> p (t n)"),
                        w[:, 0].rearrange("p t n -> p (t n)"), SW).then_inc(w_lo, 1)
                else:
                    low(w[:, 1], raw, w[:, 0], SW).then_inc(w_lo, 1)
            dve.wait_ge(consts, 16)

            def wait_apart(signal, value):
                dve.wait_ge(signal, value)
                dve.sem_inc(passed, 1)

            def refine(chain, n0, n1):
                y, t, v = rstd[:, n0:n1], nwt[:, n0:n1], mv[:, n0:n1, 1]
                chain.link(tt_(t, y, y, ALU.mult))
                chain.link(stt(out=t, in0=v, scalar=EPS, in1=t, op0=ALU.add, op1=ALU.mult))
                chain.link(ts_(t, t, -0.5, 1.5, ALU.mult, ALU.add))
                chain.link(tt_(y, y, t, ALU.mult))

            with dve.Fori(0, B) as b:
                def split(u, out, hi, scale, view=lambda x: x):
                    dve.wait_ge(a_hi, b * len(A_HI) + (A_HI.index(u) + 1))
                    low(out, view(a_bank(u)), hi, scale).then_inc(a_drained[a_slot(u)], 1)

                for d in range(DT):
                    split(("xT", d), xT[:, 1, d, :], xT[:, 0, d, :], SX)
                split(("c",), cT[:, 1, :], cT[:, 0, :], 1.0 / SW)

                def low_cat(v):
                    dve.wait_ge(cat_hi, b * (2 * TT) + (v + 1))
                    dst = cat[:, v % 2, :, 2] if v % 2 == 0 else cat[:, v % 2, :, 1]
                    tt_(dst, rows[:, v % 2], cat[:, v % 2, :, 0], ALU.subtract).then_inc(cat_lo, 1)

                def evac_cat(v):
                    dst = (qcT, kcT)[v % 2]
                    t = v // 2
                    for half in range(2):
                        u = ("cat", v, half)
                        wait_a_filled(dve, b, u)
                        nc.vector.tensor_copy(dst[0:3 * HD, half * 8:half * 8 + 8, t * P:(t + 1) * P],
                                              a_bank(u).bitcast(F16)[0:3 * HD, :].rearrange("p (h n) -> p h n", h=8))\
                            .then_inc(a_drained[a_slot(u)], 1)

                for t in range(TT):
                    split(("v", t), vcat[:, t, :, HD:2 * HD], vcat[:, t, :, 0:HD], SV / (SX * SW),
                          lambda x: x.rearrange("p (h n) -> p h n", h=H))
                    if t:
                        evac_cat(2 * t - 2)
                        evac_cat(2 * t - 1)
                    low_cat(2 * t)
                    low_cat(2 * t + 1)
                evac_cat(2 * TT - 2)
                evac_cat(2 * TT - 1)

                def maxima(h):
                    g = h // G
                    if h % G == 0:
                        dve.wait_ge(nm_ready, b * (H // G) + g)
                    dve.wait_ge(max_ready, b * H + (h + 1))
                    for i in (3, 2, 0, 1):
                        o, w = OFF[i + 1], (i + 1) * P
                        nc.vector.tensor_reduce(nmf[:, i, h % G:h % G + 1], max_ps[:, o:o + w], AX, ALU.max, negate=True)\
                            .then_inc(max_done, 1)
                    if h % G == G - 1:
                        dve.wait_ge(max_done, b * (4 * H) + 4 * (h + 1))
                        if g:
                            wait_a_filled(dve, b, ("mT", g - 1))
                        ts_(nm16[:, :, 0:G], nmf[:, :, :], 1.0 / SNM, None, ALU.mult).then_inc(nm_ready, 1)

                def evac_max(g):
                    u = ("mT", g)
                    wait_a_filled(dve, b, u)
                    nc.vector.tensor_copy(mT[:, g % 2, :], a_bank(u).bitcast(F16)[:, 0:S]).then_inc(a_drained[a_slot(u)], 1)

                for h in range(AHEAD):
                    maxima(h)
                evac_max(0)
                for h in range(H):
                    if h + AHEAD < H:
                        maxima(h + AHEAD)
                    if h % G == G - 1 and h < H - 1:
                        evac_max((h + 1) // G)
                    dve.wait_ge(p_hi, b * H + (h + 1))
                    tt_(plo[:, h % 2, POOL_COLS:TRI], pf[:, h % 2, POOL_COLS:TRI], phi[:, h % 2, POOL_COLS:TRI],
                        ALU.subtract).then_inc(p_lo_dve, 1)

                wait_a_drained(dve, b, ("pv", H - 1))
                wait_a_drained(dve, b, ("pv", H - 2))
                chain = Chain(dve, norm_step, b * A_NORM)
                chain.link(nc.vector.reciprocal(rsum[:, :, :], osb[:, :, :, 64]))
                dve.wait_ge(res_loaded, b * 16 + 16)
                for t in range(TT):
                    o3 = att[:, :].rearrange("p (h n) -> p h n", h=H)
                    chain.link(tt_(o3, osb[:, :, t, 0:HD], osb[:, :, t, HD:2 * HD], ALU.add))
                    chain.link(tt_(o3, o3, rsum[:, :, t].unsqueeze(2).to_broadcast([P, H, HD]), ALU.mult))
                    row = resid[:, b * TT + t, :]
                    stt(out=row, in0=att[:, :], scalar=1.0 / SV, in1=x_res[:, t, :], op0=ALU.mult, op1=ALU.add)\
                        .then_inc(res_read, 1)
                    wait_apart(res_read, b * TT + (t + 1))
                    chain.link(nc.vector.bn_stats(stats[:, t, :], row), wait_apart)
                    if t < TT - 1:
                        chain.link(nc.vector.bn_aggr(mv[:, t, :], stats[:, t, :]))
                    else:
                        nc.vector.bn_aggr(mv[:, t, :], stats[:, t, :]).then_inc(var_ready, 1)
                dve.wait_ge(rstd_ready, b + 1)
                refine(chain, 0, TT)
                for t in range(TT):
                    row = resid[:, b * TT + t, :]
                    ts_(row, row, mv[:, t, 0:1], rstd[:, t:t + 1], ALU.subtract, ALU.mult).then_inc(x1_written, 1)
                assert chain.n == A_NORM, chain.n

            chain = Chain(dve, coef_step)
            dve.wait_ge(coef_act, 2)
            chain.link(ts_(coef[:, 4:5], coef[:, 4:5], 1.0, None, ALU.add))
            chain.link(nc.vector.reciprocal(coef[:, 4:5], coef[:, 4:5]))
            chain.link(ts_(coef[:, 6:7], coef[:, 4:5], -1.0, 1.0, ALU.mult, ALU.add))
            chain.link(tt_(coef[:, 6:7], coef[:, 6:7], coef[:, 2:3], ALU.mult))
            chain.link(stt(out=coef[:, 6:7], in0=coef[:, 4:5], scalar=coef[:, 1:2], in1=coef[:, 6:7], op0=ALU.mult, op1=ALU.add))
            chain.link(ts_(coef[:, 6:7], coef[:, 6:7], D ** -0.5, 1.0 / (SX * SX), ALU.mult, ALU.mult))
            chain.link(tt_(coef[:, 7:8], coef[:, 6:7], coef[:, 5:6], ALU.mult))
            assert chain.n == COEF_STEPS
            dve.wait_ge(x1_written, NT)
            dve.wait_ge(bw_hi, 1)
            low(wqw[:, 1].rearrange("p t n -> p (t n)"), raw_q[:, :, :].rearrange("p t n -> p (t n)"),
                wqw[:, 0].rearrange("p t n -> p (t n)"), SW).then_inc(bw_lo, 1)
            for d in range(DT):
                dve.wait_ge(wo_hi, d + 1)
                low(woT[:, 1, d, :], banks[:, 0, :], woT[:, 0, d, :], SW).then_inc(wo_drained, 1)
            with dve.Fori(0, B) as b:
                def split(u, out, hi, scale):
                    dve.wait_ge(b_hi, b * len(B_SPLIT) + (B_HI[u] + 1))
                    bank = b_bank(u)
                    if len(out.shape) == 3:
                        bank = bank.rearrange("p (t n) -> p t n", n=out.shape[-1])
                    low(out, bank, hi, scale).then_inc(b_drained[B_AT[u] % 8], 1)

                for d in range(DT):
                    split(("cT", d), cxT[:, 1, d, :], cxT[:, 0, d, :], SX)
                for d in range(DT):
                    split(("A", d), kq[:, 1, d, :], kq[:, 0, d, :], 1.0 / SW)
                for t in range(4):
                    split(("CW", t), cw[:, 1, t, :], cw[:, 0, t, :], 1.0 / SW)
                for t in range(TT):
                    split(("xT", t), x1T[:, t % 2, 1], x1T[:, t % 2, 0], SX)

                top = Chain(dve, top_step, b * (TT * TOP_STEPS))
                chain = Chain(dve, b_step, b * (TT * B_STEPS))

                def top_k(t):
                    wait_b_drained(dve, b, ("sc", t))
                    wait_apart(att_ready, b * TT + t)
                    sm = small[:, t % 2]
                    src = tsc[:, t, :]
                    top.link(nc.vector.max(top8[:, 0, :], src))
                    top.link(ts_(sm[:, 0:1], top8[:, 0, 0:1], -1.0, None, ALU.mult))
                    top.link(ts_(tm[:, :], src, sm[:, 0:1], None, ALU.add), wait_apart)
                    for r in range((TOPK - 1) // 8):
                        top.link(nc.vector.match_replace(wk[:, r % 2, :], top8[:, r, :], src, -3.0e38), wait_apart)
                        src = wk[:, r % 2, :]
                        top.link(nc.vector.max(top8[:, r + 1, :], src), wait_apart)
                    last = (TOPK - 1) % 8
                    top.link(ts_(sm[:, 1:2], top8[:, (TOPK - 1) // 8, last:last + 1], sm[:, 0:1], None, ALU.add))
                    dve.wait_ge(ex_ready, b * TT + (t + 1))
                    if t >= 2:
                        wait_b_filled(dve, b, ("aT", t - 2))
                    stt(out=attf[:, t % 2, :], in0=tm[:, :], scalar=sm[:, 1:2], in1=ex[:, t % 2, :], op0=ALU.is_ge,
                        op1=ALU.mult, accum_out=sm[:, 2:3]).then_inc(att_ready, 1)

                def turned(t):
                    split(("aT", t), attT[:, t % 2, 1], attT[:, t % 2, 0], SP)

                def norm(t):
                    sm = small[:, t % 2]
                    dve.wait_ge(att_ready, b * TT + (t + 1))
                    chain.link(nc.vector.reciprocal(sm[:, 3:4], sm[:, 2:3]))
                    chain.link(ts_(sm[:, 3:4], sm[:, 3:4], 1.0 / (SP * SX), None, ALU.mult))
                    u = ("out", t)
                    wait_b_filled(dve, b, u)
                    if t == 0:
                        dve.wait_ge(x2_kept, b * 16)
                    row = x2row[:, t, :]
                    stt(out=row, in0=b_bank(u), scalar=sm[:, 3:4], in1=x1row[:, t, :], op0=ALU.mult, op1=ALU.add)\
                        .then_inc(b_drained[B_AT[u] % 8], 1)
                    n = B_AT[u]
                    wait_apart(b_drained[n % 8], b * (B_N // 8) + (n // 8 + 1))
                    chain.link(nc.vector.bn_stats(stats[:, t, :], row), wait_apart)
                    nc.vector.bn_aggr(mv[:, t, :], stats[:, t, :]).then_inc(b_var, 1)

                def finish(t):
                    row = x2row[:, t, :]
                    dve.wait_ge(b_rstd, b * TT + (t + 1))
                    refine(chain, t, t + 1)
                    ts_(row, row, mv[:, t, 0:1], rstd[:, t:t + 1], ALU.subtract, ALU.mult).then_inc(x2_written, 1)

                def low_x2(t):
                    cols = bass.ds(b * S + t * P, P)
                    split(("x2", t), x2T[:, 1, :, cols], x2T[:, 0, :, cols], SX)

                top_k(0)
                for t in range(TT):
                    turned(t)
                    if t + 1 < TT:
                        top_k(t + 1)
                    norm(t)
                    finish(t)
                    if t:
                        low_x2(t - 1)
                low_x2(TT - 1)
                assert top.n == TT * TOP_STEPS, top.n
                assert chain.n == TT * B_STEPS, chain.n

            dve.wait_ge(x2_kept, 16 * B)
            dve.wait_ge(wr_step, 1)
            low(wr16[:, :, E:2 * E], wr_raw[:, :, :], wr16[:, :, 0:E], SW).then_inc(wr_step, 1)
            chain = Chain(dve, r_step)
            chain.link(nc.vector.reciprocal(temp[:, 1:2], temp[:, 0:1]))
            dve.wait_ge(r_act, 1)
            tt3 = rt[:, 2]
            dve_tmp = rt[:, 7]
            tt_(dve_tmp, rt[:, 0], rt[:, 1], ALU.add).then_inc(wr_step, 1)
            dve.wait_ge(wr_step, 3)
            chain.link(ts_(tt3, dve_tmp, temp[:, 1:2], None, ALU.mult))
            dve.wait_ge(r_act, 5)
            inh, e1, fb = rt[:, 3], rt[:, 5], rt[:, 6]
            zone, w, msk, cur, eq, pr, pr2 = (rt[:, n] for n in (7, 8, 9, 10, 11, 12, 13))
            wide = [P, NT, E]

            def over(x):
                return x.unsqueeze(2).to_broadcast(wide)

            chain.link(ts_(zone, inh, float(np.float32(GOLDEN_LOWER)), None, ALU.is_ge))
            chain.link(stt(out=zone, in0=inh, scalar=GOLDEN_UPPER, in1=zone, op0=ALU.is_le, op1=ALU.mult))
            chain.link(tt_(w, e1, zone, ALU.mult))
            wsum, mx, none, some, fsum = (rs1[:, n] for n in range(5))
            chain.link(nc.vector.tensor_reduce(wsum, w, AX, ALU.add))
            chain.link(ts_(none, wsum, 1e-8, None, ALU.is_lt))
            chain.link(ts_(some, none, -1.0, 1.0, ALU.mult, ALU.add))
            chain.link(nc.vector.tensor_copy(cur, fb))
            for pick in range(2):
                chain.link(nc.vector.tensor_reduce(mx, cur, AX, ALU.max))
                chain.link(tt_(eq, cur, over(mx), ALU.is_equal))
                chain.link(nc.vector.tensor_copy(pr, eq))
                src, dst = pr, pr2
                for sh in (1, 2, 4):
                    chain.link(tt_(dst[:, :, sh:E], src[:, :, sh:E], src[:, :, 0:E - sh], ALU.add))
                    chain.link(nc.vector.tensor_copy(dst[:, :, 0:sh], src[:, :, 0:sh]))
                    src, dst = dst, src
                chain.link(stt(out=eq, in0=src, scalar=1.0, in1=eq, op0=ALU.is_equal, op1=ALU.mult))
                if pick == 0:
                    chain.link(nc.vector.tensor_copy(msk, eq))
                    chain.link(stt(out=cur, in0=eq, scalar=-2.0, in1=cur, op0=ALU.mult, op1=ALU.add))
                else:
                    chain.link(tt_(msk, msk, eq, ALU.add))
            chain.link(tt_(msk, fb, msk, ALU.mult))
            chain.link(nc.vector.tensor_reduce(fsum, msk, AX, ALU.add))
            chain.link(ts_(fsum, fsum, 1e-8, None, ALU.max))
            chain.link(nc.vector.reciprocal(fsum, fsum))
            chain.link(tt_(msk, msk, over(fsum), ALU.mult))
            chain.link(tt_(msk, msk, over(none), ALU.mult))
            chain.link(tt_(w, w, over(some), ALU.mult))
            chain.link(tt_(w, w, msk, ALU.add))
            chain.link(nc.vector.tensor_reduce(wsum, w, AX, ALU.add))
            chain.link(ts_(wsum, wsum, 1e-8, None, ALU.max))
            chain.link(nc.vector.reciprocal(wsum, wsum))
            chain.link(ts_(wsum, wsum, 1.0 / (SM * SW), None, ALU.mult))
            chain.link(tt_(wt[:, :, :], w, over(wsum), ALU.mult))

            def low_rank(e, m):
                n = 3 * e + m
                for k, (dst, src) in enumerate(((laT, banks[0:R, 0, :]), (lb16, lb_raw[:, :]))):
                    dve.wait_ge(lora_hi, 2 * n + k + 1)
                    low(dst[:, 1, :], src, dst[:, 0, :], SW).then_inc(lora_lo, 1)
                dve.wait_ge(stage_loaded[m], 16 * (e + 1))
                for t in range(4):
                    dve.wait_ge(lora_mm, 4 * n + t + 1)
                    stt(out=stage[:, m, t, :], in0=banks[:, 1 + t, :], scalar=1.0 / (SW * SW), in1=stage[:, m, t, :],
                        op0=ALU.mult, op1=ALU.add).then_inc(lora_added, 1)

            def low_w(e, par, m):
                dve.wait_ge(e_hi, e * 3 + (m + 1))
                low(w16[:, par, m, 1].rearrange("p t n -> p (t n)"), stage[:, m].rearrange("p t n -> p (t n)"),
                    w16[:, par, m, 0].rearrange("p t n -> p (t n)"), SW).then_inc(e_lo, 1)

            for m in range(3):
                low_rank(0, m)
            for m in range(3):
                low_w(0, 0, m)
            for m in range(3):
                low_rank(1, m)
            for m in range(3):
                low_w(1, 1, m)

            def expert(e, par):
                def hidden(c):
                    for f in range(FT):
                        n = c * FT + f
                        u = ("u", c, f)
                        g = C_AT[("g", c, f)]
                        dve.wait_ge(c_drained[g % 8], e * (C_N // 8) + (g // 8 + 1))
                        wait_c_filled(dve, e, u)
                        if n >= 2:
                            dve.wait_ge(mid_lo, e * (B * FT) + (n - 1))
                        else:
                            dve.wait_ge(mid_lo, e * (B * FT))
                        stt(out=midf[:, n % 2, :], in0=c_bank(u), scalar=SM / (SX * SW), in1=sil[:, n % 2, :],
                            op0=ALU.mult, op1=ALU.mult).then_inc(c_drained[C_AT[u] % 8], 1)

                def add(c):
                    for t in range(TT):
                        u = ("d", c, t)
                        wait_c_filled(dve, e, u)
                        row = resid[:, c * TT + t, :]
                        stt(out=row, in0=c_bank(u), scalar=wt[:, c * TT + t, bass.ds(e, 1)], in1=row,
                            op0=ALU.mult, op1=ALU.add).then_inc(c_drained[C_AT[u] % 8], 1)

                for c in range(B + 1):
                    if c < B:
                        hidden(c)
                    if c:
                        add(c - 1)

            with dve.Fori(0, E // 2 - 1) as pair:
                for par in range(2):
                    expert(pair * 2 + par, par)
                    for m in range(3):
                        low_w((pair * 2 + par) + 2, par, m)
            for par in range(2):
                expert(E - 2 + par, par)

            chain = Chain(dve, f_step)
            for c in range(B):
                for t in range(TT):
                    wait_c_drained(dve, E - 1, ("d", c, t))
                    row = resid[:, c * TT + t, :]
                    chain.link(nc.vector.bn_stats(stats[:, t, :], row))
                    ins = nc.vector.bn_aggr(mv[:, t, :], stats[:, t, :])
                    if t < TT - 1:
                        chain.link(ins)
                    else:
                        ins.then_inc(f_var, 1)
                dve.wait_ge(f_rstd, c + 1)
                refine(chain, 0, TT)
                for t in range(TT):
                    row = resid[:, c * TT + t, :]
                    ins = ts_(row, row, mv[:, t, 0:1], rstd[:, t:t + 1], ALU.subtract, ALU.mult)
                    if t < TT - 1:
                        chain.link(ins)
                    else:
                        ins.then_inc(y_ready, 1)
                        dve.wait_ge(y_ready, c + 1)


AHEAD = 5
POOL_COLS = 896
A_NORM = 1 + 4 * TT - 1 + 4
TOP_STEPS = 3 + 2 * ((TOPK - 1) // 8) + 1
B_STEPS = 3 + 4
COEF_STEPS = 7


def rotary_tables():
    freqs = np.float32(1.0) / np.float32(10000.0) ** (np.arange(0, ROPE, 2, dtype=np.float32) / np.float32(ROPE))
    emb = np.arange(S, dtype=np.float32)[:, None] * freqs[None, :].astype(np.float32)
    c, s = np.cos(emb), np.sin(emb)
    both = np.stack([np.stack([c, s], -1), np.stack([s, c], -1)])
    return np.ascontiguousarray(both.reshape(2, TT, P, ROPE // 2, 2).transpose(2, 0, 1, 3, 4)).astype(np.float32)


def kernel(**inputs):
    import concourse.bacc as bacc
    from concourse.bass_utils import run_bass_kernel_spmd

    names = {"x": "x", "ctx": "ctx_2048", "Wq": "L0_attn_Wq", "Wkv": "L0_attn_Wkv_down", "Wku": "L0_attn_Wk_up",
             "Wvu": "L0_attn_Wv_up", "W_qkv": "L0_xattn_W_qkv", "W_o": "L0_xattn_W_o", "beta_q": "L0_xattn_beta_q",
             "beta_k": "L0_xattn_beta_k", "gate": "L0_xattn_gate", "log_tau": "L0_xattn_log_tau", "Wg": "L0_ffn_Wg",
             "Wu": "L0_ffn_Wu", "Wd": "L0_ffn_Wd", "Ga": "L0_ffn_Ga", "Gb": "L0_ffn_Gb", "Ua": "L0_ffn_Ua",
             "Ub": "L0_ffn_Ub", "Da": "L0_ffn_Da", "Db": "L0_ffn_Db", "Wr": "L0_ffn_Wr", "temperature": "L0_ffn_temperature"}
    nc = bacc.Bacc("TRN2", target_bir_lowering=False, num_devices=1)
    arrays, aps = {}, {}
    for short, name in names.items():
        v = np.ascontiguousarray(inputs[name])
        if v.size == 1:
            v = v.reshape(1, 1)
        arrays[short] = v
    arrays["cossin"] = rotary_tables()
    for short, v in arrays.items():
        aps[short] = nc.dram_tensor("in_" + short, v.shape, mybir.dt.from_np(v.dtype), kind="ExternalInput").ap()
    y = nc.dram_tensor("y", (N, D), F32, kind="ExternalOutput")
    aps["y"] = y.ap()
    decoder(nc, aps)
    r = run_bass_kernel_spmd(nc, [{"in_" + k: v for k, v in arrays.items()}], core_ids=[0])
    return r.results[0]["y"].reshape(B, S, D)
```

```python
import math
from contextlib import ExitStack

import numpy as np

import concourse.bass as bass
from concourse import mybir
from concourse.alu_op_type import AluOpType as ALU

ACT = mybir.ActivationFunctionType
AX = mybir.AxisListType.X
F32 = mybir.dt.float32
F16 = mybir.dt.float16
BF16 = mybir.dt.bfloat16

P = 128
B, S, D = 4, 512, 512
H, HD, NOPE = 16, 32, 8
ROPE = HD - NOPE
LAT = 128
E, F, R = 8, 512, 64
NL = 2
TOPK = 54
TT = S // P
DT = D // P
FT = F // P
N = B * S
NT = N // P
EPS = 1e-5
NEG = -1.0e30

SX = 16.0
SW = 64.0
SQ = 4.0
SV = 16.0
SP = 1024.0
SM = 64.0
SNM = 64.0

G = 4
TRI = sum((i + 1) * P for i in range(TT))
OFF = {4: 0, 3: 512, 1: 896, 2: 1024}

AHEAD = 5
A_NEXT = ("xT", "c", "row", "rope", "rhi", "rlo", "v", "cat0", "bqn", "maxn", "mTn")
A_KIND = {"mTn": "mT"}
A_PER = {"xT": DT, "c": 1, "row": 2 * TT, "v": TT, "cat0": 2 * TT, "cat1": 2 * TT, "mT": H // G, "pv": H}
A_BANK = {"xT": (7, 7, 6, 7),
          "cat1": (6, 6, 6, 6, 6, 7, 7, 7),
          "c": (7,),
          "pv": (6, 7, 7, 7, 6, 6, 6, 6, 7, 6, 7, 6, 6, 7, 7, 6),
          "row": (7, 6, 6, 6, 7, 7, 7, 7),
          "mT": (None, 6, 6, 6),
          "v": (7, 6, 6, 6),
          "cat0": (7, 7, 7, 7, 6, 7, 6, 7),
          "mTn": (7,)}


def steps(text):
    return [(k, int(i)) for k, i in (word.split(".") for word in text.split())]


A_PE = steps("""
    xT.0 cat1.0 bk.0 xT.1 cat1.1 bq.5 xT.2 xT.3 bk.1 cat1.2 row.0 cat1.3 bq.6 c.0 cat1.4 bk.2 cat1.5 row.1 bq.7
    cat1.6 pv.0 v.0 row.2 cat1.7 bk.3 mT.1 bq.8 pv.1 bk.4 v.1 pv.2 bq.9 row.3 row.4 bk.5 bq.10 v.2 pv.3 bk.6
    pv.4 row.5 bq.11 bk.7 cat0.0 pv.5 cat0.1 bq.12 mT.2 row.6 bq.13 bk.8 cat0.2 pv.6 row.7 bq.14 bk.9 cat0.3
    cat0.4 bq.15 cat0.5 pv.7 bk.10 mT.3 pv.8 cat0.6 bk.11 cat0.7 pv.9 bk.12 bqn.0 pv.10 bk.13 pv.11 bqn.1 bk.14
    pv.12 bqn.2 bk.15 pv.13 bqn.3 v.3 pv.14 bqn.4 mTn.0 pv.15
""")
A_ACT = steps("""
    xT.0 xT.1 exp.0 xT.2 xT.3 exp.1 hi.0 row.0 c.0 hi.1 row.1 exp.2 pv.0 hi.2 v.0 rhi.0 row.2 exp.3 rhi.1 hi.3
    pv.1 v.1 exp.4 pv.2 rhi.2 row.3 hi.4 row.4 exp.5 v.2 pv.3 hi.5 exp.6 row.5 pv.4 hi.6 rhi.3 exp.7 pv.5 hi.7
    ln.0 row.6 rhi.4 rhi.5 exp.8 row.7 hi.8 pv.6 exp.9 rhi.6 rhi.7 pv.7 hi.9 exp.10 pv.8 hi.10 exp.11 hi.11
    exp.12 pv.9 hi.12 pv.10 exp.13 pv.11 hi.13 exp.14 hi.14 pv.12 exp.15 pv.13 hi.15 v.3 pv.14 pv.15
""")
A_DVE = steps("""
    xT.0 cat1.0 cat1.1 xT.1 max.5 xT.2 xT.3 cat1.2 res.0 cat1.3 res.1 max.6 c.0 cat1.4 lo.0 cat1.5 cat1.6 lo.1
    max.7 v.0 cat1.7 mT.1 res.2 lo.2 max.8 v.1 rlo.0 max.9 res.3 rlo.1 lo.3 rlo.2 lo.4 max.10 v.2 comb.0 lo.5
    max.11 lo.6 cat0.0 cat0.1 max.12 rlo.3 mT.2 max.13 lo.7 cat0.2 rlo.4 rlo.5 max.14 lo.8 cat0.3 cat0.4 max.15
    cat0.5 rlo.6 rlo.7 mT.3 cat0.6 lo.9 lo.10 cat0.7 ln.0 maxn.0 lo.11 comb.1 lo.12 maxn.1 lo.13 comb.2 maxn.2
    lo.14 maxn.3 v.3 lo.15 mTn.0 maxn.4 comb.3
""")
A_POOL = steps("""
    rope.0 lo.0 lo.1 rope.1 lo.2 rope.2 lo.3 rope.3 lo.4 lo.5 rope.4 lo.6 rope.5 lo.7 rope.6 rope.7 lo.8 lo.9
    lo.10 lo.11 lo.12 lo.13 lo.14 lo.15
""")


def next_part(seq, kinds):
    return [u for u in seq if u[0] in kinds]


def own_part(seq, kinds):
    return [u for u in seq if u[0] not in kinds]


A_FIN = [("res", t) for t in range(TT)] + [("ln", 0)]


def _four(kind, *ts):
    return [(kind, t) for t in ts or range(4)]


B_BODY_PE = steps("""
    aT.0 aT.1 cT.0 cT.1 xT.0 cT.2 cT.3 out.0 xT.1 A.0 A.1 A.2 A.3 aT.2 out.1 aT.3 out.2 out.3 sc.0 xT.2 sc.1
    xT.3 CW.0 sc.2 CW.1 x2.0 x2.1 x2.2 CW.2 sc.3 CW.3 x2.3
""")
B_BODY_ACT = steps("""
    aT.0 cT.0 cT.1 cT.2 cT.3 A.0 top.2 aT.1 A.1 xT.0 top.3 A.2 aT.2 aT.3 xT.1 A.3 ln.0 sc.0 sc.1 xT.2 xT.3 x2.0
    x2.1 first.0 CW.0 sc.2 CW.1 first.1 x2.2 CW.2 CW.3 x2.3 sc.3
""")
B_BODY_DVE = steps("""
    aT.0 top.2 aT.1 norm.0 aT.2 norm.1 aT.3 xT.0 norm.2 norm.3 xT.1 ln.0 xT.2 xT.3 first.0 x2.0 x2.1 x2.2 x2.3
""")
B_BODY_POOL = steps("""
    cT.0 cT.1 cT.2 cT.3 A.0 A.1 A.2 A.3 CW.0 CW.1 CW.2 CW.3
""")
B_FIRST = [(k, t) for k in ("cT", "A") for t in range(4)]
B_FIRST += [("xT", 0), ("xT", 1), ("sc", 0), ("xT", 2), ("sc", 1), ("xT", 3), ("sc", 2), ("sc", 3), ("first", 0), ("first", 1)]
B_FIRST += [("CW", t) for t in range(4)]
B_LAST = _four("aT", 0, 1) + _four("lr", 0) + _four("out", 0, 1) + _four("top", 2, 3) + _four("norm", 0, 1) + \
    _four("lr", 1) + _four("aT", 2, 3) + _four("out", 2, 3) + _four("lr", 2) + _four("norm", 2, 3) + _four("lr", 3, 4) + \
    _four("ln", 0) + _four("x2") + _four("lr", 5)
B_BANK = {"aT": (3, 0, 2, 3),
          "cT": (7, 1, 2, 4),
          "out": (3, 0, 2, 3),
          "xT": (6, 7, 4, 7),
          "A": (4, 5, 2, 1),
          "sc": (2, 1, 7, 6),
          "CW": (1, 4, 5, 4),
          "x2": (3, 0, 2, 1)}
COPIED = {"cT": (0, 1, 0, 1), "A": (2, 3, 2, 3), "CW": (0, 1, 0, 1)}
B_NEXT = ("cT", "A", "CW", "xT", "sc")


def bank_before(bank, seq, n, earlier):
    at = lambda u: bank[u[0]][u[1]] if u[0] in bank else None
    for m in range(n - 1, -1, -1):
        if at(seq[m]) == at(seq[n]):
            return seq[m], False
    for u in reversed(earlier):
        if at(u) == at(seq[n]):
            return u, True
    return None, False


C_SEQ = []
for _c in range(B + 1):
    if _c < B:
        C_SEQ += [(x, _c, f) for f in range(FT) for x in ("g", "u")]
    if _c:
        C_SEQ += [("d", _c - 1, t) for t in range(TT)]
C_AT = {u: n for n, u in enumerate(C_SEQ)}
C_N = len(C_SEQ)
assert C_N % 8 == 0

GOLDEN_CENTER = 1.0 / math.e
GOLDEN_LOWER = 0.5 - math.log(4.0 / 3.0)
GOLDEN_UPPER = 0.5


class Chain:

    def __init__(self, eng, sem, base=0):
        self.eng, self.sem, self.base, self.n = eng, sem, base, 0

    def link(self, ins, wait=None):
        self.n += 1
        ins.then_inc(self.sem, 1)
        (wait or self.eng.wait_ge)(self.sem, self.base + self.n)

    def step(self, ins):
        self.n += 1
        ins.then_inc(self.sem, 1)

    def passed(self, wait=None):
        (wait or self.eng.wait_ge)(self.sem, self.base + self.n)


def decoder(nc, a):
    ctx = ExitStack()

    def sem(name):
        return ctx.enter_context(nc.semaphore(name))

    def sb(stack, name, shape, dt=F32):
        return stack.enter_context(nc.sbuf_tensor(name, shape, dt))

    with ctx:
        banks = ctx.enter_context(nc.psum_tensor("banks", [P, 8, 512], F32))
        max_ps = banks[:, 0:3, :].rearrange("p b n -> p (b n)")
        st_ps = banks[:, 3:6, :].rearrange("p b n -> p (b n)")
        resid = sb(ctx, "resid", [P, NT, D])
        identf = sb(ctx, "identf", [P, P])
        ident16 = sb(ctx, "ident16", [P, P], F16)
        identb = sb(ctx, "identb", [P, P], BF16)
        eps = sb(ctx, "eps", [P, 1])
        negc = sb(ctx, "negc", [P, 1])
        stats = sb(ctx, "stats", [P, TT, 6])
        mv = sb(ctx, "mv", [P, TT, 2])
        lnv = sb(ctx, "lnv", [P, TT])
        rstd = sb(ctx, "rstd", [P, TT])
        nwt = sb(ctx, "nwt", [P, TT])
        coef = sb(ctx, "coef", [P, 8])
        wr_raw = sb(ctx, "wr_raw", [P, DT, E])
        wr16 = sb(ctx, "wr16", [P, DT, 2 * E], F16)
        temp = sb(ctx, "temp", [P, 2])

        sa = ctx.enter_context(ExitStack())
        x_in = sb(sa, "x_in", [P, TT, D])
        x_res = sb(sa, "x_res", [P, TT, D])
        xT = sb(sa, "xT", [P, 2, DT, S], F16)
        cT = sb(sa, "cT", [P, 2, S], F16)
        wq = sb(sa, "wq", [P, 2, DT, D], F16)
        wkvd = sb(sa, "wkvd", [P, 2, DT, LAT], F16)
        wku = sb(sa, "wku", [P, 2, D], F16)
        wvu = sb(sa, "wvu", [P, 2, D], F16)
        rows = sb(sa, "rows", [P, 4, H, HD])
        turn_a = sb(sa, "turn_a", [P, H, ROPE // 2, 2])
        turn_b = sb(sa, "turn_b", [P, H, ROPE // 2, 2])
        cossin = sb(sa, "cossin", [P, 2, TT, ROPE // 2, 2])
        cat = sb(sa, "cat", [P, 2 * TT, H, 3, HD], F16)
        qcT = sb(sa, "qcT", [P, H, S], F16)
        kcT = sb(sa, "kcT", [P, H, S], F16)
        vcat = sb(sa, "vcat", [P, H, TT, 66], F16)
        vnext = sb(sa, "vnext", [P, H, TT, 66], F16)
        pf = sb(sa, "pf", [P, 2, TRI])
        phi = sb(sa, "phi", [P, 2, TRI], F16)
        plo = sb(sa, "plo", [P, 2, TRI], F16)
        osb = sb(sa, "osb", [P, 2, G, TT, 65])
        nmf = sb(sa, "nmf", [P, TT, G])
        nm16 = sb(sa, "nm16", [P, TT, P], F16)
        mT = sb(sa, "mT", [P, 2, S], F16)
        sel = sb(sa, "sel", [P, G, P], F16)
        mask_qk = sb(sa, "mask_qk", [P, P], BF16)
        mask_kq = sb(sa, "mask_kq", [P, P], BF16)
        rsum = sb(sa, "rsum", [P, G, TT])
        att = sb(sa, "att", [P, TT, D])
        raw_wq = pf[:, :, :].rearrange("p a n -> p (a n)")[:, 0:DT * D].rearrange("p (t n) -> p t n", t=DT)
        raw_osb = osb[:, :, :, :, :].rearrange("p a h t n -> p (a h t n)")
        raw_kvd = raw_osb[:, 0:DT * LAT].rearrange("p (t n) -> p t n", t=DT)
        raw_ku = raw_osb[:, 512:1024]
        raw_vu = raw_osb[:, 1024:1536]
        sa.close()

        x2T = sb(ctx, "x2T", [P, 2, DT, N], F16)
        stage = sb(ctx, "stage", [P, 3, 4, 512])
        la_raw = sb(ctx, "la_raw", [P, 4, R])
        lb_raw = sb(ctx, "lb_raw", [R, 512])
        laT = sb(ctx, "laT", [R, 2, 512], F16)
        lb16 = sb(ctx, "lb16", [R, 2, 512], F16)
        copyf = sb(ctx, "copyf", [P, 4, 512])
        fold = copyf[:, 0:2, :]
        ca = ctx.enter_context(ExitStack())
        c_raw = sb(ca, "c_raw", [P, 4, D])
        cxT = sb(ca, "cxT", [P, 2, DT, 512], F16)
        wqw = sb(ca, "wqw", [P, 2, 4, D], F16)
        woT = sb(ca, "woT", [P, 2, DT, D], F16)
        kq = sb(ca, "kq", [P, 2, DT, 512], F16)
        cw = sb(ca, "cw", [P, 2, 4, D], F16)
        x1row = sb(ca, "x1row", [P, TT, D])
        x2row = sb(ca, "x2row", [P, TT, D])
        x1T = sb(ca, "x1T", [P, 2, 2, DT, P], F16)
        tsc = sb(ca, "tsc", [P, 4, 512])
        raw_q, raw_o = x2row, tsc
        wk = sb(ca, "wk", [P, 2, 2, 512])
        top8 = sb(ca, "top8", [P, 2, 7, 8])
        small = sb(ca, "small", [P, TT, 4])
        ex = sb(ca, "ex", [P, 2, 512])
        attf = sb(ca, "attf", [P, TT, 512])
        attT = sb(ca, "attT", [P, 2, 2, 4, P], F16)
        ca.close()

        w16 = sb(ctx, "w16", [P, 2, 3, 2, 4, 512], F16)
        mid16 = sb(ctx, "mid16", [P, 2, 2, FT, 512], F16)
        sil = sb(ctx, "sil", [P, 2, 512])
        midf = sb(ctx, "midf", [P, 2, 512])
        rt = sb(ctx, "rt", [P, 14, NT, E])
        rs1 = sb(ctx, "rs1", [P, 8, NT])
        wt = sb(ctx, "wt", [P, NT, E])

        w_loaded = sem("w_loaded")
        consts = sem("consts")
        sel_ready = sem("sel_ready")
        w_hi = sem("w_hi")
        w_lo = sem("w_lo")
        x_loaded = sem("x_loaded")
        res_loaded = sem("res_loaded")
        a_ready = {k: sem(f"a_{k}_ready") for k in A_PER}
        a_hi = {k: sem(f"a_{k}_hi") for k in ("xT", "c", "v")}
        a_drained = {k: sem(f"a_{k}_drained") for k in A_PER}
        v_moved = [sem(f"v_moved{k}") for k in range(2)]
        comb_done = sem("comb_done")
        roped = sem("roped")
        cat_hi = sem("cat_hi")
        cat_lo = sem("cat_lo")
        max_ready = sem("max_ready")
        max_done = sem("max_done")
        nm_ready = sem("nm_ready")
        st_ready = sem("st_ready")
        exp_done = sem("exp_done")
        p_hi = sem("p_hi")
        p_lo_pool = sem("p_lo_pool")
        p_lo_dve = sem("p_lo_dve")
        norm_step = sem("norm_step")
        res_read = sem("res_read")
        comb_step = sem("comb_step")
        passed = sem("passed")
        var_ready = sem("var_ready")
        ln_done = sem("ln_done")
        rstd_ready = sem("rstd_ready")
        x1_written = sem("x1_written")
        b_loaded = sem("b_loaded")
        s_loaded = sem("s_loaded")
        coef_step = sem("coef_step")
        coef_act = sem("coef_act")
        ctx_loaded = sem("ctx_loaded")
        bw_hi = sem("bw_hi")
        bw_lo = sem("bw_lo")
        wo_ready = sem("wo_ready")
        wo_hi = sem("wo_hi")
        wo_drained = sem("wo_drained")
        b_ready = {k: sem(f"b_{k}_ready") for k in B_BANK}
        b_hi = {k: sem(f"b_{k}_hi") for k in B_BANK}
        b_low = {k: sem(f"b_{k}_low") for k in COPIED}
        b_drained = {k: sem(f"b_{k}_drained") for k in B_BANK}
        top_step = [sem(f"top_step{j}") for j in range(2)]
        neg_ready = sem("neg_ready")
        ex_ready = sem("ex_ready")
        att_ready = sem("att_ready")
        b_step = sem("b_step")
        b_var = sem("b_var")
        b_ln = sem("b_ln")
        b_rstd = sem("b_rstd")
        x2_written = sem("x2_written")
        x1_fetched = sem("x1_fetched")
        x2_kept = sem("x2_kept")
        stage_loaded = [sem(f"stage{m}_loaded") for m in range(3)]
        lora_loaded = sem("lora_loaded")
        la_turned = sem("la_turned")
        lora_hi = sem("lora_hi")
        lora_lo = sem("lora_lo")
        lora_mm = sem("lora_mm")
        lora_out = sem("lora_out")
        lora_added = sem("lora_added")
        e_hi = sem("e_hi")
        e_lo = sem("e_lo")
        wr_step = sem("wr_step")
        logits_ready = sem("logits_ready")
        r_act = sem("r_act")
        r_step = sem("r_step")
        wt_ready = sem("wt_ready")
        c_ready = sem("c_ready")
        c_drained = [sem(f"c_bank{k}_drained") for k in range(8)]
        mid_hi = sem("mid_hi")
        mid_lo = sem("mid_lo")
        f_step = sem("f_step")
        f_var = sem("f_var")
        f_ln = sem("f_ln")
        f_rstd = sem("f_rstd")
        y_ready = sem("y_ready")
        y_stored = sem("y_stored")

        def a_bank(u):
            return banks[:, A_BANK[u[0]][u[1]], :]

        def a_count(b, u):
            return b * A_PER[A_KIND.get(u[0], u[0])] + (u[1] + 1)

        def a_upto(b, u):
            return b * A_PER[A_KIND.get(u[0], u[0])] + (u[1] + 1 + FREE)

        def b_bank(u):
            return banks[:, B_BANK[u[0]][u[1]], :]

        def count(b, u):
            return b * 4 + (u[1] + 1)

        def upto(b, u):
            return b * 4 + (u[1] + 1 + FREE)

        def c_bank(u):
            return banks[:, C_AT[u] % 8, :]

        def wait_c_filled(eng, e, u):
            eng.wait_ge(c_ready, e * C_N + (C_AT[u] + 1))

        def wait_c_free(eng, e, u):
            n = C_AT[u]
            eng.wait_ge(c_drained[n % 8], e * (C_N // 8) + (n // 8 + FREE))

        def wait_c_drained(eng, e, u):
            n = C_AT[u]
            eng.wait_ge(c_drained[n % 8], e * (C_N // 8) + (n // 8 + 1 + FREE))

        K3 = 3 * HD
        LORA = [("Ga", "Gb"), ("Ua", "Ub"), ("Da", "Db")]
        WN = ["Wg", "Wu", "Wd"]

        block = ctx.enter_context(nc.Block())

        @block.sync
        def _(sp):
            sp.dma_start(raw_wq, a["Wq"].rearrange("(t p) n -> p t n", p=P)).then_inc(w_loaded, 16)
            sp.dma_start(raw_kvd, a["Wkv"].rearrange("(t p) n -> p t n", p=P)).then_inc(w_loaded, 16)
            sp.dma_start(raw_ku, a["Wku"]).then_inc(w_loaded, 16)
            sp.dma_start(raw_vu, a["Wvu"]).then_inc(w_loaded, 16)
            sp.dma_start(cossin[:, :, :, :, :], a["cossin"]).then_inc(w_loaded, 16)
            sp.dma_start(wr_raw[:, :, :], a["Wr"].rearrange("(t p) e -> p t e", p=P)).then_inc(s_loaded, 16)
            for n, name in enumerate(("gate", "beta_q", "beta_k", "log_tau")):
                sp.dma_start(coef[:, n:n + 1], a[name].partition_broadcast(P)).then_inc(s_loaded, 16)
            sp.dma_start(temp[:, 0:1], a["temperature"].partition_broadcast(P)).then_inc(s_loaded, 16)
            def load_x(dst, b, done):
                sp.dma_start(dst[:, :, :], a["x"][b].rearrange("(t p) d -> p t d", p=P)).then_inc(done, 16)

            load_x(x_in, 0, x_loaded)

            def move_values(b, half):
                heads = slice(half * 8, half * 8 + 8)
                sp.wait_ge(a_ready["pv"], a_upto(b - 1, ("pv", half * 8 + 7)))
                sp.dma_start(vcat[:, heads], vnext[:, heads]).then_inc(v_moved[half], 16)

            with sp.Fori(0, B - 1) as b:
                sp.wait_ge(a_ready["xT"], a_upto(b, ("xT", DT - 1)))
                load_x(x_in, b + 1, x_loaded)
                sp.wait_ge(a_drained["v"], a_upto(b, ("v", TT - 1)))
                move_values(b, 0)
                move_values(b, 1)
                sp.wait_ge(res_read, b * TT + FREE)
                load_x(x_res, b, res_loaded)
            sp.wait_ge(a_drained["v"], a_upto(B - 1, ("v", TT - 1)))
            move_values(B - 1, 0)
            move_values(B - 1, 1)
            sp.wait_ge(res_read, (B - 1) * TT + FREE)
            load_x(x_res, B - 1, res_loaded)

            sp.wait_ge(x1_written, NT)
            sp.dma_start(raw_q[:, :, :], a["W_qkv"][0:D].rearrange("(t p) n -> p t n", p=P)).then_inc(b_loaded, 16)
            sp.dma_start(raw_o[:, :, :], a["W_o"].rearrange("(t p) n -> p t n", p=P)).then_inc(b_loaded, 16)
            def load_x1(b):
                sp.dma_start(x1row[:, :, :], resid[:, bass.ds(b * TT, TT), :]).then_inc(x1_fetched, 16)

            def load_context(b):
                sp.dma_start(c_raw[:, :, :], a["ctx"][b].rearrange("(t p) d -> p t d", p=P)).then_inc(ctx_loaded, 16)

            load_context(0)
            load_x1(0)
            for m in range(3):
                sp.dma_start(stage[:, m], a[WN[m]][0].rearrange("(t p) n -> p t n", p=P)).then_inc(stage_loaded[m], 16)
            with sp.Fori(0, B - 1) as b:
                sp.wait_ge(b_ready["cT"], upto(b, ("cT", 3)))
                load_context(b + 1)
                sp.wait_ge(b_ready["xT"], upto(b, ("xT", 3)))
                load_x1(b + 1)

            for e in range(NL):
                for m in range(3):
                    n = 3 * e + m
                    if n:
                        sp.wait_ge(lora_lo, 2 * n)
                    sp.dma_start(la_raw[:, :, :], a[LORA[m][0]][e].rearrange("(t p) r -> p t r", p=P)).then_inc(lora_loaded, 16)
                    sp.dma_start(lb_raw[:, :], a[LORA[m][1]][e]).then_inc(lora_loaded, 16)
                    if 1 <= n <= 3:
                        sp.wait_ge(e_lo, n)
                        sp.dma_start(stage[:, n - 1], a[WN[n - 1]][1].rearrange("(t p) n -> p t n", p=P)).then_inc(stage_loaded[n - 1], 16)
            with sp.Fori(1, E - 1) as e:
                for m in range(3):
                    sp.wait_ge(e_lo, e * 3 + (m + 1))
                    sp.dma_start(stage[:, m], a[WN[m]][e + 1].rearrange("(t p) n -> p t n", p=P)).then_inc(stage_loaded[m], 16)
            y = a["y"].rearrange("(c t p) d -> c p t d", p=P, t=TT)
            for c in range(B - 1):
                sp.wait_ge(y_ready, c * TT + TT)
                sp.dma_start(y[c], resid[:, c * TT:(c + 1) * TT, :]).then_inc(y_stored, 16)
            for t in range(TT):
                sp.wait_ge(y_ready, (B - 1) * TT + (t + 1))
                sp.dma_start(y[B - 1, :, t], resid[:, (B - 1) * TT + t, :]).then_inc(y_stored, 16)
            sp.wait_ge(y_stored, 16 * (B - 1 + TT))

        @block.gpsimd
        def _(pool):
            for s in [max_done, st_ready, exp_done, p_lo_pool, p_lo_dve, roped, cat_lo, nm_ready, v_moved[0], v_moved[1], comb_done, res_read,
                      att_ready, x2_kept, mid_lo] + c_drained + \
                    [d[k] for d in (a_ready, a_drained) for k in A_PER] + [d[k] for d in (b_ready, b_drained) for k in B_BANK] + \
                    [b_low[k] for k in COPIED]:
                pool.sem_inc(s, FREE)
            for t in (identf, ident16, identb):
                pool.memset(t[:, :], 0.0).then_inc(consts, 1)
            pool.memset(mask_qk[:, :], 0.0).then_inc(consts, 1)
            pool.memset(mask_kq[:, :], 0.0).then_inc(consts, 1)
            pool.memset(sel[:, :, :], 0.0).then_inc(consts, 1)
            pool.memset(eps[:, :], EPS).then_inc(consts, 1)
            pool.memset(negc[:, :], -GOLDEN_CENTER).then_inc(consts, 1)
            pool.memset(nm16[:, :, :], 0.0).then_inc(consts, 1)
            pool.memset(vnext[:, :, :, 64:66], 1.0).then_inc(consts, 1)
            pool.wait_ge(consts, 10)
            for t in (identf, ident16, identb):
                pool.affine_select(out=t[:, :], in_=t[:, :], compare_op=ALU.not_equal, fill=1.0, base=0,
                                   pattern=[[-1, P]], channel_multiplier=1).then_inc(consts, 1)
            pool.affine_select(out=mask_qk[:, :], in_=mask_qk[:, :], compare_op=ALU.is_ge, fill=NEG, base=0,
                               pattern=[[-1, P]], channel_multiplier=1).then_inc(consts, 1)
            pool.affine_select(out=mask_kq[:, :], in_=mask_kq[:, :], compare_op=ALU.is_ge, fill=NEG, base=0,
                               pattern=[[1, P]], channel_multiplier=-1).then_inc(consts, 1)
            pool.affine_select(out=sel[:, :, :], in_=sel[:, :, :], compare_op=ALU.not_equal, fill=SNM, base=0,
                               pattern=[[-1, G], [0, P]], channel_multiplier=1).then_inc(consts, 1)

            pool.wait_ge(w_loaded, 80)

            def heads(seq, b, nxt):
                for k, i in seq:
                    if k == "rope":
                        n, t = nxt * (2 * TT) + i, i // 2
                        pool.wait_ge(a_drained["row"], a_upto(nxt, ("row", i)))
                        pool.wait_ge(roped, n * 4 + FREE)
                        pair = rows[:, i % 4, :, NOPE:HD].rearrange("p h (i two) -> p h i two", two=2)
                        for j, dst in ((0, turn_a), (1, turn_b)):
                            cs = cossin[:, j, t].unsqueeze(1).to_broadcast([P, H, ROPE // 2, 2])
                            nc.gpsimd.tensor_tensor(dst[:, :, :, :], pair, cs, ALU.mult).then_inc(roped, 1)
                        pool.wait_ge(roped, n * 4 + (2 + FREE))
                        half = NOPE + ROPE // 2
                        nc.gpsimd.tensor_tensor(rows[:, i % 4, :, NOPE:half], turn_a[:, :, :, 0], turn_a[:, :, :, 1],
                                                ALU.subtract).then_inc(roped, 1)
                        nc.gpsimd.tensor_tensor(rows[:, i % 4, :, half:HD], turn_b[:, :, :, 1], turn_b[:, :, :, 0],
                                                ALU.add).then_inc(roped, 1)
                    elif k == "lo":
                        pool.wait_ge(p_hi, b * H + (i + 1))
                        nc.gpsimd.tensor_tensor(plo[:, i % 2, 0:POOL_COLS], pf[:, i % 2, 0:POOL_COLS],
                                                phi[:, i % 2, 0:POOL_COLS], ALU.subtract).then_inc(p_lo_pool, 1)

            heads(next_part(A_POOL, A_NEXT), None, 0)
            with pool.Fori(0, B - 1) as b:
                heads(A_POOL, b, b + 1)
            heads(own_part(A_POOL, A_NEXT), B - 1, None)

            def cross(seq, nxt):
                for k, t in seq:
                    dst = {"cT": cxT, "A": kq, "CW": cw}[k]
                    pool.wait_ge(b_hi[k], count(nxt, (k, t)))
                    nc.gpsimd.tensor_tensor(dst[:, 1, t, :], copyf[:, COPIED[k][t], :], dst[:, 0, t, :], ALU.subtract)\
                        .then_inc(b_low[k], 1)

            cross([u for u in B_FIRST if u[0] in COPIED], 0)
            with pool.Fori(0, B - 1) as b:
                cross(B_BODY_POOL, b + 1)

            for n in range(2 * 3 * TT):
                m, t = n // TT % 3, n % TT
                if t == 0:
                    pool.wait_ge(stage_loaded[m], 16 * (n // (3 * TT) + 1))
                pool.wait_ge(lora_out, n + 1)
                nc.gpsimd.tensor_tensor(stage[:, m, t, :], stage[:, m, t, :], fold[:, n % 2, :], ALU.add).then_inc(lora_added, 1)

            with pool.Fori(0, E) as e:
                for n in range(B * FT):
                    pool.wait_ge(mid_hi, e * (B * FT) + (n + 1))
                    c, f = n // FT, n % FT
                    nc.gpsimd.tensor_tensor(mid16[:, c % 2, 1, f, :], midf[:, n % 2, :], mid16[:, c % 2, 0, f, :],
                                            ALU.subtract).then_inc(mid_lo, 1)

        @block.tensor
        def _(pe):
            def three(out, l, r, n, done=None):
                for i in range(n):
                    for j, (x, y) in enumerate(((0, 0), (0, 1), (1, 0))):
                        mm = nc.tensor.matmul(out, l(x, i), r(y, i), start=(i == 0 and j == 0),
                                              stop=(i == n - 1 and j == 2))
                if done is not None:
                    mm.then_inc(done, 1)
                return mm

            pe.wait_ge(consts, 16)
            pe.wait_ge(w_lo, 4)
            def heads(seq, b, nxt, earlier):
                for n, (k, i) in enumerate(seq):
                    u = (k, i)
                    own = nxt if k in A_NEXT else b
                    if k in A_BANK:
                        bank, done = a_bank(u), a_ready[A_KIND.get(k, k)]
                        v, before = bank_before(A_BANK, seq, n, earlier)
                        if v is not None:
                            of = nxt if v[0] in A_NEXT else b
                            pe.wait_ge(a_drained[A_KIND.get(v[0], v[0])], a_upto(of - 1 if before else of, v))
                    if k == "xT":
                        if i == 0:
                            pe.wait_ge(x_loaded, own * 16 + 16)
                        for t in range(TT):
                            mm = nc.tensor.transpose(bank[:, t * P:(t + 1) * P], x_in[:, t, i * P:(i + 1) * P], identf[:, :])
                        mm.then_inc(done, 1)
                    elif k == "c":
                        pe.wait_ge(a_drained["xT"], a_upto(own, ("xT", DT - 1)))
                        three(bank, lambda x, j: wkvd[:, x, j, :], lambda y, j: xT[:, y, j, :], DT, done)
                    elif k == "row":
                        ts = slice(i // 2 * P, (i // 2 + 1) * P)
                        if i == 0:
                            pe.wait_ge(a_drained["xT"], a_upto(own, ("xT", DT - 1)))
                        if i % 2 == 0:
                            three(bank, lambda x, j: xT[:, x, j, ts], lambda y, j: wq[:, y, j, :], DT, done)
                        else:
                            if i == 1:
                                pe.wait_ge(a_drained["c"], a_upto(own, ("c", 0)))
                            three(bank, lambda x, j: cT[:, x, ts], lambda y, j: wku[:, y, :], 1, done)
                    elif k == "v":
                        if i == 0:
                            pe.wait_ge(a_drained["c"], a_upto(own, ("c", 0)))
                        three(bank, lambda x, j: cT[:, x, i * P:(i + 1) * P], lambda y, j: wvu[:, y, :], 1, done)
                    elif k in ("cat0", "cat1"):
                        pe.wait_ge(cat_lo, own * (2 * TT) + (i + 1 + FREE))
                        out = bank.bitcast(F16)
                        for j in range(8):
                            src = cat[:, i, (k == "cat1") * 8 + j].rearrange("p a n -> p (a n)")
                            mm = nc.tensor.transpose(out[0:K3, j * P:(j + 1) * P], src, ident16[:, :])
                        mm.then_inc(done, 1)
                    elif k in ("bq", "bqn"):
                        pe.wait_ge(max_done, (own * H + i) * 4 + FREE)
                        if k == "bqn" and i == 0:
                            pe.wait_ge(a_drained["cat0"], a_upto(own, ("cat0", 2 * TT - 1)))
                        if k == "bq" and i == 8:
                            pe.wait_ge(a_drained["cat1"], a_upto(own, ("cat1", 2 * TT - 1)))
                        for t in range(TT):
                            w = (t + 1) * P
                            o = OFF[t + 1]
                            nc.tensor.matmul(max_ps[:, o:o + w], qcT[0:K3, i, t * P:(t + 1) * P], kcT[0:K3, i, 0:w],
                                             start=True, stop=False)
                            mm = nc.tensor.matmul(max_ps[:, o + w - P:o + w], identb[:, :], mask_qk[:, :],
                                                  start=False, stop=True)
                        mm.then_inc(max_ready, 1)
                    elif k in ("mT", "mTn"):
                        pe.wait_ge(nm_ready, own * (H // G) + (i + 1 + FREE))
                        out = bank.bitcast(F16)
                        for t in range(TT):
                            mm = nc.tensor.transpose(out[:, t * P:(t + 1) * P], nm16[:, t, :], ident16[:, :])
                        mm.then_inc(done, 1)
                    elif k == "bk":
                        if i % G == 0:
                            pe.wait_ge(a_drained["mT"], a_upto(own, ("mT", i // G)))
                        pe.wait_ge(exp_done, own * H + (i + FREE))
                        for t in range(TT):
                            w = S - t * P
                            o = OFF[TT - t]
                            nc.tensor.matmul(st_ps[:, o:o + w], kcT[0:K3, i, t * P:(t + 1) * P], qcT[0:K3, i, t * P:S],
                                             start=True, stop=False)
                            nc.tensor.matmul(st_ps[:, o:o + P], identb[:, :], mask_kq[:, :], start=False, stop=False)
                            mm = nc.tensor.matmul(st_ps[:, o:o + w], sel[:, i % G, :], mT[:, (i // G) % 2, t * P:S],
                                                  start=False, stop=True)
                        mm.then_inc(st_ready, 1)
                    elif k == "pv":
                        pe.wait_ge(p_lo_pool, own * H + (i + 1 + FREE))
                        pe.wait_ge(p_lo_dve, own * H + (i + 1 + FREE))
                        if i % 8 == 0:
                            pe.wait_ge(v_moved[i // 8], own * 16 + (16 + FREE))
                        for q in range(TT):
                            out = bank[:, q * 65:(q + 1) * 65]
                            for t in range(q + 1):
                                o = OFF[TT - t] + (q - t) * P
                                for x, w in enumerate((phi, plo)):
                                    mm = nc.tensor.matmul(out, w[:, i % 2, o:o + P], vcat[:, i, t, 0:65],
                                                          start=(t == 0 and x == 0), stop=(t == q and x == 1))
                        mm.then_inc(done, 1)

            heads(next_part(A_PE, A_NEXT), None, 0, [])
            for k in ("xT", "c", "row", "v", "cat0"):
                pe.wait_ge(a_drained[k], a_upto(0, (k, A_PER[k] - 1)))
            pe.wait_ge(a_drained["mT"], a_upto(0, ("mT", 0)))
            with pe.Fori(0, B - 1) as b:
                heads(A_PE, b, b + 1, A_PE)
            heads(own_part(A_PE, A_NEXT), B - 1, B, A_PE)

            pe.wait_ge(x1_written, NT)
            pe.wait_ge(b_loaded, 32)
            for d in range(DT):
                if d:
                    pe.wait_ge(wo_drained, d)
                for t in range(4):
                    mm = nc.tensor.transpose(banks[:, 0, t * P:(t + 1) * P], raw_o[:, t, d * P:(d + 1) * P], identf[:, :])
                mm.then_inc(wo_ready, 1)
            pe.wait_ge(wo_drained, DT)
            pe.wait_ge(bw_lo, 1)

            def low_rank(n):
                pe.wait_ge(lora_loaded, 32 * (n + 1))
                if n:
                    pe.wait_ge(lora_lo, 2 * n)
                for t in range(4):
                    mm = nc.tensor.transpose(banks[0:R, 4, t * P:(t + 1) * P], la_raw[:, t, :], identf[:, :])
                mm.then_inc(la_turned, 1)
                pe.wait_ge(lora_lo, 2 * (n + 1))
                for t in range(4):
                    ts = slice(t * P, (t + 1) * P)
                    if 4 * n + t >= 3:
                        pe.wait_ge(lora_out, 4 * n + t - 2)
                    three(banks[:, 5 + (4 * n + t) % 3, :], lambda x, i: laT[:, x, ts], lambda y, i: lb16[:, y, :], 1, lora_mm)

            def cross(seq, b, nxt, earlier):
                for n, (k, t) in enumerate(seq):
                    u = (k, t)
                    own = nxt if k in B_NEXT else b
                    if k in B_BANK:
                        v, before = bank_before(B_BANK, seq, n, earlier)
                        if v is not None:
                            of = nxt if v[0] in B_NEXT else b
                            pe.wait_ge(b_drained[v[0]], upto(of - 1 if before else of, v))
                        bank = b_bank(u)
                    if k == "cT":
                        if t == 0:
                            pe.wait_ge(ctx_loaded, own * 16 + 16)
                        for i in range(4):
                            mm = nc.tensor.transpose(bank[:, i * P:(i + 1) * P], c_raw[:, i, t * P:(t + 1) * P], identf[:, :])
                        mm.then_inc(b_ready[k], 1)
                    elif k == "A":
                        if t == 0:
                            pe.wait_ge(b_low["cT"], upto(own, ("cT", 3)))
                        three(bank, lambda x, i: wqw[:, x, i, t * P:(t + 1) * P], lambda y, i: cxT[:, y, i, :], 4, b_ready[k])
                    elif k == "CW":
                        if t == 0:
                            pe.wait_ge(b_low["cT"], upto(own, ("cT", 3)))
                        three(bank, lambda x, i: cxT[:, x, i, t * P:(t + 1) * P], lambda y, i: woT[:, y, i, :], 4, b_ready[k])
                    elif k in ("xT", "aT", "x2"):
                        if k == "xT" and t == 0:
                            pe.wait_ge(x1_fetched, own * 16 + 16)
                        if k == "aT":
                            pe.wait_ge(att_ready, upto(own, u))
                        if k == "x2":
                            pe.wait_ge(x2_written, count(own, u))
                        src = {"xT": x1row[:, t, :], "aT": attf[:, t, :], "x2": x2row[:, t, :]}[k]
                        for i in range(4):
                            mm = nc.tensor.transpose(bank[:, i * P:(i + 1) * P], src[:, i * P:(i + 1) * P], identf[:, :])
                        mm.then_inc(b_ready[k], 1)
                    elif k == "sc":
                        pe.wait_ge(b_drained["xT"], upto(own, ("xT", t)))
                        if t == 0:
                            pe.wait_ge(b_low["A"], upto(own, ("A", 3)))
                        three(bank, lambda x, i: x1T[:, t % 2, x, i, :], lambda y, i: kq[:, y, i, :], DT, b_ready[k])
                    elif k == "out":
                        pe.wait_ge(b_drained["aT"], upto(own, ("aT", t)))
                        if t == 0:
                            pe.wait_ge(b_low["CW"], upto(own, ("CW", 3)))
                        three(bank, lambda x, i: attT[:, t % 2, x, i, :], lambda y, i: cw[:, y, i, :], 4, b_ready[k])
                    elif k == "lr":
                        low_rank(t)

            cross(B_FIRST, None, 0, [])
            for k in ("A", "CW", "xT", "sc"):
                pe.wait_ge(b_drained[k], upto(0, (k, 3)))
            with pe.Fori(0, B - 1) as b:
                cross(B_BODY_PE, b, b + 1, B_BODY_PE)
            for k in ("CW", "sc"):
                pe.wait_ge(b_drained[k], upto(B - 1, (k, 3)))
            cross(B_LAST, B - 1, B, B_BODY_PE)

            for k in ("aT", "out", "x2"):
                pe.wait_ge(b_drained[k], upto(B - 1, (k, 3)))
            pe.wait_ge(wr_step, 2)
            for t in range(NT):
                ts = slice(t * P, (t + 1) * P)
                out = banks[:, 0, t * 16:(t + 1) * 16]
                for i in range(DT):
                    for x in range(2):
                        mm = nc.tensor.matmul(out, x2T[:, x, i, ts], wr16[:, i, :], start=(i == 0 and x == 0),
                                              stop=(i == DT - 1 and x == 1))
            mm.then_inc(logits_ready, 1)

            pe.wait_ge(lora_out, 24)
            pe.wait_ge(r_act, 1)

            def expert(e, par):
                def ffn_in(c):
                    cs = slice(c * 512, (c + 1) * 512)
                    for f in range(FT):
                        for m, name in enumerate("gu"):
                            u = (name, c, f)
                            wait_c_free(pe, e, u)
                            if c == 0 and f == 0:
                                pe.wait_ge(e_lo, e * 3 + (m + 1))
                            three(c_bank(u), lambda x, i: w16[:, par, m, x, i, f * P:(f + 1) * P],
                                  lambda y, i: x2T[:, y, i, cs], DT, c_ready)

                def ffn_out(c):
                    pe.wait_ge(mid_lo, e * (B * FT) + (FT * (c + 1) + FREE))
                    if c == 0:
                        pe.wait_ge(e_lo, e * 3 + 3)
                    for t in range(TT):
                        u = ("d", c, t)
                        wait_c_free(pe, e, u)
                        three(c_bank(u), lambda x, i: mid16[:, c % 2, x, i, t * P:(t + 1) * P],
                              lambda y, i: w16[:, par, 2, y, i, :], FT, c_ready)

                for c in range(B + 1):
                    if c < B:
                        ffn_in(c)
                    if c:
                        ffn_out(c - 1)

            with pe.Fori(0, E // 2) as pair:
                for par in range(2):
                    expert(pair * 2 + par, par)

        @block.scalar
        def _(act):
            def scaled(out, in_, scale):
                return nc.scalar.activation(out, in_, ACT.Copy, scale=scale)

            act.wait_ge(w_loaded, 80)
            scaled(wq[:, 0], raw_wq, SW).then_inc(w_hi, 1)
            scaled(wkvd[:, 0], raw_kvd, SW).then_inc(w_hi, 1)
            scaled(wku[:, 0], raw_ku, SW).then_inc(w_hi, 1)
            scaled(wvu[:, 0], raw_vu, SW).then_inc(w_hi, 1)
            act.wait_ge(w_lo, 4)
            act.wait_ge(consts, 16)

            def heads(seq, b, nxt):
                for k, i in seq:
                    u = (k, i)
                    own = nxt if k in A_NEXT else b
                    was = None if b is None else b - 1
                    if k in ("xT", "c", "row", "v", "pv"):
                        act.wait_ge(a_ready[k], a_upto(own, u))
                    if k == "xT":
                        if i == 0:
                            act.wait_ge(a_ready["row"], a_upto(own - 1, ("row", 2 * TT - 2)))
                        scaled(xT[:, 0, i, :], a_bank(u), SX).then_inc(a_hi[k], 1)
                    elif k == "c":
                        act.wait_ge(a_ready["v"], a_upto(own - 1, ("v", TT - 1)))
                        scaled(cT[:, 0, :], a_bank(u), 1.0 / SW).then_inc(a_hi[k], 1)
                    elif k == "row":
                        act.wait_ge(cat_lo, own * (2 * TT) + (i - 3 + FREE))
                        scaled(rows[:, i % 4], a_bank(u).rearrange("p (h n) -> p h n", h=H), SQ / (SX * SW))\
                            .then_inc(a_drained[k], 1)
                    elif k == "v":
                        if i == 0:
                            act.wait_ge(v_moved[0], own * 16 + FREE)
                            act.wait_ge(v_moved[1], own * 16 + FREE)
                        scaled(vnext[:, :, i, 0:HD], a_bank(u).rearrange("p (h n) -> p h n", h=H), SV / (SX * SW))\
                            .then_inc(a_hi[k], 1)
                    elif k == "rhi":
                        act.wait_ge(roped, own * (8 * TT) + (4 * (i + 1) + FREE))
                        act.wait_ge(a_ready["cat1"], a_upto(own - 1, ("cat1", i)))
                        dst = cat[:, i, :, 0:2] if i % 2 == 0 else cat[:, i, :, 0:3:2]
                        scaled(dst, rows[:, i % 4].unsqueeze(2).to_broadcast([P, H, 2, HD]), 1.0).then_inc(cat_hi, 1)
                    elif k == "exp":
                        g = own * H + i
                        act.wait_ge(st_ready, g + (1 + FREE))
                        act.wait_ge(p_lo_pool, g + (FREE - 1))
                        act.wait_ge(p_lo_dve, g + (FREE - 1))
                        nc.scalar.activation(pf[:, i % 2, :], st_ps[:, 0:TRI], ACT.Exp,
                                             scale=1.0 / (SQ * SQ * math.sqrt(HD))).then_inc(exp_done, 1)
                    elif k == "hi":
                        g = own * H + i
                        act.wait_ge(exp_done, g + (1 + FREE))
                        act.wait_ge(a_ready["pv"], g + (FREE - 1))
                        scaled(phi[:, i % 2, :], pf[:, i % 2, :], 1.0).then_inc(p_hi, 1)
                    elif k == "pv":
                        if i % G == 0:
                            act.wait_ge(comb_done, own * (H // G) + (i // G - 1 + FREE))
                        scaled(osb[:, i // G % 2, i % G], a_bank(u)[:, 0:TT * 65].rearrange("p (t n) -> p t n", t=TT), 1.0)\
                            .then_inc(a_drained[k], 1)
                    elif k == "ln":
                        act.wait_ge(var_ready, was * TT + TT)
                        nc.scalar.activation(lnv[:, :], mv[:, :, 1], ACT.Ln, bias=eps[:, 0:1]).then_inc(ln_done, 1)
                        act.wait_ge(ln_done, was + 1)
                        nc.scalar.activation(rstd[:, :], lnv[:, :], ACT.Exp, scale=-0.5).then_inc(rstd_ready, 1)

            heads(next_part(A_ACT, A_NEXT), None, 0)
            heads(own_part(A_ACT, ("res", "ln")), 0, 1)
            with act.Fori(1, B - 1) as b:
                heads(A_ACT, b, b + 1)
            heads(own_part(A_ACT, A_NEXT), B - 1, None)
            heads(A_FIN, B, None)

            act.wait_ge(s_loaded, 96)
            nc.scalar.activation(coef[:, 4:5], coef[:, 0:1], ACT.Exp, scale=-1.0).then_inc(coef_act, 1)
            nc.scalar.activation(coef[:, 5:6], coef[:, 3:4], ACT.Exp).then_inc(coef_act, 1)
            scaled(wr16[:, :, 0:E], wr_raw[:, :, :], SW).then_inc(wr_step, 1)
            act.wait_ge(x1_written, NT)
            act.wait_ge(b_loaded, 32)
            scaled(wqw[:, 0], raw_q[:, :, :], SW).then_inc(bw_hi, 1)
            for d in range(DT):
                act.wait_ge(wo_ready, d + 1)
                scaled(woT[:, 0, d, :], banks[:, 0, :], SW).then_inc(wo_hi, 1)
            act.wait_ge(coef_step, COEF_STEPS)

            def low_rank(n):
                act.wait_ge(la_turned, n + 1)
                if n:
                    act.wait_ge(lora_mm, 4 * n)
                scaled(laT[:, 0, :], banks[0:R, 4, :], SW).then_inc(lora_hi, 1)
                scaled(lb16[:, 0, :], lb_raw[:, :], SW).then_inc(lora_hi, 1)
                for t in range(4):
                    i = 4 * n + t
                    act.wait_ge(lora_mm, i + 1)
                    if i >= 2:
                        act.wait_ge(lora_added, i - 1)
                    scaled(fold[:, i % 2, :], banks[:, 5 + i % 3, :], 1.0 / (SW * SW)).then_inc(lora_out, 1)
                if n < 3:
                    act.wait_ge(lora_added, 4 * (n + 1))
                    scaled(w16[:, 0, n, 0], stage[:, n], SW).then_inc(e_hi, 1)

            def cross(seq, b, nxt):
                for k, t in seq:
                    u = (k, t)
                    own = nxt if k in B_NEXT else b
                    if k in COPIED:
                        dst, scale = {"cT": (cxT[:, 0, t, :], SX), "A": (kq[:, 0, t, :], 1.0 / SW), "CW": (cw[:, 0, t, :], 1.0 / SW)}[k]
                        copy = copyf[:, COPIED[k][t], :]
                        before = {"cT": (own - 1, ("CW", t + 2)), "A": (own - 1, ("A", t + 2)), "CW": (own, ("cT", t + 2))}[k] \
                            if t < 2 else (own, (k, t - 2))
                        act.wait_ge(b_low[before[1][0]], upto(*before))
                        act.wait_ge(b_ready[k], upto(own, u))
                        scaled(copy, b_bank(u), scale).then_inc(b_drained[k], 1)
                        if t == 0:
                            if k == "CW":
                                act.wait_ge(b_ready["out"], upto(own - 1, ("out", 3)))
                            if k == "A":
                                act.wait_ge(b_ready["sc"], upto(own - 1, ("sc", 3)))
                            if k == "cT":
                                act.wait_ge(b_ready["CW"], upto(own - 1, ("CW", 3)))
                        act.wait_ge(b_drained[k], upto(own, u))
                        scaled(dst, copy, 1.0).then_inc(b_hi[k], 1)
                    elif k in ("xT", "aT", "x2"):
                        act.wait_ge(b_ready[k], upto(own, u))
                        if k == "aT":
                            act.wait_ge(b_ready["out"], upto(own, u) - 2)
                        if k == "xT":
                            act.wait_ge(b_ready["sc"], upto(own, u) - 2)
                        dst = {"xT": lambda: x1T[:, t % 2, 0], "aT": lambda: attT[:, t % 2, 0],
                               "x2": lambda: x2T[:, 0, :, bass.ds(own * S + t * P, P)]}[k]()
                        src = b_bank(u).rearrange("p (t n) -> p t n", n=P)
                        scale = {"xT": SX, "aT": SP, "x2": SX}[k]
                        scaled(dst, src, scale).then_inc(b_hi[k], 1)
                        if u == ("x2", 3):
                            act.dma_start(resid[:, bass.ds(own * TT, TT), :], x2row[:, :, :]).then_inc(x2_kept, 16)
                    elif k == "sc":
                        act.wait_ge(b_ready[k], upto(own, u))
                        act.wait_ge(att_ready, upto(own - 1, u))
                        nc.scalar.activation(tsc[:, t, :], b_bank(u), ACT.Copy, scale=coef[:, 7:8]).then_inc(b_drained[k], 1)
                    elif k in ("top", "first"):
                        g = (b if k == "top" else nxt) * TT + t
                        act.wait_ge(neg_ready, g + 1)
                        act.wait_ge(att_ready, g - 1 + FREE)
                        nc.scalar.activation(ex[:, t % 2, :], tsc[:, t, :], ACT.Exp, bias=small[:, t, 0:1]).then_inc(ex_ready, 1)
                    elif k == "ln":
                        act.wait_ge(b_var, b * TT + TT)
                        nc.scalar.activation(lnv[:, :], mv[:, :, 1], ACT.Ln, bias=eps[:, 0:1]).then_inc(b_ln, 1)
                        act.wait_ge(b_ln, b + 1)
                        nc.scalar.activation(rstd[:, :], lnv[:, :], ACT.Exp, scale=-0.5).then_inc(b_rstd, 1)
                    elif k == "lr":
                        low_rank(t)

            act.wait_ge(bw_lo, 1)
            act.wait_ge(wo_drained, DT)
            cross(B_FIRST, None, 0)
            with act.Fori(0, B - 1) as b:
                cross(B_BODY_ACT, b, b + 1)
            act.wait_ge(b_low["CW"], upto(B - 1, ("CW", 3)))
            cross(B_LAST, B - 1, B)

            act.wait_ge(x2_written, NT)
            act.wait_ge(logits_ready, 1)
            scaled(rt[:, 0:2].rearrange("p a t e -> p t a e"), banks[:, 0, 0:NT * 16].rearrange("p (t a e) -> p t a e", t=NT, a=2),
                   1.0 / (SX * SW)).then_inc(r_act, 1)
            act.wait_ge(r_step, 2)
            nc.scalar.activation(rt[:, 3], rt[:, 2], ACT.Sigmoid).then_inc(r_act, 1)
            act.wait_ge(r_act, 2)
            nc.scalar.activation(rt[:, 4], rt[:, 3], ACT.Abs, bias=negc[:, 0:1]).then_inc(r_act, 1)
            act.wait_ge(r_act, 3)
            nc.scalar.activation(rt[:, 5], rt[:, 4], ACT.Exp, scale=-1.0 / 0.1).then_inc(r_act, 1)
            nc.scalar.activation(rt[:, 6], rt[:, 4], ACT.Exp, scale=-1.0 / 0.3).then_inc(r_act, 1)

            for m in range(3):
                act.wait_ge(b_ready["out"], upto(B - 1, ("out", 3)))
                act.wait_ge(lora_added, 4 * (m + 4))
                scaled(w16[:, 1, m, 0], stage[:, m], SW).then_inc(e_hi, 1)

            def final_norm(c):
                act.wait_ge(f_var, (c + 1) * TT)
                nc.scalar.activation(lnv[:, :], mv[:, :, 1], ACT.Ln, bias=eps[:, 0:1]).then_inc(f_ln, 1)
                act.wait_ge(f_ln, c + 1)
                nc.scalar.activation(rstd[:, :], lnv[:, :], ACT.Exp, scale=-0.5).then_inc(f_rstd, 1)

            def expert(e, par, last=False):
                for c in range(B):
                    for f in range(FT):
                        if last and c >= 2 and f == FT // 2:
                            final_norm(c - 2)
                        n = c * FT + f
                        u = ("g", c, f)
                        wait_c_filled(act, e, u)
                        nc.scalar.activation(sil[:, n % 2, :], c_bank(u), ACT.Silu, scale=1.0 / (SX * SW))\
                            .then_inc(c_drained[C_AT[u] % 8], 1)
                        wait_c_drained(act, e, ("u", c, f))
                        scaled(mid16[:, c % 2, 0, f, :], midf[:, n % 2, :], 1.0).then_inc(mid_hi, 1)

            with act.Fori(0, E // 2 - 1) as pair:
                for par in range(2):
                    expert(pair * 2 + par, par)
                    for m in range(3):
                        wait_c_filled(act, pair * 2 + par, ("d", B - 1, TT - 1))
                        act.wait_ge(stage_loaded[m], (pair * 2 + par) * 16 + 48)
                        scaled(w16[:, par, m, 0], stage[:, m], SW).then_inc(e_hi, 1)
            for par in range(2):
                expert(E - 2 + par, par, par == 1)
            for c in (B - 2, B - 1):
                final_norm(c)

        @block.vector
        def _(dve):
            ts_, tt_, stt = nc.vector.tensor_scalar, nc.vector.tensor_tensor, nc.vector.scalar_tensor_tensor

            def low(out, src, hi, scale):
                return stt(out=out, in0=src, scalar=scale, in1=hi, op0=ALU.mult, op1=ALU.subtract)

            dve.wait_ge(w_loaded, 80)
            for n, (w, raw) in enumerate(((wq, raw_wq), (wkvd, raw_kvd), (wku, raw_ku), (wvu, raw_vu))):
                dve.wait_ge(w_hi, n + 1)
                if len(raw.shape) == 3:
                    low(w[:, 1].rearrange("p t n -> p (t n)"), raw.rearrange("p t n -> p (t n)"),
                        w[:, 0].rearrange("p t n -> p (t n)"), SW).then_inc(w_lo, 1)
                else:
                    low(w[:, 1], raw, w[:, 0], SW).then_inc(w_lo, 1)
            dve.wait_ge(consts, 16)

            def wait_apart(signal, value):
                dve.wait_ge(signal, value)
                dve.sem_inc(passed, 1)

            def refine(chain, n0, n1):
                y, t, v = rstd[:, n0:n1], nwt[:, n0:n1], mv[:, n0:n1, 1]
                chain.link(tt_(t, y, y, ALU.mult))
                chain.link(stt(out=t, in0=v, scalar=EPS, in1=t, op0=ALU.add, op1=ALU.mult))
                chain.link(ts_(t, t, -0.5, 1.5, ALU.mult, ALU.add))
                chain.link(tt_(y, y, t, ALU.mult))

            def heads(seq, b, nxt):
                for k, i in seq:
                    u = (k, i)
                    own = nxt if k in A_NEXT else b
                    if k in ("xT", "c", "v"):
                        dve.wait_ge(a_hi[k], a_count(own, u))
                        if k == "xT":
                            ins = low(xT[:, 1, i, :], a_bank(u), xT[:, 0, i, :], SX)
                        elif k == "c":
                            ins = low(cT[:, 1, :], a_bank(u), cT[:, 0, :], 1.0 / SW)
                        else:
                            ins = low(vnext[:, :, i, HD:2 * HD], a_bank(u).rearrange("p (h n) -> p h n", h=H),
                                      vnext[:, :, i, 0:HD], SV / (SX * SW))
                        ins.then_inc(a_drained[k], 1)
                    elif k == "rlo":
                        dve.wait_ge(cat_hi, own * (2 * TT) + (i + 1))
                        dst = cat[:, i, :, 2] if i % 2 == 0 else cat[:, i, :, 1]
                        tt_(dst, rows[:, i % 4], cat[:, i, :, 0], ALU.subtract).then_inc(cat_lo, 1)
                    elif k in ("cat0", "cat1"):
                        half = int(k == "cat1")
                        dve.wait_ge(a_ready[k], a_upto(own, u))
                        if i == 0:
                            dve.wait_ge(st_ready, (own - 1) * H + (8 * half + 8 + FREE))
                        nc.vector.tensor_copy((qcT, kcT)[i % 2][0:K3, half * 8:half * 8 + 8, i // 2 * P:(i // 2 + 1) * P],
                                              a_bank(u).bitcast(F16)[0:K3, :].rearrange("p (h n) -> p h n", h=8))\
                            .then_inc(a_drained[k], 1)
                    elif k in ("max", "maxn"):
                        g = own * H + i
                        if i % G == 0:
                            dve.wait_ge(nm_ready, own * (H // G) + (i // G + FREE))
                        dve.wait_ge(max_ready, g + 1)
                        for t in (3, 2, 0, 1):
                            o, w = OFF[t + 1], (t + 1) * P
                            nc.vector.tensor_reduce(nmf[:, t, i % G:i % G + 1], max_ps[:, o:o + w], AX, ALU.max, negate=True)\
                                .then_inc(max_done, 1)
                        if i % G == G - 1:
                            dve.wait_ge(max_done, g * 4 + (4 + FREE))
                            dve.wait_ge(a_ready["mT"], own * (H // G) + (i // G + FREE))
                            ts_(nm16[:, :, 0:G], nmf[:, :, :], 1.0 / SNM, None, ALU.mult).then_inc(nm_ready, 1)
                    elif k in ("mT", "mTn"):
                        dve.wait_ge(a_ready["mT"], a_upto(own, u))
                        nc.vector.tensor_copy(mT[:, i % 2, :], a_bank(u).bitcast(F16)[:, 0:S]).then_inc(a_drained["mT"], 1)
                    elif k == "lo":
                        dve.wait_ge(p_hi, own * H + (i + 1))
                        tt_(plo[:, i % 2, POOL_COLS:TRI], pf[:, i % 2, POOL_COLS:TRI], phi[:, i % 2, POOL_COLS:TRI],
                            ALU.subtract).then_inc(p_lo_dve, 1)
                    elif k == "comb":
                        chain = Chain(dve, comb_step, own * (2 * H // G) + 2 * i)
                        dve.wait_ge(comb_done, own * (H // G) + (i + FREE))
                        dve.wait_ge(a_drained["pv"], a_upto(own, ("pv", i * G + G - 1)))
                        src = osb[:, i % 2]
                        o4 = att[:, :, i * P:(i + 1) * P].rearrange("p t (h n) -> p h t n", h=G)
                        chain.link(nc.vector.reciprocal(rsum[:, :, :], src[:, :, :, 64]))
                        chain.link(tt_(o4, src[:, :, :, 0:HD], src[:, :, :, HD:2 * HD], ALU.add))
                        tt_(o4, o4, rsum[:, :, :].unsqueeze(3).to_broadcast([P, G, TT, HD]), ALU.mult).then_inc(comb_done, 1)
                    elif k == "res":
                        was = b - 1
                        chain = Chain(dve, norm_step, was * A_NORM + i)
                        dve.wait_ge(comb_done, b * (H // G) + FREE)
                        dve.wait_ge(res_loaded, was * 16 + 16)
                        row = resid[:, was * TT + i, :]
                        stt(out=row, in0=att[:, i, :], scalar=1.0 / SV, in1=x_res[:, i, :], op0=ALU.mult, op1=ALU.add)\
                            .then_inc(res_read, 1)
                        wait_apart(res_read, was * TT + (i + 1 + FREE))
                        chain.link(nc.vector.bn_stats(stats[:, i, :], row), wait_apart)
                        nc.vector.bn_aggr(mv[:, i, :], stats[:, i, :]).then_inc(var_ready, 1)
                    elif k == "ln":
                        was = b - 1
                        chain = Chain(dve, norm_step, was * A_NORM + TT)
                        dve.wait_ge(rstd_ready, was + 1)
                        refine(chain, 0, TT)
                        for t in range(TT):
                            row = resid[:, was * TT + t, :]
                            ts_(row, row, mv[:, t, 0:1], rstd[:, t:t + 1], ALU.subtract, ALU.mult).then_inc(x1_written, 1)
                        assert chain.n == A_NORM - TT, chain.n

            heads(next_part(A_DVE, A_NEXT), None, 0)
            heads(own_part(A_DVE, ("res", "ln")), 0, 1)
            with dve.Fori(1, B - 1) as b:
                heads(A_DVE, b, b + 1)
            heads(own_part(A_DVE, A_NEXT), B - 1, None)
            heads(A_FIN, B, None)

            chain = Chain(dve, coef_step)
            dve.wait_ge(coef_act, 2)
            chain.link(ts_(coef[:, 4:5], coef[:, 4:5], 1.0, None, ALU.add))
            chain.link(nc.vector.reciprocal(coef[:, 4:5], coef[:, 4:5]))
            chain.link(ts_(coef[:, 6:7], coef[:, 4:5], -1.0, 1.0, ALU.mult, ALU.add))
            chain.link(tt_(coef[:, 6:7], coef[:, 6:7], coef[:, 2:3], ALU.mult))
            chain.link(stt(out=coef[:, 6:7], in0=coef[:, 4:5], scalar=coef[:, 1:2], in1=coef[:, 6:7], op0=ALU.mult, op1=ALU.add))
            chain.link(ts_(coef[:, 6:7], coef[:, 6:7], D ** -0.5, 1.0 / (SX * SX), ALU.mult, ALU.mult))
            chain.link(tt_(coef[:, 7:8], coef[:, 6:7], coef[:, 5:6], ALU.mult))
            assert chain.n == COEF_STEPS
            dve.wait_ge(wr_step, 1)
            low(wr16[:, :, E:2 * E], wr_raw[:, :, :], wr16[:, :, 0:E], SW).then_inc(wr_step, 1)
            dve.wait_ge(x1_written, NT)
            dve.wait_ge(bw_hi, 1)
            low(wqw[:, 1].rearrange("p t n -> p (t n)"), raw_q[:, :, :].rearrange("p t n -> p (t n)"),
                wqw[:, 0].rearrange("p t n -> p (t n)"), SW).then_inc(bw_lo, 1)
            for d in range(DT):
                dve.wait_ge(wo_hi, d + 1)
                low(woT[:, 1, d, :], banks[:, 0, :], woT[:, 0, d, :], SW).then_inc(wo_drained, 1)

            def low_w(e, par, m):
                dve.wait_ge(e_hi, e * 3 + (m + 1))
                low(w16[:, par, m, 1].rearrange("p t n -> p (t n)"), stage[:, m].rearrange("p t n -> p (t n)"),
                    w16[:, par, m, 0].rearrange("p t n -> p (t n)"), SW).then_inc(e_lo, 1)

            def low_rank(n):
                for k, (dst, src) in enumerate(((laT, banks[0:R, 4, :]), (lb16, lb_raw[:, :]))):
                    dve.wait_ge(lora_hi, 2 * n + k + 1)
                    low(dst[:, 1, :], src, dst[:, 0, :], SW).then_inc(lora_lo, 1)

            def top_k(t0, b):
                first = b * (TT // 2) + t0 // 2
                steps_of = [Chain(dve, top_step[j], first * TOP_STEPS) for j in range(2)]
                srcs = [tsc[:, t0 + j, :] for j in range(2)]
                for j in range(2):
                    t = t0 + j
                    dve.wait_ge(b_drained["sc"], upto(b, ("sc", t)))
                    wait_apart(att_ready, b * TT + (t0 + FREE))
                    steps_of[j].step(nc.vector.max(top8[:, j, 0, :], srcs[j]))
                for j in range(2):
                    steps_of[j].passed()
                    ts_(small[:, t0 + j, 0:1], top8[:, j, 0, 0:1], -1.0, None, ALU.mult).then_inc(neg_ready, 1)
                for r in range((TOPK - 1) // 8):
                    for j in range(2):
                        steps_of[j].passed(wait_apart)
                        steps_of[j].step(nc.vector.match_replace(wk[:, j, r % 2, :], top8[:, j, r, :], srcs[j], -3.0e38))
                        srcs[j] = wk[:, j, r % 2, :]
                    for j in range(2):
                        steps_of[j].passed(wait_apart)
                        steps_of[j].step(nc.vector.max(top8[:, j, r + 1, :], srcs[j]))
                dve.wait_ge(b_ready["aT"], upto(b - 1, ("aT", t0 + 1)))
                for j in range(2):
                    t = t0 + j
                    steps_of[j].passed()
                    dve.wait_ge(ex_ready, b * TT + (t + 1))
                    kth = top8[:, j, (TOPK - 1) // 8, (TOPK - 1) % 8:(TOPK - 1) % 8 + 1]
                    stt(out=attf[:, t, :], in0=tsc[:, t, :], scalar=kth, in1=ex[:, t % 2, :], op0=ALU.is_ge,
                        op1=ALU.mult, accum_out=small[:, t, 2:3]).then_inc(att_ready, 1)

            def cross(seq, b, nxt):
                chain = None if b is None else Chain(dve, b_step, b * B_STEPS)
                for k, t in seq:
                    u = (k, t)
                    own = nxt if k in B_NEXT else b
                    if k in ("xT", "aT", "x2"):
                        dve.wait_ge(b_hi[k], count(own, u))
                        dst = {"xT": lambda h: x1T[:, t % 2, h], "aT": lambda h: attT[:, t % 2, h],
                               "x2": lambda h: x2T[:, h, :, bass.ds(own * S + t * P, P)]}[k]
                        src = b_bank(u).rearrange("p (t n) -> p t n", n=P)
                        scale = {"xT": SX, "aT": SP, "x2": SX}[k]
                        low(dst(1), src, dst(0), scale).then_inc(b_drained[k], 1)
                    elif k in ("top", "first"):
                        if t % 2 == 0:
                            top_k(t, b if k == "top" else nxt)
                    elif k == "norm":
                        sm = small[:, t]
                        dve.wait_ge(att_ready, upto(b, u))
                        chain.link(nc.vector.reciprocal(sm[:, 3:4], sm[:, 2:3]))
                        chain.link(ts_(sm[:, 3:4], sm[:, 3:4], 1.0 / (SP * SX), None, ALU.mult))
                        dve.wait_ge(b_ready["out"], upto(b, ("out", t)))
                        if t == 0:
                            dve.wait_ge(x2_kept, b * 16 + FREE)
                        row = x2row[:, t, :]
                        stt(out=row, in0=b_bank(("out", t)), scalar=sm[:, 3:4], in1=resid[:, b * TT + t, :], op0=ALU.mult,
                            op1=ALU.add).then_inc(b_drained["out"], 1)
                        wait_apart(b_drained["out"], upto(b, ("out", t)))
                        chain.link(nc.vector.bn_stats(stats[:, t, :], row), wait_apart)
                        nc.vector.bn_aggr(mv[:, t, :], stats[:, t, :]).then_inc(b_var, 1)
                    elif k == "ln":
                        dve.wait_ge(b_rstd, b + 1)
                        refine(chain, 0, TT)
                        for i in range(TT):
                            row = x2row[:, i, :]
                            ts_(row, row, mv[:, i, 0:1], rstd[:, i:i + 1], ALU.subtract, ALU.mult).then_inc(x2_written, 1)
                    elif k == "lr":
                        low_rank(t)
                        if 1 <= t <= 3:
                            low_w(0, 0, t - 1)
                assert chain is None or chain.n == B_STEPS, chain.n

            cross(B_FIRST, None, 0)
            with dve.Fori(0, B - 1) as b:
                cross(B_BODY_DVE, b, b + 1)
            cross(B_LAST, B - 1, B)

            chain = Chain(dve, r_step)
            chain.link(nc.vector.reciprocal(temp[:, 1:2], temp[:, 0:1]))
            dve.wait_ge(r_act, 1)
            tt3 = rt[:, 2]
            dve_tmp = rt[:, 7]
            tt_(dve_tmp, rt[:, 0], rt[:, 1], ALU.add).then_inc(wr_step, 1)
            dve.wait_ge(wr_step, 3)
            chain.link(ts_(tt3, dve_tmp, temp[:, 1:2], None, ALU.mult))
            dve.wait_ge(r_act, 5)
            inh, e1, fb = rt[:, 3], rt[:, 5], rt[:, 6]
            zone, w, msk, cur, eq, pr, pr2 = (rt[:, n] for n in (7, 8, 9, 10, 11, 12, 13))
            wide = [P, NT, E]

            def over(x):
                return x.unsqueeze(2).to_broadcast(wide)

            chain.link(ts_(zone, inh, float(np.float32(GOLDEN_LOWER)), None, ALU.is_ge))
            chain.link(stt(out=zone, in0=inh, scalar=GOLDEN_UPPER, in1=zone, op0=ALU.is_le, op1=ALU.mult))
            chain.link(tt_(w, e1, zone, ALU.mult))
            wsum, mx, none, some, fsum = (rs1[:, n] for n in range(5))
            chain.link(nc.vector.tensor_reduce(wsum, w, AX, ALU.add))
            chain.link(ts_(none, wsum, 1e-8, None, ALU.is_lt))
            chain.link(ts_(some, none, -1.0, 1.0, ALU.mult, ALU.add))
            chain.link(nc.vector.tensor_copy(cur, fb))
            for pick in range(2):
                chain.link(nc.vector.tensor_reduce(mx, cur, AX, ALU.max))
                chain.link(tt_(eq, cur, over(mx), ALU.is_equal))
                chain.link(nc.vector.tensor_copy(pr, eq))
                src, dst = pr, pr2
                for sh in (1, 2, 4):
                    chain.link(tt_(dst[:, :, sh:E], src[:, :, sh:E], src[:, :, 0:E - sh], ALU.add))
                    chain.link(nc.vector.tensor_copy(dst[:, :, 0:sh], src[:, :, 0:sh]))
                    src, dst = dst, src
                chain.link(stt(out=eq, in0=src, scalar=1.0, in1=eq, op0=ALU.is_equal, op1=ALU.mult))
                if pick == 0:
                    chain.link(nc.vector.tensor_copy(msk, eq))
                    chain.link(stt(out=cur, in0=eq, scalar=-2.0, in1=cur, op0=ALU.mult, op1=ALU.add))
                else:
                    chain.link(tt_(msk, msk, eq, ALU.add))
            chain.link(tt_(msk, fb, msk, ALU.mult))
            chain.link(nc.vector.tensor_reduce(fsum, msk, AX, ALU.add))
            chain.link(ts_(fsum, fsum, 1e-8, None, ALU.max))
            chain.link(nc.vector.reciprocal(fsum, fsum))
            chain.link(tt_(msk, msk, over(fsum), ALU.mult))
            chain.link(tt_(msk, msk, over(none), ALU.mult))
            chain.link(tt_(w, w, over(some), ALU.mult))
            chain.link(tt_(w, w, msk, ALU.add))
            chain.link(nc.vector.tensor_reduce(wsum, w, AX, ALU.add))
            chain.link(ts_(wsum, wsum, 1e-8, None, ALU.max))
            chain.link(nc.vector.reciprocal(wsum, wsum))
            chain.link(ts_(wsum, wsum, 1.0 / (SM * SW), None, ALU.mult))
            chain.link(tt_(wt[:, :, :], w, over(wsum), ALU.mult))

            for m in range(3):
                low_w(1, 1, m)

            final = Chain(dve, f_step)

            def moments(c):
                for t in range(TT):
                    wait_c_drained(dve, E - 1, ("d", c, t))
                    final.link(nc.vector.bn_stats(stats[:, t, :], resid[:, c * TT + t, :]))
                    nc.vector.bn_aggr(mv[:, t, :], stats[:, t, :]).then_inc(f_var, 1)

            def final_norm(c):
                dve.wait_ge(f_rstd, c + 1)
                refine(final, 0, TT)
                for t in range(TT):
                    row = resid[:, c * TT + t, :]
                    ts_(row, row, mv[:, t, 0:1], rstd[:, t:t + 1], ALU.subtract, ALU.mult).then_inc(y_ready, 1)

            def expert(e, par, last=False):
                def hidden(c):
                    for f in range(FT):
                        n = c * FT + f
                        u = ("u", c, f)
                        g = C_AT[("g", c, f)]
                        dve.wait_ge(c_drained[g % 8], e * (C_N // 8) + (g // 8 + 1 + FREE))
                        wait_c_filled(dve, e, u)
                        dve.wait_ge(mid_lo, e * (B * FT) + (n - 1 + FREE))
                        stt(out=midf[:, n % 2, :], in0=c_bank(u), scalar=SM / (SX * SW), in1=sil[:, n % 2, :],
                            op0=ALU.mult, op1=ALU.mult).then_inc(c_drained[C_AT[u] % 8], 1)

                def add(c):
                    for t in range(TT):
                        u = ("d", c, t)
                        wait_c_filled(dve, e, u)
                        row = resid[:, c * TT + t, :]
                        stt(out=row, in0=c_bank(u), scalar=wt[:, c * TT + t, bass.ds(e, 1)], in1=row,
                            op0=ALU.mult, op1=ALU.add).then_inc(c_drained[C_AT[u] % 8], 1)

                for c in range(B + 1):
                    if c < B:
                        hidden(c)
                    if last and c >= 2:
                        final_norm(c - 2)
                    if c:
                        add(c - 1)
                    if last and c:
                        moments(c - 1)
                if last:
                    final_norm(B - 1)

            dve.wait_ge(x2_kept, 16 * B + FREE)
            with dve.Fori(0, E // 2 - 1) as pair:
                for par in range(2):
                    expert(pair * 2 + par, par)
                    for m in range(3):
                        low_w((pair * 2 + par) + 2, par, m)
            for par in range(2):
                expert(E - 2 + par, par, par == 1)


FREE = 16
POOL_COLS = 896
A_NORM = TT + 4
TOP_STEPS = 1 + 2 * ((TOPK - 1) // 8)
B_STEPS = 3 * TT + 4
COEF_STEPS = 7


def rotary_tables():
    freqs = np.float32(1.0) / np.float32(10000.0) ** (np.arange(0, ROPE, 2, dtype=np.float32) / np.float32(ROPE))
    emb = np.arange(S, dtype=np.float32)[:, None] * freqs[None, :].astype(np.float32)
    c, s = np.cos(emb), np.sin(emb)
    both = np.stack([np.stack([c, s], -1), np.stack([s, c], -1)])
    return np.ascontiguousarray(both.reshape(2, TT, P, ROPE // 2, 2).transpose(2, 0, 1, 3, 4)).astype(np.float32)


def kernel(**inputs):
    import concourse.bacc as bacc
    from concourse.bass_utils import run_bass_kernel_spmd

    names = {"x": "x", "ctx": "ctx_2048", "Wq": "L0_attn_Wq", "Wkv": "L0_attn_Wkv_down", "Wku": "L0_attn_Wk_up",
             "Wvu": "L0_attn_Wv_up", "W_qkv": "L0_xattn_W_qkv", "W_o": "L0_xattn_W_o", "beta_q": "L0_xattn_beta_q",
             "beta_k": "L0_xattn_beta_k", "gate": "L0_xattn_gate", "log_tau": "L0_xattn_log_tau", "Wg": "L0_ffn_Wg",
             "Wu": "L0_ffn_Wu", "Wd": "L0_ffn_Wd", "Ga": "L0_ffn_Ga", "Gb": "L0_ffn_Gb", "Ua": "L0_ffn_Ua",
             "Ub": "L0_ffn_Ub", "Da": "L0_ffn_Da", "Db": "L0_ffn_Db", "Wr": "L0_ffn_Wr", "temperature": "L0_ffn_temperature"}
    nc = bacc.Bacc("TRN2", target_bir_lowering=False, num_devices=1)
    arrays, aps = {}, {}
    for short, name in names.items():
        v = np.ascontiguousarray(inputs[name])
        if v.size == 1:
            v = v.reshape(1, 1)
        arrays[short] = v
    arrays["cossin"] = rotary_tables()
    for short, v in arrays.items():
        aps[short] = nc.dram_tensor("in_" + short, v.shape, mybir.dt.from_np(v.dtype), kind="ExternalInput").ap()
    y = nc.dram_tensor("y", (N, D), F32, kind="ExternalOutput")
    aps["y"] = y.ap()
    decoder(nc, aps)
    r = run_bass_kernel_spmd(nc, [{"in_" + k: v for k, v in arrays.items()}], core_ids=[0])
    return r.results[0]["y"].reshape(B, S, D)
```

```python
import math
from contextlib import ExitStack

import numpy as np

import concourse.bass as bass
from concourse import mybir
from concourse.alu_op_type import AluOpType as ALU

ACT = mybir.ActivationFunctionType
AX = mybir.AxisListType.X
F32 = mybir.dt.float32
F16 = mybir.dt.float16
BF16 = mybir.dt.bfloat16

P = 128
B, S, D = 4, 512, 512
H, HD, NOPE = 16, 32, 8
ROPE = HD - NOPE
LAT = 128
E, F, R = 8, 512, 64
NL = 2
TOPK = 54
TT = S // P
DT = D // P
FT = F // P
N = B * S
NT = N // P
EPS = 1e-5
NEG = -1.0e30

SX = 16.0
SW = 64.0
SQ = 4.0
SV = 16.0
SP = 1024.0
SM = 64.0
SNM = 64.0

G = 4
TRI = sum((i + 1) * P for i in range(TT))
OFF = {4: 0, 3: 512, 1: 896, 2: 1024}

A_NEXT = ("xT", "c", "row", "rope", "rhi", "rlo", "v", "cat0", "bqn", "maxn", "mTn")
A_KIND = {"mTn": "mT"}
A_PER = {"xT": DT, "c": 1, "row": 2 * TT, "v": TT, "cat0": 2 * TT, "cat1": 2 * TT, "mT": H // G, "pv": H}
A_BANK = {"xT": (6, 7, 6, 7),
          "cat1": (6, 7, 6, 7, 7, 7, 6, 6),
          "row": (6, 7, 7, 7, 6, 7, 6, 7),
          "c": (6,),
          "pv": (7, 7, 7, 7, 6, 6, 7, 6, 6, 6, 7, 7, 7, 7, 7, 7),
          "mT": (None, 6, 7, 7),
          "v": (6, 6, 6, 6),
          "cat0": (6, 7, 6, 6, 7, 7, 7, 6),
          "mTn": (6,)}


def steps(text):
    return [(k, int(i)) for k, i in (word.split(".") for word in text.split())]


A_PE = steps("""
    xT.0 xT.1 bk.0 bq.5 cat1.0 cat1.1 xT.2 xT.3 bk.1 cat1.2 bq.6 cat1.3 row.0 cat1.4 bk.2 cat1.5 c.0 pv.0 bq.7
    cat1.6 row.1 bk.3 cat1.7 row.2 mT.1 bq.8 pv.1 v.0 row.3 bk.4 bq.9 pv.2 row.4 bq.10 v.1 pv.3 bq.11 bk.5 v.2
    row.5 bq.12 row.6 bk.6 mT.2 pv.4 bq.13 row.7 bk.7 cat0.0 bq.14 cat0.1 pv.5 bk.8 cat0.2 pv.6 cat0.3 bk.9
    cat0.4 bq.15 pv.7 cat0.5 bk.10 pv.8 cat0.6 cat0.7 bk.11 mT.3 pv.9 bqn.0 bk.12 pv.10 bqn.1 bk.13 pv.11 bk.14
    pv.12 bqn.2 bk.15 pv.13 bqn.3 v.3 pv.14 mTn.0 bqn.4 pv.15
""")
A_ACT = steps("""
    xT.0 xT.1 exp.0 xT.2 xT.3 exp.1 hi.0 hi.1 row.0 exp.2 c.0 pv.0 hi.2 row.1 rhi.0 exp.3 row.2 rhi.1 pv.1 hi.3
    row.3 v.0 exp.4 rhi.2 hi.4 pv.2 row.4 rhi.3 v.1 ln.0 pv.3 v.2 row.5 exp.5 rhi.4 hi.5 row.6 rhi.5 exp.6 pv.4
    hi.6 row.7 exp.7 rhi.6 pv.5 hi.7 exp.8 pv.6 hi.8 rhi.7 exp.9 pv.7 hi.9 exp.10 pv.8 hi.10 exp.11 hi.11 pv.9
    exp.12 pv.10 hi.12 exp.13 pv.11 hi.13 exp.14 pv.12 hi.14 exp.15 pv.13 hi.15 v.3 pv.14 pv.15
""")
A_DVE = steps("""
    xT.0 xT.1 cat1.0 cat1.1 max.5 xT.2 xT.3 cat1.2 res.0 cat1.3 lo.0 cat1.4 max.6 cat1.5 res.1 c.0 lo.1 cat1.6
    max.7 cat1.7 res.2 mT.1 rlo.0 lo.2 max.8 lo.3 rlo.1 v.0 max.9 rlo.2 res.3 max.10 v.1 lo.4 rlo.3 max.11 v.2
    ln.0 max.12 rlo.4 mT.2 lo.5 max.13 lo.6 cat0.0 rlo.5 cat0.1 max.14 cat0.2 lo.7 comb.0 cat0.3 cat0.4 max.15
    lo.8 rlo.6 cat0.5 rlo.7 lo.9 cat0.6 cat0.7 lo.10 mT.3 maxn.0 lo.11 comb.1 lo.12 maxn.1 comb.2 lo.13 maxn.2
    lo.14 maxn.3 v.3 lo.15 mTn.0 maxn.4 comb.3
""")
A_POOL = steps("""
    lo.0 rope.0 lo.1 rope.1 lo.2 rope.2 rope.3 lo.3 rope.4 lo.4 rope.5 lo.5 rope.6 lo.6 rope.7 lo.7 lo.8 lo.9
    lo.10 lo.11 lo.12 lo.13 lo.14 lo.15
""")


def next_part(seq, kinds):
    return [u for u in seq if u[0] in kinds]


def own_part(seq, kinds):
    return [u for u in seq if u[0] not in kinds]


A_FIN = [("res", t) for t in range(TT)] + [("ln", 0)]


def _four(kind, *ts):
    return [(kind, t) for t in ts or range(4)]


B_BODY_PE = steps("""
    aT.0 aT.1 cT.0 cT.1 xT.0 cT.2 cT.3 out.0 xT.1 A.0 A.1 A.2 A.3 aT.2 out.1 aT.3 out.2 out.3 sc.0 xT.2 sc.1
    xT.3 CW.0 sc.2 CW.1 x2.0 x2.1 x2.2 CW.2 sc.3 CW.3 x2.3
""")
B_BODY_ACT = steps("""
    aT.0 cT.0 cT.1 cT.2 cT.3 A.0 top.2 aT.1 A.1 xT.0 top.3 A.2 aT.2 aT.3 xT.1 A.3 ln.0 sc.0 sc.1 xT.2 xT.3 x2.0
    x2.1 first.0 CW.0 sc.2 CW.1 first.1 x2.2 CW.2 CW.3 x2.3 sc.3
""")
B_BODY_DVE = steps("""
    aT.0 top.2 aT.1 norm.0 aT.2 norm.1 aT.3 xT.0 norm.2 norm.3 xT.1 ln.0 xT.2 xT.3 first.0 x2.0 x2.1 x2.2 x2.3
""")
B_BODY_POOL = steps("""
    cT.0 cT.1 cT.2 cT.3 A.0 A.1 A.2 A.3 CW.0 CW.1 CW.2 CW.3
""")
B_FIRST = [(k, t) for k in ("cT", "A", "wo") for t in range(4)]
B_FIRST += [("xT", 0), ("xT", 1), ("sc", 0), ("xT", 2), ("sc", 1), ("xT", 3), ("sc", 2), ("sc", 3), ("first", 0), ("first", 1)]
B_FIRST += [("CW", t) for t in range(4)]
B_LAST = steps("""
    aT.0 aT.1 lt.0 out.0 out.1 top.2 top.3 lt.1 lr.0 norm.0 aT.2 aT.3 norm.1 out.2 out.3 lt.2 norm.2 norm.3 ln.0
    lr.1 x2.0 x2.1 x2.2 x2.3 lr.2
""")
B_BANK = {"aT": (3, 0, 2, 3),
          "cT": (7, 1, 2, 4),
          "out": (3, 0, 2, 3),
          "xT": (6, 7, 4, 7),
          "A": (4, 5, 2, 1),
          "sc": (2, 1, 7, 6),
          "CW": (1, 4, 5, 4),
          "x2": (3, 0, 2, 1),
          "wo": (0, 3, 6, 7)}
COPIED = {"cT": (0, 1, 0, 1), "A": (2, 3, 2, 3), "CW": (0, 1, 0, 1)}
B_NEXT = ("wo", "cT", "A", "CW", "xT", "sc")


def bank_before(bank, seq, n, earlier):
    at = lambda u: bank[u[0]][u[1]] if u[0] in bank else None
    for m in range(n - 1, -1, -1):
        if at(seq[m]) == at(seq[n]):
            return seq[m], False
    for u in reversed(earlier):
        if at(u) == at(seq[n]):
            return u, True
    return None, False


C_SEQ = []
for _c in range(B + 1):
    if _c < B:
        C_SEQ += [(x, _c, f) for f in range(FT) for x in ("g", "u")]
    if _c:
        C_SEQ += [("d", _c - 1, t) for t in range(TT)]
C_AT = {u: n for n, u in enumerate(C_SEQ)}
C_N = len(C_SEQ)
assert C_N % 8 == 0
ORDER = [0] + list(range(NL, E)) + [1]
assert NL == 2
C_FOLD = []
for _c in range(B + 1):
    _fold = 1 <= _c <= 3
    C_FOLD += [("lt", _c - 1)] if _fold else []
    C_FOLD += [u for u in C_SEQ if u[0] in "gu" and u[1] == _c]
    C_FOLD += [("lp", _c - 1, t) for t in range(TT)] if _fold else []
    C_FOLD += [u for u in C_SEQ if u[0] == "d" and u[1] == _c - 1]
C_LAST = {E - 2: {u: (E - 2) * C_N + n for n, u in enumerate(C_FOLD)},
          E - 1: {u: (E - 2) * C_N + len(C_FOLD) + n for n, u in enumerate(C_SEQ)}}

GOLDEN_CENTER = 1.0 / math.e
GOLDEN_LOWER = 0.5 - math.log(4.0 / 3.0)
GOLDEN_UPPER = 0.5


class Chain:

    def __init__(self, eng, sem, base=0):
        self.eng, self.sem, self.base, self.n = eng, sem, base, 0

    def link(self, ins, wait=None):
        self.n += 1
        ins.then_inc(self.sem, 1)
        (wait or self.eng.wait_ge)(self.sem, self.base + self.n)

    def step(self, ins):
        self.n += 1
        ins.then_inc(self.sem, 1)

    def passed(self, wait=None):
        (wait or self.eng.wait_ge)(self.sem, self.base + self.n)


def decoder(nc, a):
    ctx = ExitStack()

    def sem(name):
        return ctx.enter_context(nc.semaphore(name))

    def sb(stack, name, shape, dt=F32):
        return stack.enter_context(nc.sbuf_tensor(name, shape, dt))

    with ctx:
        banks = ctx.enter_context(nc.psum_tensor("banks", [P, 8, 512], F32))
        max_ps = banks[:, 0:3, :].rearrange("p b n -> p (b n)")
        st_ps = banks[:, 3:6, :].rearrange("p b n -> p (b n)")
        resid = sb(ctx, "resid", [P, NT, D])
        identf = sb(ctx, "identf", [P, P])
        ident16 = sb(ctx, "ident16", [P, P], F16)
        identb = sb(ctx, "identb", [P, P], BF16)
        eps = sb(ctx, "eps", [P, 1])
        negc = sb(ctx, "negc", [P, 1])
        stats = sb(ctx, "stats", [P, TT, 6])
        mv = sb(ctx, "mv", [P, TT, 2])
        lnv = sb(ctx, "lnv", [P, TT])
        rstd = sb(ctx, "rstd", [P, TT])
        nwt = sb(ctx, "nwt", [P, TT])
        coef = sb(ctx, "coef", [P, 8])
        wr_raw = sb(ctx, "wr_raw", [P, DT, E])
        wr16 = sb(ctx, "wr16", [P, DT, 2 * E], F16)
        temp = sb(ctx, "temp", [P, 2])

        sa = ctx.enter_context(ExitStack())
        x_in = sb(sa, "x_in", [P, TT, D])
        xT = sb(sa, "xT", [P, 2, DT, S], F16)
        cT = sb(sa, "cT", [P, 2, S], F16)
        wq = sb(sa, "wq", [P, 2, DT, D], F16)
        wkvd = sb(sa, "wkvd", [P, 2, DT, LAT], F16)
        wku = sb(sa, "wku", [P, 2, D], F16)
        wvu = sb(sa, "wvu", [P, 2, D], F16)
        rows = sb(sa, "rows", [P, 4, H, HD])
        turn_a = sb(sa, "turn_a", [P, H, ROPE // 2, 2])
        turn_b = sb(sa, "turn_b", [P, H, ROPE // 2, 2])
        cossin = sb(sa, "cossin", [P, 2, TT, ROPE // 2, 2])
        cat = sb(sa, "cat", [P, 2 * TT, H, 3, HD], F16)
        vnext = sb(sa, "vnext", [P, H, TT, 66], F16)
        nm16 = sb(sa, "nm16", [P, TT, P], F16)
        qcT = sb(sa, "qcT", [P, H, S], F16)
        kcT = sb(sa, "kcT", [P, H, S], F16)
        vcat = sb(sa, "vcat", [P, H, TT, 66], F16)
        pf = sb(sa, "pf", [P, 2, TRI])
        phi = sb(sa, "phi", [P, 2, TRI], F16)
        plo = sb(sa, "plo", [P, 2, TRI], F16)
        osb = sb(sa, "osb", [P, 2, G, TT, 65])
        nmf = sb(sa, "nmf", [P, TT, G])
        mask_qk = sb(sa, "mask_qk", [P, P], BF16)
        mask_kq = sb(sa, "mask_kq", [P, P], BF16)
        rsum = sb(sa, "rsum", [P, G, TT])
        x_res = sb(sa, "x_res", [P, TT, D])
        att = sb(sa, "att", [P, TT, D])
        raw_wq = pf[:, :, :].rearrange("p a n -> p (a n)")[:, 0:DT * D].rearrange("p (t n) -> p t n", t=DT)
        raw_osb = osb[:, :, :, :, :].rearrange("p a h t n -> p (a h t n)")
        raw_kvd = raw_osb[:, 0:DT * LAT].rearrange("p (t n) -> p t n", t=DT)
        raw_ku = raw_osb[:, 512:1024]
        raw_vu = raw_osb[:, 1024:1536]
        sa.close()

        copyf = sb(ctx, "copyf", [P, 4, 512])
        fold = copyf[:, 0:2, :]
        ca = ctx.enter_context(ExitStack())
        c_raw = sb(ca, "c_raw", [P, 4, D])
        cxT = sb(ca, "cxT", [P, 2, DT, 512], F16)
        wqw = sb(ca, "wqw", [P, 2, 4, D], F16)
        woT = sb(ca, "woT", [P, 2, DT, D], F16)
        kq = sb(ca, "kq", [P, 2, DT, 512], F16)
        cw = sb(ca, "cw", [P, 2, 4, D], F16)
        tsc = sb(ca, "tsc", [P, 4, 512])
        x2row = sb(ca, "x2row", [P, TT, D])
        raw_q, raw_o = x2row, tsc
        x1row = sb(ca, "x1row", [P, TT, D])
        la_raw = [x1row[:, 0, n * 256:(n + 1) * 256].rearrange("p (t r) -> p t r", r=R) for n in range(2)]
        lb_raw = [x1row[0:R, 1 + n, :] for n in range(2)]
        la_copy, lb_copy = copyf[0:R, 2, :], copyf[0:R, 3, :]
        wk = sb(ca, "wk", [P, 2, 2, 512])
        top8 = sb(ca, "top8", [P, 2, 7, 8])
        small = sb(ca, "small", [P, TT, 4])
        ex = sb(ca, "ex", [P, 2, 512])
        attf = sb(ca, "attf", [P, TT, 512])
        attT = sb(ca, "attT", [P, 2, 2, 4, P], F16)
        x1T = sb(ca, "x1T", [P, 2, 2, DT, P], F16)
        laT = [x1T[0:R, n].rearrange("p h d n -> p (h d n)").rearrange("p (h n) -> p h n", h=2) for n in range(2)]
        ca.close()

        w16 = sb(ctx, "w16", [P, 2, 3, 2, 4, 512], F16)
        mid16 = sb(ctx, "mid16", [P, 2, 2, FT, 512], F16)
        sil = sb(ctx, "sil", [P, 2, 512])
        midf = sb(ctx, "midf", [P, 2, 512])
        rt = sb(ctx, "rt", [P, 14, NT, E])
        rs1 = sb(ctx, "rs1", [P, 8, NT])
        wt = sb(ctx, "wt", [P, NT, E])
        rest = sb(ctx, "rest", [P, 5248])
        la_last = [copyf[:, 0, n * 256:(n + 1) * 256].rearrange("p (t r) -> p t r", r=R) for n in range(2)]
        lb_last = [copyf[0:R, 1 + n, :] for n in range(2)]

        x2T = sb(ctx, "x2T", [P, 2, DT, N], F16)
        stage = sb(ctx, "stage", [P, 3, 4, 512])
        lb16 = [sb(ctx, f"lb16_{n}", [R, 2, 512], F16) for n in range(2)]

        w_loaded = [sem(f"w_loaded{n}") for n in range(4)]
        cossin_loaded = sem("cossin_loaded")
        consts = sem("consts")
        own_rows = sem("own_rows")
        w_hi = sem("w_hi")
        w_lo = sem("w_lo")
        x_loaded = sem("x_loaded")
        res_loaded = sem("res_loaded")
        a_ready = {k: sem(f"a_{k}_ready") for k in A_PER}
        a_hi = {k: sem(f"a_{k}_hi") for k in ("xT", "c", "v")}
        a_drained = {k: sem(f"a_{k}_drained") for k in A_PER}
        v_moved = [sem(f"v_moved{k}") for k in range(2)]
        comb_done = sem("comb_done")
        roped = sem("roped")
        cat_hi = sem("cat_hi")
        cat_lo = sem("cat_lo")
        max_ready = sem("max_ready")
        max_done = sem("max_done")
        nm_ready = sem("nm_ready")
        st_ready = sem("st_ready")
        exp_done = sem("exp_done")
        p_hi = sem("p_hi")
        p_lo_pool = sem("p_lo_pool")
        p_lo_dve = sem("p_lo_dve")
        norm_step = sem("norm_step")
        res_read = sem("res_read")
        comb_step = sem("comb_step")
        passed = sem("passed")
        var_ready = sem("var_ready")
        ln_done = sem("ln_done")
        rstd_ready = sem("rstd_ready")
        x1_written = sem("x1_written")
        bq_loaded = sem("bq_loaded")
        bo_loaded = sem("bo_loaded")
        s_loaded = sem("s_loaded")
        coef_step = sem("coef_step")
        coef_act = sem("coef_act")
        ctx_loaded = sem("ctx_loaded")
        bw_hi = sem("bw_hi")
        bw_lo = sem("bw_lo")
        b_ready = {k: sem(f"b_{k}_ready") for k in B_BANK}
        b_hi = {k: sem(f"b_{k}_hi") for k in B_BANK}
        b_low = {k: sem(f"b_{k}_low") for k in COPIED}
        b_drained = {k: sem(f"b_{k}_drained") for k in B_BANK}
        top_step = [sem(f"top_step{j}") for j in range(2)]
        neg_ready = sem("neg_ready")
        ex_ready = sem("ex_ready")
        att_ready = sem("att_ready")
        b_step = sem("b_step")
        b_var = sem("b_var")
        b_ln = sem("b_ln")
        b_rstd = sem("b_rstd")
        x2_written = sem("x2_written")
        x1_fetched = sem("x1_fetched")
        x2_kept = sem("x2_kept")
        stage_loaded = [sem(f"stage{m}_loaded") for m in range(3)]
        lora_loaded = [sem(f"lora{n}_loaded") for n in range(2)]
        la_copied = sem("la_copied")
        lb_copied = sem("lb_copied")
        la_turned = sem("la_turned")
        lora_hi = sem("lora_hi")
        lora_lo = sem("lora_lo")
        lora_mm = sem("lora_mm")
        lora_out = sem("lora_out")
        lora_added = sem("lora_added")
        e_hi = sem("e_hi")
        e_lo = sem("e_lo")
        wr_step = sem("wr_step")
        logits_ready = sem("logits_ready")
        r_act = sem("r_act")
        r_step = sem("r_step")
        c_ready = sem("c_ready")
        c_drained = [sem(f"c_bank{k}_drained") for k in range(8)]
        mid_hi = sem("mid_hi")
        mid_lo = sem("mid_lo")
        f_step = sem("f_step")
        f_var = sem("f_var")
        f_ln = sem("f_ln")
        f_rstd = sem("f_rstd")
        y_ready = sem("y_ready")
        y_stored = sem("y_stored")

        def a_bank(u):
            return banks[:, A_BANK[u[0]][u[1]], :]

        def a_count(b, u):
            return b * A_PER[A_KIND.get(u[0], u[0])] + (u[1] + 1)

        def a_upto(b, u):
            return b * A_PER[A_KIND.get(u[0], u[0])] + (u[1] + 1 + FREE)

        def b_bank(u):
            return banks[:, B_BANK[u[0]][u[1]], :]

        def count(b, u):
            return b * 4 + (u[1] + 1)

        def upto(b, u):
            return b * 4 + (u[1] + 1 + FREE)

        def c_place(e, u, more=0):
            if type(e) is int:
                n = C_LAST[e][u] if e in C_LAST else e * C_N + C_AT[u]
                return n % 8, n // 8 + more, n + more
            n = C_AT[u]
            return n % 8, e * (C_N // 8) + (n // 8 + more), e * C_N + (n + more)

        def c_bank(e, u):
            return banks[:, c_place(e, u)[0], :]

        def c_read(e, u):
            return c_drained[c_place(e, u)[0]]

        def wait_c_filled(eng, e, u):
            eng.wait_ge(c_ready, c_place(e, u, 1)[2])

        def wait_c_free(eng, e, u):
            bank, fills, _ = c_place(e, u, FREE)
            eng.wait_ge(c_drained[bank], fills)

        def wait_c_drained(eng, e, u):
            bank, fills, _ = c_place(e, u, 1 + FREE)
            eng.wait_ge(c_drained[bank], fills)

        K3 = 3 * HD
        LORA = [("Ga", "Gb"), ("Ua", "Ub"), ("Da", "Db")]
        WN = ["Wg", "Wu", "Wd"]

        block = ctx.enter_context(nc.Block())

        @block.sync
        def _(sp):
            def load_x(dst, b, done):
                sp.dma_start(dst[:, :, :], a["x"][b].rearrange("(t p) d -> p t d", p=P)).then_inc(done, 16)

            load_x(x_in, 0, x_loaded)
            sp.dma_start(raw_wq, a["Wq"].rearrange("(t p) n -> p t n", p=P)).then_inc(w_loaded[0], 16)
            sp.dma_start(raw_kvd, a["Wkv"].rearrange("(t p) n -> p t n", p=P)).then_inc(w_loaded[1], 16)
            sp.dma_start(raw_ku, a["Wku"]).then_inc(w_loaded[2], 16)
            sp.dma_start(raw_vu, a["Wvu"]).then_inc(w_loaded[3], 16)
            sp.dma_start(cossin[:, :, :, :, :], a["cossin"]).then_inc(cossin_loaded, 16)
            sp.dma_start(wr_raw[:, :, :], a["Wr"].rearrange("(t p) e -> p t e", p=P)).then_inc(s_loaded, 16)
            for n, name in enumerate(("gate", "beta_q", "beta_k", "log_tau")):
                sp.dma_start(coef[:, n:n + 1], a[name].partition_broadcast(P)).then_inc(s_loaded, 16)
            sp.dma_start(temp[:, 0:1], a["temperature"].partition_broadcast(P)).then_inc(s_loaded, 16)


            def move_values(b, half):
                heads = slice(half * 8, half * 8 + 8)
                sp.wait_ge(a_ready["pv"], a_upto(b - 1, ("pv", half * 8 + 7)))
                sp.dma_start(vcat[:, heads], vnext[:, heads]).then_inc(v_moved[half], 16)

            with sp.Fori(0, B - 1) as b:
                sp.wait_ge(a_ready["xT"], a_upto(b, ("xT", DT - 1)))
                load_x(x_in, b + 1, x_loaded)
                sp.wait_ge(a_drained["v"], a_upto(b, ("v", TT - 1)))
                move_values(b, 0)
                move_values(b, 1)
                sp.wait_ge(res_read, b * TT + FREE)
                load_x(x_res, b, res_loaded)
            sp.wait_ge(a_drained["v"], a_upto(B - 1, ("v", TT - 1)))
            move_values(B - 1, 0)
            move_values(B - 1, 1)

            def load_x1(b):
                sp.dma_start(x1row[:, :, :], resid[:, bass.ds(b * TT, TT), :]).then_inc(x1_fetched, 16)

            def load_context(b):
                sp.dma_start(c_raw[:, :, :], a["ctx"][b].rearrange("(t p) d -> p t d", p=P)).then_inc(ctx_loaded, 16)

            sp.wait_ge(a_ready["cat1"], a_upto(B - 1, ("cat1", 2 * TT - 1)))
            for half in range(2):
                sp.wait_ge(v_moved[half], B * 16 + FREE)
            sp.dma_start(raw_q[:, :, :], a["W_qkv"][0:D].rearrange("(t p) n -> p t n", p=P)).then_inc(bq_loaded, 16)
            load_context(0)
            sp.dma_start(raw_o[:, :, :], a["W_o"].rearrange("(t p) n -> p t n", p=P)).then_inc(bo_loaded, 16)
            sp.wait_ge(res_read, (B - 1) * TT + FREE)
            load_x(x_res, B - 1, res_loaded)
            sp.wait_ge(st_ready, B * H + FREE)
            load_x1(0)
            sp.wait_ge(x1_written, NT)
            for m in range(3):
                sp.dma_start(stage[:, m], a[WN[m]][0].rearrange("(t p) n -> p t n", p=P)).then_inc(stage_loaded[m], 16)
            with sp.Fori(0, B - 1) as b:
                sp.wait_ge(b_ready["cT"], upto(b, ("cT", 3)))
                load_context(b + 1)
                sp.wait_ge(b_ready["xT"], upto(b, ("xT", 3)))
                load_x1(b + 1)

            sp.wait_ge(b_ready["xT"], upto(B - 1, ("xT", 3)))
            def load_factors(n, la_to, lb_to):
                la, lb = (a[name][n // 3] for name in LORA[n % 3])
                sp.dma_start(la_to, la.rearrange("(t p) r -> p t r", p=P)).then_inc(lora_loaded[n % 2], 16)
                sp.dma_start(lb_to, lb).then_inc(lora_loaded[n % 2], 16)

            def load_weights(m, expert):
                sp.dma_start(stage[:, m], a[WN[m]][expert].rearrange("(t p) n -> p t n", p=P)).then_inc(stage_loaded[m], 16)

            for n in range(3):
                if n == 2:
                    sp.wait_ge(la_turned, n - 1)
                    sp.wait_ge(lb_copied, n - 1)
                load_factors(n, la_raw[n % 2], lb_raw[n % 2])
            for m in range(3):
                sp.wait_ge(e_lo, m + 1)
                load_weights(m, ORDER[1])
            with sp.Fori(1, E - 2) as e:
                for m in range(3):
                    sp.wait_ge(e_lo, e * 3 + (m + 1))
                    load_weights(m, e + 2)
            for m in range(3):
                sp.wait_ge(e_lo, (E - 2) * 3 + (m + 1))
                load_weights(m, ORDER[E - 1])
            for n in range(3, 6):
                if n == 5:
                    sp.wait_ge(lora_lo, 2 * (n - 1))
                load_factors(n, la_last[n % 2], lb_last[n % 2])
            y = a["y"].rearrange("(c t p) d -> c p t d", p=P, t=TT)
            for c in range(B - 1):
                sp.wait_ge(y_ready, c * TT + TT)
                sp.dma_start(y[c], resid[:, c * TT:(c + 1) * TT, :]).then_inc(y_stored, 16)
            for t in range(TT):
                sp.wait_ge(y_ready, (B - 1) * TT + (t + 1))
                sp.dma_start(y[B - 1, :, t], resid[:, (B - 1) * TT + t, :]).then_inc(y_stored, 16)
            sp.wait_ge(y_stored, 16 * (B - 1 + TT))

        @block.gpsimd
        def _(pool):
            for s in [max_done, st_ready, exp_done, p_lo_pool, p_lo_dve, roped, cat_lo, nm_ready, v_moved[0], v_moved[1], comb_done, res_read,
                      att_ready, x2_kept, mid_lo] + c_drained + \
                    [d[k] for d in (a_ready, a_drained) for k in A_PER] + [d[k] for d in (b_ready, b_drained) for k in B_BANK] + \
                    [b_low[k] for k in COPIED]:
                pool.sem_inc(s, FREE)
            for t in (identf, ident16, identb):
                pool.memset(t[:, :], 0.0).then_inc(consts, 1)
            pool.memset(mask_qk[:, :], 0.0).then_inc(consts, 1)
            pool.memset(mask_kq[:, :], 0.0).then_inc(consts, 1)
            pool.memset(eps[:, :], EPS).then_inc(consts, 1)
            pool.memset(negc[:, :], -GOLDEN_CENTER).then_inc(consts, 1)
            pool.memset(nm16[:, :, :], 0.0).then_inc(consts, 1)
            pool.memset(vnext[:, :, :, 64:66], 1.0).then_inc(consts, 1)
            pool.wait_ge(consts, 9)
            for t in (identf, ident16, identb):
                pool.affine_select(out=t[:, :], in_=t[:, :], compare_op=ALU.not_equal, fill=1.0, base=0,
                                   pattern=[[-1, P]], channel_multiplier=1).then_inc(consts, 1)
            pool.affine_select(out=mask_qk[:, :], in_=mask_qk[:, :], compare_op=ALU.is_ge, fill=NEG, base=0,
                               pattern=[[-1, P]], channel_multiplier=1).then_inc(consts, 1)
            pool.affine_select(out=mask_kq[:, :], in_=mask_kq[:, :], compare_op=ALU.is_ge, fill=NEG, base=0,
                               pattern=[[1, P]], channel_multiplier=-1).then_inc(consts, 1)
            own_row = kcT[K3:K3 + G, :, :].rearrange("p (g j) n -> p g j n", j=G)
            pool.wait_ge(consts, 14)
            pool.memset(kcT[K3:K3 + G, :, :], 0.0).then_inc(own_rows, 1)
            pool.wait_ge(own_rows, 1)
            pool.affine_select(out=own_row, in_=own_row, compare_op=ALU.not_equal, fill=SNM, base=0,
                               pattern=[[0, H // G], [-1, G], [0, S]], channel_multiplier=1).then_inc(own_rows, 1)

            pool.wait_ge(own_rows, 2)
            pool.wait_ge(cossin_loaded, 16)

            def heads(seq, b, nxt):
                for k, i in seq:
                    if k == "rope":
                        n, t = nxt * (2 * TT) + i, i // 2
                        pool.wait_ge(a_drained["row"], a_upto(nxt, ("row", i)))
                        pool.wait_ge(roped, n * 4 + FREE)
                        pair = rows[:, i % 4, :, NOPE:HD].rearrange("p h (i two) -> p h i two", two=2)
                        for j, dst in ((0, turn_a), (1, turn_b)):
                            cs = cossin[:, j, t].unsqueeze(1).to_broadcast([P, H, ROPE // 2, 2])
                            nc.gpsimd.tensor_tensor(dst[:, :, :, :], pair, cs, ALU.mult).then_inc(roped, 1)
                        pool.wait_ge(roped, n * 4 + (2 + FREE))
                        half = NOPE + ROPE // 2
                        nc.gpsimd.tensor_tensor(rows[:, i % 4, :, NOPE:half], turn_a[:, :, :, 0], turn_a[:, :, :, 1],
                                                ALU.subtract).then_inc(roped, 1)
                        nc.gpsimd.tensor_tensor(rows[:, i % 4, :, half:HD], turn_b[:, :, :, 1], turn_b[:, :, :, 0],
                                                ALU.add).then_inc(roped, 1)
                    elif k == "lo":
                        pool.wait_ge(p_hi, b * H + (i + 1))
                        nc.gpsimd.tensor_tensor(plo[:, i % 2, 0:POOL_COLS], pf[:, i % 2, 0:POOL_COLS],
                                                phi[:, i % 2, 0:POOL_COLS], ALU.subtract).then_inc(p_lo_pool, 1)

            heads(next_part(A_POOL, A_NEXT), None, 0)
            with pool.Fori(0, B - 1) as b:
                heads(A_POOL, b, b + 1)
            heads(own_part(A_POOL, A_NEXT), B - 1, None)

            def cross(seq, nxt):
                for k, t in seq:
                    dst = {"cT": cxT, "A": kq, "CW": cw}[k]
                    pool.wait_ge(b_hi[k], count(nxt, (k, t)))
                    nc.gpsimd.tensor_tensor(dst[:, 1, t, :], copyf[:, COPIED[k][t], :], dst[:, 0, t, :], ALU.subtract)\
                        .then_inc(b_low[k], 1)

            cross([u for u in B_FIRST if u[0] in COPIED], 0)
            with pool.Fori(0, B - 1) as b:
                cross(B_BODY_POOL, b + 1)

            def factor_lows(n):
                for k, (dst, src) in enumerate(((lb16[n % 2], lb_copy), (laT[n % 2], la_copy))):
                    pool.wait_ge(lora_hi, 2 * n + k + 1)
                    nc.gpsimd.tensor_tensor(dst[:, 1, :], src, dst[:, 0, :], ALU.subtract).then_inc(lora_lo, 1)

            factor_lows(0)
            for n in range(3):
                if n < 2:
                    factor_lows(n + 1)
                m = n
                pool.wait_ge(stage_loaded[m], 16)
                for t in range(TT):
                    i = n * TT + t
                    pool.wait_ge(lora_out, i + 1)
                    nc.gpsimd.tensor_tensor(stage[:, m, t, :], stage[:, m, t, :], fold[:, i % 2, :], ALU.add).then_inc(lora_added, 1)

            with pool.Fori(0, E) as e:
                for n in range(B * FT):
                    pool.wait_ge(mid_hi, e * (B * FT) + (n + 1))
                    c, f = n // FT, n % FT
                    nc.gpsimd.tensor_tensor(mid16[:, c % 2, 1, f, :], midf[:, n % 2, :], mid16[:, c % 2, 0, f, :],
                                            ALU.subtract).then_inc(mid_lo, 1)

        @block.tensor
        def _(pe):
            def three(out, l, r, n, done=None):
                for i in range(n):
                    for j, (x, y) in enumerate(((0, 0), (0, 1), (1, 0))):
                        mm = nc.tensor.matmul(out, l(x, i), r(y, i), start=(i == 0 and j == 0),
                                              stop=(i == n - 1 and j == 2))
                if done is not None:
                    mm.then_inc(done, 1)
                return mm

            pe.wait_ge(consts, 14)
            def heads(seq, b, nxt, earlier):
                for n, (k, i) in enumerate(seq):
                    u = (k, i)
                    own = nxt if k in A_NEXT else b
                    if k in A_BANK:
                        bank, done = a_bank(u), a_ready[A_KIND.get(k, k)]
                        v, before = bank_before(A_BANK, seq, n, earlier)
                        if v is not None:
                            of = nxt if v[0] in A_NEXT else b
                            pe.wait_ge(a_drained[A_KIND.get(v[0], v[0])], a_upto(of - 1 if before else of, v))
                    if k == "xT":
                        if i == 0:
                            pe.wait_ge(x_loaded, own * 16 + 16)
                        for t in range(TT):
                            mm = nc.tensor.transpose(bank[:, t * P:(t + 1) * P], x_in[:, t, i * P:(i + 1) * P], identf[:, :])
                        mm.then_inc(done, 1)
                    elif k == "c":
                        pe.wait_ge(w_lo, 2)
                        pe.wait_ge(a_drained["xT"], a_upto(own, ("xT", DT - 1)))
                        three(bank, lambda x, j: wkvd[:, x, j, :], lambda y, j: xT[:, y, j, :], DT, done)
                    elif k == "row":
                        ts = slice(i // 2 * P, (i // 2 + 1) * P)
                        if i == 0:
                            pe.wait_ge(w_lo, 1)
                            pe.wait_ge(a_drained["xT"], a_upto(own, ("xT", DT - 1)))
                        if i % 2 == 0:
                            three(bank, lambda x, j: xT[:, x, j, ts], lambda y, j: wq[:, y, j, :], DT, done)
                        else:
                            if i == 1:
                                pe.wait_ge(w_lo, 4)
                                pe.wait_ge(a_drained["c"], a_upto(own, ("c", 0)))
                            three(bank, lambda x, j: cT[:, x, ts], lambda y, j: wku[:, y, :], 1, done)
                    elif k == "v":
                        if i == 0:
                            pe.wait_ge(a_drained["c"], a_upto(own, ("c", 0)))
                        three(bank, lambda x, j: cT[:, x, i * P:(i + 1) * P], lambda y, j: wvu[:, y, :], 1, done)
                    elif k in ("cat0", "cat1"):
                        pe.wait_ge(cat_lo, own * (2 * TT) + (i + 1 + FREE))
                        out = bank.bitcast(F16)
                        for j in range(8):
                            src = cat[:, i, (k == "cat1") * 8 + j].rearrange("p a n -> p (a n)")
                            mm = nc.tensor.transpose(out[0:K3, j * P:(j + 1) * P], src, ident16[:, :])
                        mm.then_inc(done, 1)
                    elif k in ("bq", "bqn"):
                        pe.wait_ge(max_done, (own * H + i) * 4 + FREE)
                        if k == "bqn" and i == 0:
                            pe.wait_ge(a_drained["cat0"], a_upto(own, ("cat0", 2 * TT - 1)))
                        if k == "bq" and i == 8:
                            pe.wait_ge(a_drained["cat1"], a_upto(own, ("cat1", 2 * TT - 1)))
                        for t in range(TT):
                            w = (t + 1) * P
                            o = OFF[t + 1]
                            nc.tensor.matmul(max_ps[:, o:o + w], qcT[0:K3, i, t * P:(t + 1) * P], kcT[0:K3, i, 0:w],
                                             start=True, stop=False)
                            mm = nc.tensor.matmul(max_ps[:, o + w - P:o + w], identb[:, :], mask_qk[:, :],
                                                  start=False, stop=True)
                        mm.then_inc(max_ready, 1)
                    elif k in ("mT", "mTn"):
                        pe.wait_ge(nm_ready, own * (H // G) + (i + 1 + FREE))
                        out = bank.bitcast(F16)
                        for t in range(TT):
                            mm = nc.tensor.transpose(out[:, t * P:(t + 1) * P], nm16[:, t, :], ident16[:, :])
                        mm.then_inc(done, 1)
                    elif k == "bk":
                        if i == 0:
                            pe.wait_ge(own_rows, 2)
                        if i % G == 0:
                            pe.wait_ge(a_drained["mT"], a_upto(own, ("mT", i // G)))
                        pe.wait_ge(exp_done, own * H + (i + FREE))
                        for t in range(TT):
                            w = S - t * P
                            o = OFF[TT - t]
                            nc.tensor.matmul(st_ps[:, o:o + w], kcT[0:K3 + G, i, t * P:(t + 1) * P],
                                             qcT[0:K3 + G, i, t * P:S], start=True, stop=False)
                            mm = nc.tensor.matmul(st_ps[:, o:o + P], identb[:, :], mask_kq[:, :], start=False, stop=True)
                        mm.then_inc(st_ready, 1)
                    elif k == "pv":
                        pe.wait_ge(p_lo_pool, own * H + (i + 1 + FREE))
                        pe.wait_ge(p_lo_dve, own * H + (i + 1 + FREE))
                        if i % 8 == 0:
                            pe.wait_ge(v_moved[i // 8], own * 16 + (16 + FREE))
                        for q in range(TT):
                            out = bank[:, q * 65:(q + 1) * 65]
                            for t in range(q + 1):
                                o = OFF[TT - t] + (q - t) * P
                                for x, w in enumerate((phi, plo)):
                                    mm = nc.tensor.matmul(out, w[:, i % 2, o:o + P], vcat[:, i, t, 0:65],
                                                          start=(t == 0 and x == 0), stop=(t == q and x == 1))
                        mm.then_inc(done, 1)

            heads(next_part(A_PE, A_NEXT), None, 0, [])
            for k in ("xT", "c", "row", "v", "cat0"):
                pe.wait_ge(a_drained[k], a_upto(0, (k, A_PER[k] - 1)))
            pe.wait_ge(a_drained["mT"], a_upto(0, ("mT", 0)))
            with pe.Fori(0, B - 1) as b:
                heads(A_PE, b, b + 1, A_PE)
            heads(own_part(A_PE, A_NEXT), B - 1, B, A_PE)

            pe.wait_ge(max_done, B * H * 4 + FREE)
            pe.wait_ge(exp_done, B * H + FREE)
            for k in ("cat1", "mT", "pv"):
                pe.wait_ge(a_drained[k], a_upto(B - 1, (k, A_PER[k] - 1)))

            def turn_factor(n):
                pe.wait_ge(lora_loaded[n % 2], 32 * (n // 2 + 1))
                if n:
                    pe.wait_ge(la_copied, n)
                for t in range(4):
                    mm = nc.tensor.transpose(banks[0:R, 4, t * P:(t + 1) * P], la_raw[n % 2][:, t, :], identf[:, :])
                mm.then_inc(la_turned, 1)

            def low_rank(n):
                pe.wait_ge(lora_lo, 2 * (n + 1))
                for t in range(4):
                    ts = slice(t * P, (t + 1) * P)
                    if 4 * n + t >= 3:
                        pe.wait_ge(lora_out, 4 * n + t - 2)
                    three(banks[:, 5 + (4 * n + t) % 3, :], lambda x, i: laT[n % 2][:, x, ts], lambda y, i: lb16[n % 2][:, y, :],
                          1, lora_mm)

            def cross(seq, b, nxt, earlier):
                for n, (k, t) in enumerate(seq):
                    u = (k, t)
                    own = nxt if k in B_NEXT else b
                    if k in B_BANK:
                        v, before = bank_before(B_BANK, seq, n, earlier)
                        if v is not None:
                            of = nxt if v[0] in B_NEXT else b
                            pe.wait_ge(b_drained[v[0]], upto(of - 1 if before else of, v))
                        bank = b_bank(u)
                    if k == "cT":
                        if t == 0:
                            pe.wait_ge(ctx_loaded, own * 16 + 16)
                        for i in range(4):
                            mm = nc.tensor.transpose(bank[:, i * P:(i + 1) * P], c_raw[:, i, t * P:(t + 1) * P], identf[:, :])
                        mm.then_inc(b_ready[k], 1)
                    elif k == "wo":
                        if t == 0:
                            pe.wait_ge(bo_loaded, 16)
                        for i in range(4):
                            mm = nc.tensor.transpose(bank[:, i * P:(i + 1) * P], raw_o[:, i, t * P:(t + 1) * P], identf[:, :])
                        mm.then_inc(b_ready[k], 1)
                    elif k == "A":
                        if t == 0:
                            pe.wait_ge(bw_lo, 1)
                            pe.wait_ge(b_low["cT"], upto(own, ("cT", 3)))
                        three(bank, lambda x, i: wqw[:, x, i, t * P:(t + 1) * P], lambda y, i: cxT[:, y, i, :], 4, b_ready[k])
                    elif k == "CW":
                        if t == 0:
                            pe.wait_ge(b_low["cT"], upto(own, ("cT", 3)))
                        three(bank, lambda x, i: cxT[:, x, i, t * P:(t + 1) * P], lambda y, i: woT[:, y, i, :], 4, b_ready[k])
                    elif k in ("xT", "aT", "x2"):
                        if k == "xT" and t == 0:
                            pe.wait_ge(x1_fetched, own * 16 + 16)
                        if k == "aT":
                            pe.wait_ge(att_ready, upto(own, u))
                        if k == "x2":
                            pe.wait_ge(x2_written, count(own, u))
                        src = {"xT": x1row[:, t, :], "aT": attf[:, t, :], "x2": x2row[:, t, :]}[k]
                        for i in range(4):
                            mm = nc.tensor.transpose(bank[:, i * P:(i + 1) * P], src[:, i * P:(i + 1) * P], identf[:, :])
                        mm.then_inc(b_ready[k], 1)
                    elif k == "sc":
                        pe.wait_ge(b_drained["xT"], upto(own, ("xT", t)))
                        if t == 0:
                            pe.wait_ge(b_low["A"], upto(own, ("A", 3)))
                        three(bank, lambda x, i: x1T[:, t % 2, x, i, :], lambda y, i: kq[:, y, i, :], DT, b_ready[k])
                    elif k == "out":
                        pe.wait_ge(b_drained["aT"], upto(own, ("aT", t)))
                        if t == 0:
                            pe.wait_ge(b_low["CW"], upto(own, ("CW", 3)))
                        three(bank, lambda x, i: attT[:, t % 2, x, i, :], lambda y, i: cw[:, y, i, :], 4, b_ready[k])
                    elif k == "lt":
                        turn_factor(t)
                    elif k == "lr":
                        low_rank(t)

            cross(B_FIRST, None, 0, [])
            for k in ("wo", "A", "CW", "xT", "sc"):
                pe.wait_ge(b_drained[k], upto(0, (k, 3)))
            with pe.Fori(0, B - 1) as b:
                cross(B_BODY_PE, b, b + 1, B_BODY_PE)
            for k in ("CW", "sc"):
                pe.wait_ge(b_drained[k], upto(B - 1, (k, 3)))
            cross(B_LAST, B - 1, B, B_BODY_PE)

            for k in ("aT", "out", "x2"):
                pe.wait_ge(b_drained[k], upto(B - 1, (k, 3)))
            pe.wait_ge(wr_step, 2)
            for t in range(NT):
                ts = slice(t * P, (t + 1) * P)
                out = banks[:, 0, t * 16:(t + 1) * 16]
                for i in range(DT):
                    for x in range(2):
                        mm = nc.tensor.matmul(out, x2T[:, x, i, ts], wr16[:, i, :], start=(i == 0 and x == 0),
                                              stop=(i == DT - 1 and x == 1))
            mm.then_inc(logits_ready, 1)

            pe.wait_ge(lora_out, 12)
            pe.wait_ge(r_act, 1)

            def expert(e, par):
                def ffn_in(c):
                    cs = slice(c * 512, (c + 1) * 512)
                    for f in range(FT):
                        for m, name in enumerate("gu"):
                            u = (name, c, f)
                            wait_c_free(pe, e, u)
                            if c == 0 and f == 0:
                                pe.wait_ge(e_lo, e * 3 + (m + 1))
                            three(c_bank(e, u), lambda x, i: w16[:, par, m, x, i, f * P:(f + 1) * P],
                                  lambda y, i: x2T[:, y, i, cs], DT, c_ready)

                def ffn_out(c):
                    pe.wait_ge(mid_lo, e * (B * FT) + (FT * (c + 1) + FREE))
                    if c == 0:
                        pe.wait_ge(e_lo, e * 3 + 3)
                    for t in range(TT):
                        u = ("d", c, t)
                        wait_c_free(pe, e, u)
                        three(c_bank(e, u), lambda x, i: mid16[:, c % 2, x, i, t * P:(t + 1) * P],
                              lambda y, i: w16[:, par, 2, y, i, :], FT, c_ready)

                def turn_factor(m):
                    n, u = 3 + m, ("lt", m)
                    wait_c_free(pe, e, u)
                    pe.wait_ge(lora_loaded[n % 2], 32 * (n // 2 + 1))
                    for t in range(4):
                        mm = nc.tensor.transpose(c_bank(e, u)[0:R, t * P:(t + 1) * P], la_last[n % 2][:, t, :], identf[:, :])
                    mm.then_inc(c_ready, 1)

                def low_rank(m):
                    pe.wait_ge(lora_lo, 2 * (3 + m + 1))
                    for t in range(4):
                        u = ("lp", m, t)
                        wait_c_free(pe, e, u)
                        three(c_bank(e, u), lambda x, i: lb16[0][:, x, t * P:(t + 1) * P], lambda y, i: lb16[1][:, y, :], 1, c_ready)

                for c in range(B + 1):
                    fold = type(e) is int and e == E - 2 and 1 <= c <= 3
                    if fold:
                        turn_factor(c - 1)
                    if c < B:
                        ffn_in(c)
                    if fold:
                        low_rank(c - 1)
                    if c:
                        ffn_out(c - 1)

            with pe.Fori(0, E // 2 - 1) as pair:
                for par in range(2):
                    expert(pair * 2 + par, par)
            for par in range(2):
                expert(E - 2 + par, par)

        @block.scalar
        def _(act):
            def scaled(out, in_, scale):
                return nc.scalar.activation(out, in_, ACT.Copy, scale=scale)

            act.wait_ge(consts, 14)

            def heads(seq, b, nxt):
                for k, i in seq:
                    u = (k, i)
                    own = nxt if k in A_NEXT else b
                    was = None if b is None else b - 1
                    if k in ("xT", "c", "row", "v", "pv"):
                        act.wait_ge(a_ready[k], a_upto(own, u))
                    if k == "xT":
                        if i == 0:
                            act.wait_ge(a_ready["row"], a_upto(own - 1, ("row", 2 * TT - 2)))
                        scaled(xT[:, 0, i, :], a_bank(u), SX).then_inc(a_hi[k], 1)
                    elif k == "c":
                        act.wait_ge(a_ready["v"], a_upto(own - 1, ("v", TT - 1)))
                        scaled(cT[:, 0, :], a_bank(u), 1.0 / SW).then_inc(a_hi[k], 1)
                    elif k == "row":
                        act.wait_ge(cat_lo, own * (2 * TT) + (i - 3 + FREE))
                        scaled(rows[:, i % 4], a_bank(u).rearrange("p (h n) -> p h n", h=H), SQ / (SX * SW))\
                            .then_inc(a_drained[k], 1)
                    elif k == "v":
                        if i == 0:
                            act.wait_ge(v_moved[0], own * 16 + FREE)
                            act.wait_ge(v_moved[1], own * 16 + FREE)
                        scaled(vnext[:, :, i, 0:HD], a_bank(u).rearrange("p (h n) -> p h n", h=H), SV / (SX * SW))\
                            .then_inc(a_hi[k], 1)
                    elif k == "rhi":
                        act.wait_ge(roped, own * (8 * TT) + (4 * (i + 1) + FREE))
                        act.wait_ge(a_ready["cat1"], a_upto(own - 1, ("cat1", i)))
                        dst = cat[:, i, :, 0:2] if i % 2 == 0 else cat[:, i, :, 0:3:2]
                        scaled(dst, rows[:, i % 4].unsqueeze(2).to_broadcast([P, H, 2, HD]), 1.0).then_inc(cat_hi, 1)
                    elif k == "exp":
                        g = own * H + i
                        act.wait_ge(st_ready, g + (1 + FREE))
                        act.wait_ge(p_lo_pool, g + (FREE - 1))
                        act.wait_ge(p_lo_dve, g + (FREE - 1))
                        nc.scalar.activation(pf[:, i % 2, :], st_ps[:, 0:TRI], ACT.Exp,
                                             scale=1.0 / (SQ * SQ * math.sqrt(HD))).then_inc(exp_done, 1)
                    elif k == "hi":
                        g = own * H + i
                        act.wait_ge(exp_done, g + (1 + FREE))
                        act.wait_ge(a_ready["pv"], g + (FREE - 1))
                        scaled(phi[:, i % 2, :], pf[:, i % 2, :], 1.0).then_inc(p_hi, 1)
                    elif k == "pv":
                        if i % G == 0:
                            act.wait_ge(comb_done, own * (H // G) + (i // G - 1 + FREE))
                        scaled(osb[:, i // G % 2, i % G], a_bank(u)[:, 0:TT * 65].rearrange("p (t n) -> p t n", t=TT), 1.0)\
                            .then_inc(a_drained[k], 1)
                    elif k == "ln":
                        act.wait_ge(var_ready, was * TT + TT)
                        nc.scalar.activation(lnv[:, :], mv[:, :, 1], ACT.Ln, bias=eps[:, 0:1]).then_inc(ln_done, 1)
                        act.wait_ge(ln_done, was + 1)
                        nc.scalar.activation(rstd[:, :], lnv[:, :], ACT.Exp, scale=-0.5).then_inc(rstd_ready, 1)

            heads(next_part(A_ACT, A_NEXT)[:DT], None, 0)
            for n, (w, raw) in enumerate(((wq, raw_wq), (wkvd, raw_kvd), (wku, raw_ku), (wvu, raw_vu))):
                act.wait_ge(w_loaded[n], 16)
                scaled(w[:, 0], raw, SW).then_inc(w_hi, 1)
            act.wait_ge(w_lo, 4)
            heads(next_part(A_ACT, A_NEXT)[DT:], None, 0)
            heads(own_part(A_ACT, ("res", "ln")), 0, 1)
            with act.Fori(1, B - 1) as b:
                heads(A_ACT, b, b + 1)
            last = own_part(A_ACT, A_NEXT)
            at = last.index(("hi", 13))
            heads(last[:at], B - 1, None)
            act.wait_ge(bq_loaded, 16)
            scaled(wqw[:, 0], raw_q[:, :, :], SW).then_inc(bw_hi, 1)
            heads(last[at:], B - 1, None)

            act.wait_ge(s_loaded, 96)
            nc.scalar.activation(coef[:, 4:5], coef[:, 0:1], ACT.Exp, scale=-1.0).then_inc(coef_act, 1)
            nc.scalar.activation(coef[:, 5:6], coef[:, 3:4], ACT.Exp).then_inc(coef_act, 1)
            scaled(wr16[:, :, 0:E], wr_raw[:, :, :], SW).then_inc(wr_step, 1)

            def factor_halves(n):
                act.wait_ge(lora_loaded[n % 2], 32 * (n // 2 + 1))
                if n:
                    act.wait_ge(lora_lo, 2 * n)
                if n >= 2:
                    act.wait_ge(lora_mm, 4 * (n - 1))
                scaled(lb_copy, lb_raw[n % 2], SW).then_inc(lb_copied, 1)
                act.wait_ge(la_turned, n + 1)
                scaled(la_copy, banks[0:R, 4, :], SW).then_inc(la_copied, 1)
                act.wait_ge(lb_copied, n + 1)
                scaled(lb16[n % 2][:, 0, :], lb_copy, 1.0).then_inc(lora_hi, 1)
                act.wait_ge(la_copied, n + 1)
                scaled(laT[n % 2][:, 0, :], la_copy, 1.0).then_inc(lora_hi, 1)

            def low_rank(n):
                for t in range(4):
                    i = 4 * n + t
                    act.wait_ge(lora_mm, i + 1)
                    if i >= 2:
                        act.wait_ge(lora_added, i - 1)
                    scaled(fold[:, i % 2, :], banks[:, 5 + i % 3, :], 1.0 / (SW * SW)).then_inc(lora_out, 1)
                act.wait_ge(lora_added, 4 * (n + 1))
                scaled(w16[:, 0, n, 0], stage[:, n], SW).then_inc(e_hi, 1)

            def cross(seq, b, nxt):
                for k, t in seq:
                    u = (k, t)
                    own = nxt if k in B_NEXT else b
                    if k in COPIED:
                        dst, scale = {"cT": (cxT[:, 0, t, :], SX), "A": (kq[:, 0, t, :], 1.0 / SW), "CW": (cw[:, 0, t, :], 1.0 / SW)}[k]
                        copy = copyf[:, COPIED[k][t], :]
                        before = {"cT": (own - 1, ("CW", t + 2)), "A": (own - 1, ("A", t + 2)), "CW": (own, ("cT", t + 2))}[k] \
                            if t < 2 else (own, (k, t - 2))
                        act.wait_ge(b_low[before[1][0]], upto(*before))
                        act.wait_ge(b_ready[k], upto(own, u))
                        scaled(copy, b_bank(u), scale).then_inc(b_drained[k], 1)
                        if t == 0:
                            if k == "CW":
                                act.wait_ge(b_ready["out"], upto(own - 1, ("out", 3)))
                            if k == "A":
                                act.wait_ge(b_ready["sc"], upto(own - 1, ("sc", 3)))
                            if k == "cT":
                                act.wait_ge(b_ready["CW"], upto(own - 1, ("CW", 3)))
                        act.wait_ge(b_drained[k], upto(own, u))
                        scaled(dst, copy, 1.0).then_inc(b_hi[k], 1)
                    elif k in ("xT", "aT", "x2", "wo"):
                        act.wait_ge(b_ready[k], upto(own, u))
                        if k == "aT":
                            act.wait_ge(b_ready["out"], upto(own, u) - 2)
                        if k == "xT":
                            act.wait_ge(b_ready["sc"], upto(own, u) - 2)
                        if u == ("wo", 0):
                            act.wait_ge(bw_lo, 1)
                        dst = {"wo": lambda: woT[:, 0, t].rearrange("p (i n) -> p i n", n=P), "xT": lambda: x1T[:, t % 2, 0], "aT": lambda: attT[:, t % 2, 0],
                               "x2": lambda: x2T[:, 0, :, bass.ds(own * S + t * P, P)]}[k]()
                        src = b_bank(u).rearrange("p (t n) -> p t n", n=P)
                        scale = {"wo": SW, "xT": SX, "aT": SP, "x2": SX}[k]
                        scaled(dst, src, scale).then_inc(b_hi[k], 1)
                        if u == ("x2", 3):
                            act.dma_start(resid[:, bass.ds(own * TT, TT), :], x2row[:, :, :]).then_inc(x2_kept, 16)
                    elif k == "sc":
                        act.wait_ge(b_ready[k], upto(own, u))
                        act.wait_ge(att_ready, upto(own - 1, u))
                        act.wait_ge(b_drained["wo"], upto(0, ("wo", 3)))
                        nc.scalar.activation(tsc[:, t, :], b_bank(u), ACT.Copy, scale=coef[:, 7:8]).then_inc(b_drained[k], 1)
                    elif k in ("top", "first"):
                        g = (b if k == "top" else nxt) * TT + t
                        act.wait_ge(neg_ready, g + 1)
                        act.wait_ge(att_ready, g - 1 + FREE)
                        nc.scalar.activation(ex[:, t % 2, :], tsc[:, t, :], ACT.Exp, bias=small[:, t, 0:1]).then_inc(ex_ready, 1)
                    elif k == "ln":
                        act.wait_ge(b_var, b * TT + TT)
                        nc.scalar.activation(lnv[:, :], mv[:, :, 1], ACT.Ln, bias=eps[:, 0:1]).then_inc(b_ln, 1)
                        act.wait_ge(b_ln, b + 1)
                        nc.scalar.activation(rstd[:, :], lnv[:, :], ACT.Exp, scale=-0.5).then_inc(b_rstd, 1)
                    elif k == "lt":
                        factor_halves(t)
                    elif k == "lr":
                        low_rank(t)

            cross(B_FIRST[:4], None, 0)
            heads(A_FIN, B, None)
            act.wait_ge(coef_step, COEF_STEPS)
            cross(B_FIRST[4:], None, 0)
            with act.Fori(0, B - 1) as b:
                cross(B_BODY_ACT, b, b + 1)
            act.wait_ge(b_low["CW"], upto(B - 1, ("CW", 3)))
            cross(B_LAST, B - 1, B)

            act.wait_ge(x2_written, NT)
            act.wait_ge(logits_ready, 1)
            scaled(rt[:, 0:2].rearrange("p a t e -> p t a e"), banks[:, 0, 0:NT * 16].rearrange("p (t a e) -> p t a e", t=NT, a=2),
                   1.0 / (SX * SW)).then_inc(r_act, 1)
            act.wait_ge(r_step, 2)
            nc.scalar.activation(rt[:, 3], rt[:, 2], ACT.Sigmoid).then_inc(r_act, 1)
            act.wait_ge(r_act, 2)
            nc.scalar.activation(rt[:, 4], rt[:, 3], ACT.Abs, bias=negc[:, 0:1]).then_inc(r_act, 1)
            act.wait_ge(r_act, 3)
            nc.scalar.activation(rt[:, 5], rt[:, 4], ACT.Exp, scale=-1.0 / 0.1).then_inc(r_act, 1)
            nc.scalar.activation(rt[:, 6], rt[:, 4], ACT.Exp, scale=-1.0 / 0.3).then_inc(r_act, 1)

            for m in range(3):
                act.wait_ge(b_ready["out"], upto(B - 1, ("out", 3)))
                act.wait_ge(stage_loaded[m], 32)
                scaled(w16[:, 1, m, 0], stage[:, m], SW).then_inc(e_hi, 1)

            def final_norm(c):
                act.wait_ge(f_var, (c + 1) * TT)
                nc.scalar.activation(lnv[:, :], mv[:, :, 1], ACT.Ln, bias=eps[:, 0:1]).then_inc(f_ln, 1)
                act.wait_ge(f_ln, c + 1)
                nc.scalar.activation(rstd[:, :], lnv[:, :], ACT.Exp, scale=-0.5).then_inc(f_rstd, 1)

            def high_w(e, par, m):
                wait_c_filled(act, e - 2, ("d", B - 1, TT - 1))
                act.wait_ge(stage_loaded[m], e * 16 + 16)
                scaled(w16[:, par, m, 0], stage[:, m], SW).then_inc(e_hi, 1)

            def factor_halves(m):
                n, u = 3 + m, ("lt", m)
                act.wait_ge(lora_loaded[n % 2], 32 * (n // 2 + 1))
                if m:
                    wait_c_filled(act, E - 2, ("lp", m - 1, TT - 1))
                scaled(lb16[1][:, 0, :], lb_last[n % 2], SW).then_inc(lora_hi, 1)
                wait_c_filled(act, E - 2, u)
                scaled(lb16[0][:, 0, :], c_bank(E - 2, u)[0:R, :], SW).then_inc(lora_hi, 1)

            def expert(e, par, last=False):
                for c in range(B):
                    fold = type(e) is int and e == E - 2 and c >= 1
                    if fold:
                        factor_halves(c - 1)
                        if c >= 2:
                            high_fold(c - 2)
                    for f in range(FT):
                        if last and c >= 2 and f == FT // 2:
                            final_norm(c - 2)
                        n = c * FT + f
                        u = ("g", c, f)
                        wait_c_filled(act, e, u)
                        nc.scalar.activation(sil[:, n % 2, :], c_bank(e, u), ACT.Silu, scale=1.0 / (SX * SW))\
                            .then_inc(c_read(e, u), 1)
                        wait_c_drained(act, e, ("u", c, f))
                        scaled(mid16[:, c % 2, 0, f, :], midf[:, n % 2, :], 1.0).then_inc(mid_hi, 1)
                if type(e) is int and e == E - 2:
                    high_fold(2)

            def high_fold(m):
                for t in range(TT):
                    wait_c_drained(act, E - 2, ("lp", m, t))
                high_w(E - 1, 1, m)

            with act.Fori(0, E // 2 - 2) as pair:
                for par in range(2):
                    expert(pair * 2 + par, par)
                    for m in range(3):
                        high_w(pair * 2 + (par + 2), par, m)
            expert(E - 4, 0)
            for m in range(3):
                high_w(E - 2, 0, m)
            expert(E - 3, 1)
            expert(E - 2, 0)
            expert(E - 1, 1, True)
            for c in (B - 2, B - 1):
                final_norm(c)

        @block.vector
        def _(dve):
            ts_, tt_, stt = nc.vector.tensor_scalar, nc.vector.tensor_tensor, nc.vector.scalar_tensor_tensor

            def low(out, src, hi, scale):
                return stt(out=out, in0=src, scalar=scale, in1=hi, op0=ALU.mult, op1=ALU.subtract)

            dve.wait_ge(consts, 14)

            def wait_apart(signal, value):
                dve.wait_ge(signal, value)
                dve.sem_inc(passed, 1)

            def refine(chain, n0, n1):
                y, t, v = rstd[:, n0:n1], nwt[:, n0:n1], mv[:, n0:n1, 1]
                chain.link(tt_(t, y, y, ALU.mult))
                chain.link(stt(out=t, in0=v, scalar=EPS, in1=t, op0=ALU.add, op1=ALU.mult))
                chain.link(ts_(t, t, -0.5, 1.5, ALU.mult, ALU.add))
                chain.link(tt_(y, y, t, ALU.mult))

            def heads(seq, b, nxt):
                for k, i in seq:
                    u = (k, i)
                    own = nxt if k in A_NEXT else b
                    if k in ("xT", "c", "v"):
                        dve.wait_ge(a_hi[k], a_count(own, u))
                        if k == "xT":
                            ins = low(xT[:, 1, i, :], a_bank(u), xT[:, 0, i, :], SX)
                        elif k == "c":
                            ins = low(cT[:, 1, :], a_bank(u), cT[:, 0, :], 1.0 / SW)
                        else:
                            ins = low(vnext[:, :, i, HD:2 * HD], a_bank(u).rearrange("p (h n) -> p h n", h=H),
                                      vnext[:, :, i, 0:HD], SV / (SX * SW))
                        ins.then_inc(a_drained[k], 1)
                    elif k == "rlo":
                        dve.wait_ge(cat_hi, own * (2 * TT) + (i + 1))
                        dst = cat[:, i, :, 2] if i % 2 == 0 else cat[:, i, :, 1]
                        tt_(dst, rows[:, i % 4], cat[:, i, :, 0], ALU.subtract).then_inc(cat_lo, 1)
                    elif k in ("cat0", "cat1"):
                        half = int(k == "cat1")
                        dve.wait_ge(a_ready[k], a_upto(own, u))
                        if i == 0:
                            dve.wait_ge(st_ready, (own - 1) * H + (8 * half + 8 + FREE))
                        nc.vector.tensor_copy((qcT, kcT)[i % 2][0:K3, half * 8:half * 8 + 8, i // 2 * P:(i // 2 + 1) * P],
                                              a_bank(u).bitcast(F16)[0:K3, :].rearrange("p (h n) -> p h n", h=8))\
                            .then_inc(a_drained[k], 1)
                    elif k in ("max", "maxn"):
                        g = own * H + i
                        if i % G == 0:
                            dve.wait_ge(nm_ready, own * (H // G) + (i // G + FREE))
                        dve.wait_ge(max_ready, g + 1)
                        for t in (3, 2, 0, 1):
                            o, w = OFF[t + 1], (t + 1) * P
                            nc.vector.tensor_reduce(nmf[:, t, i % G:i % G + 1], max_ps[:, o:o + w], AX, ALU.max, negate=True)\
                                .then_inc(max_done, 1)
                        if i % G == G - 1:
                            dve.wait_ge(max_done, g * 4 + (4 + FREE))
                            dve.wait_ge(a_ready["mT"], own * (H // G) + (i // G + FREE))
                            ts_(nm16[:, :, K3:K3 + G], nmf[:, :, :], 1.0 / SNM, None, ALU.mult).then_inc(nm_ready, 1)
                    elif k in ("mT", "mTn"):
                        dve.wait_ge(a_ready["mT"], a_upto(own, u))
                        dve.wait_ge(st_ready, (own - 1) * H + (i * G + G + FREE))
                        src = a_bank(u).bitcast(F16)[K3:K3 + G, 0:S]
                        nc.vector.tensor_copy(qcT[K3:K3 + G, i * G:(i + 1) * G, :], src.unsqueeze(1).to_broadcast([G, G, S]))\
                            .then_inc(a_drained["mT"], 1)
                    elif k == "lo":
                        dve.wait_ge(p_hi, own * H + (i + 1))
                        tt_(plo[:, i % 2, POOL_COLS:TRI], pf[:, i % 2, POOL_COLS:TRI], phi[:, i % 2, POOL_COLS:TRI],
                            ALU.subtract).then_inc(p_lo_dve, 1)
                    elif k == "comb":
                        chain = Chain(dve, comb_step, own * (2 * H // G) + 2 * i)
                        dve.wait_ge(comb_done, own * (H // G) + (i + FREE))
                        dve.wait_ge(a_drained["pv"], a_upto(own, ("pv", i * G + G - 1)))
                        src = osb[:, i % 2]
                        o4 = att[:, :, i * P:(i + 1) * P].rearrange("p t (h n) -> p h t n", h=G)
                        chain.link(nc.vector.reciprocal(rsum[:, :, :], src[:, :, :, 64]))
                        chain.link(tt_(o4, src[:, :, :, 0:HD], src[:, :, :, HD:2 * HD], ALU.add))
                        tt_(o4, o4, rsum[:, :, :].unsqueeze(3).to_broadcast([P, G, TT, HD]), ALU.mult).then_inc(comb_done, 1)
                    elif k == "res":
                        was = b - 1
                        chain = Chain(dve, norm_step, was * A_NORM + i)
                        dve.wait_ge(comb_done, b * (H // G) + FREE)
                        dve.wait_ge(res_loaded, was * 16 + 16)
                        row = resid[:, was * TT + i, :]
                        stt(out=row, in0=att[:, i, :], scalar=1.0 / SV, in1=x_res[:, i, :], op0=ALU.mult, op1=ALU.add)\
                            .then_inc(res_read, 1)
                        wait_apart(res_read, was * TT + (i + 1 + FREE))
                        chain.link(nc.vector.bn_stats(stats[:, i, :], row), wait_apart)
                        nc.vector.bn_aggr(mv[:, i, :], stats[:, i, :]).then_inc(var_ready, 1)
                    elif k == "ln":
                        was = b - 1
                        chain = Chain(dve, norm_step, was * A_NORM + TT)
                        dve.wait_ge(rstd_ready, was + 1)
                        refine(chain, 0, TT)
                        for t in range(TT):
                            row = resid[:, was * TT + t, :]
                            ts_(row, row, mv[:, t, 0:1], rstd[:, t:t + 1], ALU.subtract, ALU.mult).then_inc(x1_written, 1)
                        assert chain.n == A_NORM - TT, chain.n

            heads(next_part(A_DVE, A_NEXT)[:DT], None, 0)
            for n, (w, raw) in enumerate(((wq, raw_wq), (wkvd, raw_kvd), (wku, raw_ku), (wvu, raw_vu))):
                dve.wait_ge(w_hi, n + 1)
                if len(raw.shape) == 3:
                    low(w[:, 1].rearrange("p t n -> p (t n)"), raw.rearrange("p t n -> p (t n)"),
                        w[:, 0].rearrange("p t n -> p (t n)"), SW).then_inc(w_lo, 1)
                else:
                    low(w[:, 1], raw, w[:, 0], SW).then_inc(w_lo, 1)
            heads(next_part(A_DVE, A_NEXT)[DT:], None, 0)
            heads(own_part(A_DVE, ("res", "ln")), 0, 1)
            with dve.Fori(1, B - 1) as b:
                heads(A_DVE, b, b + 1)
            last = own_part(A_DVE, A_NEXT)
            at = last.index(("lo", 14))
            heads(last[:at], B - 1, None)
            dve.wait_ge(bw_hi, 1)
            low(wqw[:, 1].rearrange("p t n -> p (t n)"), raw_q[:, :, :].rearrange("p t n -> p (t n)"),
                wqw[:, 0].rearrange("p t n -> p (t n)"), SW).then_inc(bw_lo, 1)
            heads(last[at:], B - 1, None)
            heads(A_FIN, B, None)

            chain = Chain(dve, coef_step)
            dve.wait_ge(coef_act, 2)
            chain.link(ts_(coef[:, 4:5], coef[:, 4:5], 1.0, None, ALU.add))
            chain.link(nc.vector.reciprocal(coef[:, 4:5], coef[:, 4:5]))
            chain.link(ts_(coef[:, 6:7], coef[:, 4:5], -1.0, 1.0, ALU.mult, ALU.add))
            chain.link(tt_(coef[:, 6:7], coef[:, 6:7], coef[:, 2:3], ALU.mult))
            chain.link(stt(out=coef[:, 6:7], in0=coef[:, 4:5], scalar=coef[:, 1:2], in1=coef[:, 6:7], op0=ALU.mult, op1=ALU.add))
            chain.link(ts_(coef[:, 6:7], coef[:, 6:7], D ** -0.5, 1.0 / (SX * SX), ALU.mult, ALU.mult))
            chain.link(tt_(coef[:, 7:8], coef[:, 6:7], coef[:, 5:6], ALU.mult))
            assert chain.n == COEF_STEPS
            dve.wait_ge(wr_step, 1)
            low(wr16[:, :, E:2 * E], wr_raw[:, :, :], wr16[:, :, 0:E], SW).then_inc(wr_step, 1)
            def low_w(e, par, m):
                dve.wait_ge(e_hi, e * 3 + (m + 1))
                low(w16[:, par, m, 1].rearrange("p t n -> p (t n)"), stage[:, m].rearrange("p t n -> p (t n)"),
                    w16[:, par, m, 0].rearrange("p t n -> p (t n)"), SW).then_inc(e_lo, 1)

            def top_k(t0, b):
                first = b * (TT // 2) + t0 // 2
                steps_of = [Chain(dve, top_step[j], first * TOP_STEPS) for j in range(2)]
                srcs = [tsc[:, t0 + j, :] for j in range(2)]
                for j in range(2):
                    t = t0 + j
                    dve.wait_ge(b_drained["sc"], upto(b, ("sc", t)))
                    wait_apart(att_ready, b * TT + (t0 + FREE))
                    steps_of[j].step(nc.vector.max(top8[:, j, 0, :], srcs[j]))
                for j in range(2):
                    steps_of[j].passed()
                    ts_(small[:, t0 + j, 0:1], top8[:, j, 0, 0:1], -1.0, None, ALU.mult).then_inc(neg_ready, 1)
                for r in range((TOPK - 1) // 8):
                    for j in range(2):
                        steps_of[j].passed(wait_apart)
                        steps_of[j].step(nc.vector.match_replace(wk[:, j, r % 2, :], top8[:, j, r, :], srcs[j], -3.0e38))
                        srcs[j] = wk[:, j, r % 2, :]
                    for j in range(2):
                        steps_of[j].passed(wait_apart)
                        steps_of[j].step(nc.vector.max(top8[:, j, r + 1, :], srcs[j]))
                dve.wait_ge(b_ready["aT"], upto(b - 1, ("aT", t0 + 1)))
                for j in range(2):
                    t = t0 + j
                    steps_of[j].passed()
                    dve.wait_ge(ex_ready, b * TT + (t + 1))
                    kth = top8[:, j, (TOPK - 1) // 8, (TOPK - 1) % 8:(TOPK - 1) % 8 + 1]
                    stt(out=attf[:, t, :], in0=tsc[:, t, :], scalar=kth, in1=ex[:, t % 2, :], op0=ALU.is_ge,
                        op1=ALU.mult, accum_out=small[:, t, 2:3]).then_inc(att_ready, 1)

            def cross(seq, b, nxt):
                chain = None if b is None else Chain(dve, b_step, b * B_STEPS)
                for k, t in seq:
                    u = (k, t)
                    own = nxt if k in B_NEXT else b
                    if k in ("xT", "aT", "x2", "wo"):
                        dve.wait_ge(b_hi[k], count(own, u))
                        dst = {"wo": lambda h: woT[:, h, t].rearrange("p (i n) -> p i n", n=P), "xT": lambda h: x1T[:, t % 2, h], "aT": lambda h: attT[:, t % 2, h],
                               "x2": lambda h: x2T[:, h, :, bass.ds(own * S + t * P, P)]}[k]
                        src = b_bank(u).rearrange("p (t n) -> p t n", n=P)
                        scale = {"wo": SW, "xT": SX, "aT": SP, "x2": SX}[k]
                        low(dst(1), src, dst(0), scale).then_inc(b_drained[k], 1)
                    elif k in ("top", "first"):
                        if t % 2 == 0:
                            top_k(t, b if k == "top" else nxt)
                    elif k == "norm":
                        sm = small[:, t]
                        dve.wait_ge(att_ready, upto(b, u))
                        chain.link(nc.vector.reciprocal(sm[:, 3:4], sm[:, 2:3]))
                        chain.link(ts_(sm[:, 3:4], sm[:, 3:4], 1.0 / (SP * SX), None, ALU.mult))
                        dve.wait_ge(b_ready["out"], upto(b, ("out", t)))
                        if t == 0:
                            dve.wait_ge(x2_kept, b * 16 + FREE)
                        row = x2row[:, t, :]
                        stt(out=row, in0=b_bank(("out", t)), scalar=sm[:, 3:4], in1=resid[:, b * TT + t, :], op0=ALU.mult,
                            op1=ALU.add).then_inc(b_drained["out"], 1)
                        wait_apart(b_drained["out"], upto(b, ("out", t)))
                        chain.link(nc.vector.bn_stats(stats[:, t, :], row), wait_apart)
                        nc.vector.bn_aggr(mv[:, t, :], stats[:, t, :]).then_inc(b_var, 1)
                    elif k == "ln":
                        dve.wait_ge(b_rstd, b + 1)
                        refine(chain, 0, TT)
                        for i in range(TT):
                            row = x2row[:, i, :]
                            ts_(row, row, mv[:, i, 0:1], rstd[:, i:i + 1], ALU.subtract, ALU.mult).then_inc(x2_written, 1)
                    elif k == "lr":
                        if t < 3:
                            low_w(0, 0, t)
                assert chain is None or chain.n == B_STEPS, chain.n

            cross(B_FIRST, None, 0)
            with dve.Fori(0, B - 1) as b:
                cross(B_BODY_DVE, b, b + 1)
            cross(B_LAST, B - 1, B)

            chain = Chain(dve, r_step)
            chain.link(nc.vector.reciprocal(temp[:, 1:2], temp[:, 0:1]))
            dve.wait_ge(r_act, 1)
            tt3 = rt[:, 2]
            dve_tmp = rt[:, 7]
            tt_(dve_tmp, rt[:, 0], rt[:, 1], ALU.add).then_inc(wr_step, 1)
            dve.wait_ge(wr_step, 3)
            chain.link(ts_(tt3, dve_tmp, temp[:, 1:2], None, ALU.mult))
            dve.wait_ge(r_act, 5)
            inh, e1, fb = rt[:, 3], rt[:, 5], rt[:, 6]
            zone, w, msk, cur, eq, pr, pr2 = (rt[:, n] for n in (7, 8, 9, 10, 11, 12, 13))
            wide = [P, NT, E]

            def over(x):
                return x.unsqueeze(2).to_broadcast(wide)

            chain.link(ts_(zone, inh, float(np.float32(GOLDEN_LOWER)), None, ALU.is_ge))
            chain.link(stt(out=zone, in0=inh, scalar=GOLDEN_UPPER, in1=zone, op0=ALU.is_le, op1=ALU.mult))
            chain.link(tt_(w, e1, zone, ALU.mult))
            wsum, mx, none, some, fsum = (rs1[:, n] for n in range(5))
            chain.link(nc.vector.tensor_reduce(wsum, w, AX, ALU.add))
            chain.link(ts_(none, wsum, 1e-8, None, ALU.is_lt))
            chain.link(ts_(some, none, -1.0, 1.0, ALU.mult, ALU.add))
            chain.link(nc.vector.tensor_copy(cur, fb))
            for pick in range(2):
                chain.link(nc.vector.tensor_reduce(mx, cur, AX, ALU.max))
                chain.link(tt_(eq, cur, over(mx), ALU.is_equal))
                chain.link(nc.vector.tensor_copy(pr, eq))
                src, dst = pr, pr2
                for sh in (1, 2, 4):
                    chain.link(tt_(dst[:, :, sh:E], src[:, :, sh:E], src[:, :, 0:E - sh], ALU.add))
                    chain.link(nc.vector.tensor_copy(dst[:, :, 0:sh], src[:, :, 0:sh]))
                    src, dst = dst, src
                chain.link(stt(out=eq, in0=src, scalar=1.0, in1=eq, op0=ALU.is_equal, op1=ALU.mult))
                if pick == 0:
                    chain.link(nc.vector.tensor_copy(msk, eq))
                    chain.link(stt(out=cur, in0=eq, scalar=-2.0, in1=cur, op0=ALU.mult, op1=ALU.add))
                else:
                    chain.link(tt_(msk, msk, eq, ALU.add))
            chain.link(tt_(msk, fb, msk, ALU.mult))
            chain.link(nc.vector.tensor_reduce(fsum, msk, AX, ALU.add))
            chain.link(ts_(fsum, fsum, 1e-8, None, ALU.max))
            chain.link(nc.vector.reciprocal(fsum, fsum))
            chain.link(tt_(msk, msk, over(fsum), ALU.mult))
            chain.link(tt_(msk, msk, over(none), ALU.mult))
            chain.link(tt_(w, w, over(some), ALU.mult))
            chain.link(tt_(w, w, msk, ALU.add))
            chain.link(nc.vector.tensor_reduce(wsum, w, AX, ALU.add))
            chain.link(ts_(wsum, wsum, 1e-8, None, ALU.max))
            chain.link(nc.vector.reciprocal(wsum, wsum))
            chain.link(ts_(wsum, wsum, 1.0 / (SM * SW), None, ALU.mult))
            for at, e, n in ((0, 0, 1), (1, NL, E - NL), (E - 1, 1, 1)):
                chain.link(tt_(wt[:, :, at:at + n], w[:, :, e:e + n], over(wsum)[:, :, e:e + n], ALU.mult))

            for m in range(3):
                low_w(1, 1, m)

            final = Chain(dve, f_step)

            def moments(c):
                for t in range(TT):
                    wait_c_drained(dve, E - 1, ("d", c, t))
                    final.link(nc.vector.bn_stats(stats[:, t, :], resid[:, c * TT + t, :]))
                    nc.vector.bn_aggr(mv[:, t, :], stats[:, t, :]).then_inc(f_var, 1)

            def final_norm(c):
                dve.wait_ge(f_rstd, c + 1)
                refine(final, 0, TT)
                for t in range(TT):
                    row = resid[:, c * TT + t, :]
                    ts_(row, row, mv[:, t, 0:1], rstd[:, t:t + 1], ALU.subtract, ALU.mult).then_inc(y_ready, 1)

            def expert(e, par, last=False):
                def hidden(c):
                    for f in range(FT):
                        n = c * FT + f
                        u = ("u", c, f)
                        wait_c_drained(dve, e, ("g", c, f))
                        wait_c_filled(dve, e, u)
                        dve.wait_ge(mid_lo, e * (B * FT) + (n - 1 + FREE))
                        stt(out=midf[:, n % 2, :], in0=c_bank(e, u), scalar=SM / (SX * SW), in1=sil[:, n % 2, :],
                            op0=ALU.mult, op1=ALU.mult).then_inc(c_read(e, u), 1)

                def add(c):
                    for t in range(TT):
                        u = ("d", c, t)
                        wait_c_filled(dve, e, u)
                        row = resid[:, c * TT + t, :]
                        stt(out=row, in0=c_bank(e, u), scalar=wt[:, c * TT + t, bass.ds(e, 1)], in1=row,
                            op0=ALU.mult, op1=ALU.add).then_inc(c_read(e, u), 1)

                for c in range(B + 1):
                    fold = type(e) is int and e == E - 2 and 1 <= c <= 3
                    if fold:
                        factor_lows(c - 1)
                    if c < B:
                        hidden(c)
                    if fold:
                        add_product(c - 1)
                        if c >= 2:
                            low_w(E - 1, 1, c - 2)
                    if last and c >= 2:
                        final_norm(c - 2)
                    if c:
                        add(c - 1)
                    if last and c:
                        moments(c - 1)
                if last:
                    final_norm(B - 1)
                if type(e) is int and e == E - 2:
                    low_w(E - 1, 1, 2)

            def factor_lows(m):
                n, u = 3 + m, ("lt", m)
                dve.wait_ge(lora_hi, 2 * n + 1)
                low(lb16[1][:, 1, :], lb_last[n % 2], lb16[1][:, 0, :], SW).then_inc(lora_lo, 1)
                dve.wait_ge(lora_hi, 2 * n + 2)
                low(lb16[0][:, 1, :], c_bank(E - 2, u)[0:R, :], lb16[0][:, 0, :], SW).then_inc(c_read(E - 2, u), 1)
                wait_c_drained(dve, E - 2, u)
                dve.sem_inc(lora_lo, 1)

            def add_product(m):
                for t in range(TT):
                    u = ("lp", m, t)
                    if t == 0:
                        dve.wait_ge(stage_loaded[m], E * 16)
                    wait_c_filled(dve, E - 2, u)
                    stt(out=stage[:, m, t, :], in0=c_bank(E - 2, u), scalar=1.0 / (SW * SW), in1=stage[:, m, t, :],
                        op0=ALU.mult, op1=ALU.add).then_inc(c_read(E - 2, u), 1)

            dve.wait_ge(x2_kept, 16 * B + FREE)
            with dve.Fori(0, E // 2 - 2) as pair:
                for par in range(2):
                    expert(pair * 2 + par, par)
                    for m in range(3):
                        low_w((pair * 2 + par) + 2, par, m)
            expert(E - 4, 0)
            for m in range(3):
                low_w(E - 2, 0, m)
            expert(E - 3, 1)
            expert(E - 2, 0)
            expert(E - 1, 1, True)


FREE = 16
POOL_COLS = 896
A_NORM = TT + 4
TOP_STEPS = 1 + 2 * ((TOPK - 1) // 8)
B_STEPS = 3 * TT + 4
COEF_STEPS = 7


def rotary_tables():
    freqs = np.float32(1.0) / np.float32(10000.0) ** (np.arange(0, ROPE, 2, dtype=np.float32) / np.float32(ROPE))
    emb = np.arange(S, dtype=np.float32)[:, None] * freqs[None, :].astype(np.float32)
    c, s = np.cos(emb), np.sin(emb)
    both = np.stack([np.stack([c, s], -1), np.stack([s, c], -1)])
    return np.ascontiguousarray(both.reshape(2, TT, P, ROPE // 2, 2).transpose(2, 0, 1, 3, 4)).astype(np.float32)


def kernel(**inputs):
    import concourse.bacc as bacc
    from concourse.bass_utils import run_bass_kernel_spmd

    names = {"x": "x", "ctx": "ctx_2048", "Wq": "L0_attn_Wq", "Wkv": "L0_attn_Wkv_down", "Wku": "L0_attn_Wk_up",
             "Wvu": "L0_attn_Wv_up", "W_qkv": "L0_xattn_W_qkv", "W_o": "L0_xattn_W_o", "beta_q": "L0_xattn_beta_q",
             "beta_k": "L0_xattn_beta_k", "gate": "L0_xattn_gate", "log_tau": "L0_xattn_log_tau", "Wg": "L0_ffn_Wg",
             "Wu": "L0_ffn_Wu", "Wd": "L0_ffn_Wd", "Ga": "L0_ffn_Ga", "Gb": "L0_ffn_Gb", "Ua": "L0_ffn_Ua",
             "Ub": "L0_ffn_Ub", "Da": "L0_ffn_Da", "Db": "L0_ffn_Db", "Wr": "L0_ffn_Wr", "temperature": "L0_ffn_temperature"}
    nc = bacc.Bacc("TRN2", target_bir_lowering=False, num_devices=1)
    arrays, aps = {}, {}
    for short, name in names.items():
        v = np.ascontiguousarray(inputs[name])
        if v.size == 1:
            v = v.reshape(1, 1)
        arrays[short] = v
    arrays["cossin"] = rotary_tables()
    for short, v in arrays.items():
        aps[short] = nc.dram_tensor("in_" + short, v.shape, mybir.dt.from_np(v.dtype), kind="ExternalInput").ap()
    y = nc.dram_tensor("y", (N, D), F32, kind="ExternalOutput")
    aps["y"] = y.ap()
    decoder(nc, aps)
    r = run_bass_kernel_spmd(nc, [{"in_" + k: v for k, v in arrays.items()}], core_ids=[0])
    return r.results[0]["y"].reshape(B, S, D)
```
